# Optimizing a Trainium2 kernel written in Bass

```python
import numpy as np
import jax
import jax.numpy as jnp

def _softmax(x, axis=-1):
    return jax.nn.softmax(x, axis=axis)

def _gelu(x):
    return jax.nn.gelu(x, approximate=True)

def _silu(x):
    return jax.nn.silu(x)

def _sigmoid(x):
    return jax.nn.sigmoid(x)

def _layernorm(x, axis=-1, eps=1e-05):
    m = jnp.mean(x, axis=axis, keepdims=True)
    v = jnp.var(x, axis=axis, keepdims=True)
    return (x - m) / jnp.sqrt(v + eps)

def _scatter_add(tgt, idx, src, axis=0):
    return tgt.at[idx].add(src)

def _segment_sum(src, seg, n):
    return jax.ops.segment_sum(src, seg, n)
kernel_name = 'mk_seq_preln_d2_jaxref_r8_697505'

def setup_inputs(seed: int=0):
    np.random.seed(seed)
    _w = jnp.asarray

    def _L0_attn_setup():
        import jax, jax.numpy as jnp
        import numpy as np
        from jax import lax
        D_MODEL = 128
        BATCH, SEQ = (4, 1024)

        def _binary_operator_diag(q_i, q_j):
            a_i, b_i = q_i
            a_j, b_j = q_j
            return (a_i * a_j, a_j * b_i + b_j)

        def _parallel_scan(a, b):
            a = jnp.moveaxis(a, 1, 0)
            b = jnp.moveaxis(b, 1, 0)
            _, h = lax.associative_scan(_binary_operator_diag, (a, b))
            return jnp.moveaxis(h, 0, 1)
        key = jax.random.key(seed)
        k_x, k_wz, k_wh = jax.random.split(key, 3)
        scale = 1.0 / np.sqrt(D_MODEL)
        x = jax.random.normal(k_x, (BATCH, SEQ, D_MODEL), dtype=jnp.float32)
        Wz = jax.random.normal(k_wz, (D_MODEL, D_MODEL), dtype=jnp.float32) * scale
        bz = jnp.zeros((D_MODEL,), dtype=jnp.float32)
        Wh = jax.random.normal(k_wh, (D_MODEL, D_MODEL), dtype=jnp.float32) * scale
        bh = jnp.zeros((D_MODEL,), dtype=jnp.float32)
        return {'x': x, 'Wz': Wz, 'bz': bz, 'Wh': Wh, 'bh': bh}
    _L0_attn_in = _L0_attn_setup()

    def _L0_ffn_setup():
        import jax, jax.numpy as jnp
        import numpy as np
        DIM = 128
        DEPTH = 6
        HEADS = 16
        DIM_HEAD = 64
        WINDOW = 32
        INNER = HEADS * DIM_HEAD
        DIM_INNER = int(DIM * 4 * 2 / 3)
        QK_SCALE = 8.0

        def shift_tokens(t):
            a, s = jnp.split(t, 2, -1)
            s = jnp.pad(s, ((0, 0), (1, 0), (0, 0)))[:, :-1]
            return jnp.concatenate([a, s], -1)

        def l2norm(t):
            return t / jnp.maximum(jnp.linalg.norm(t, axis=-1, keepdims=True), 1e-12)

        def rotate_half(x):
            x1, x2 = jnp.split(x, 2, -1)
            return jnp.concatenate([-x2, x1], -1)

        def rotary_tables(n):
            half = jnp.arange(0, DIM_HEAD, 2, dtype=jnp.float32)
            inv_freq = 1.0 / 10000.0 ** (half / DIM_HEAD)
            t = jnp.arange(n, dtype=jnp.float32)
            freqs = t[:, None] * inv_freq[None, :]
            freqs = jnp.concatenate([freqs, freqs], -1)
            base_scale = (half + 0.4 * DIM_HEAD) / (1.4 * DIM_HEAD)
            power = (t - n // 2) / (WINDOW // 2)
            scale = base_scale[None, :] ** power[:, None]
            scale = jnp.concatenate([scale, scale], -1)
            return (freqs, scale)

        def local_attention(q, k, v):
            b, h, n, d = q.shape
            w = WINDOW
            nw = n // w
            bq = q.reshape(b, h, nw, w, d)
            bk = k.reshape(b, h, nw, w, d)
            bv = v.reshape(b, h, nw, w, d)

            def look(t):
                p = jnp.pad(t, ((0, 0), (0, 0), (1, 0), (0, 0), (0, 0)))
                return jnp.concatenate([p[:, :, :nw], p[:, :, 1:]], axis=3)
            bk2, bv2 = (look(bk), look(bv))
            seq = jnp.arange(n).reshape(nw, w)
            seq_p = jnp.pad(seq, ((1, 0), (0, 0)), constant_values=-1)
            jt = jnp.concatenate([seq_p[:nw], seq_p[1:]], axis=1)
            it = seq[:, :, None]
            jb = jt[:, None, :]
            mask = (it < jb) | (it > jb + w) | (jb == -1)
            sim = jnp.einsum('bhwie,bhwje->bhwij', bq, bk2) * QK_SCALE
            sim = jnp.where(mask, -jnp.finfo(sim.dtype).max, sim)
            attn = jax.nn.softmax(sim, -1)
            out = jnp.einsum('bhwij,bhwje->bhwie', attn, bv2)
            return out.reshape(b, h, n, d)

        def attn_layer(x, Wqkv, qs, ksc, Wo):
            b, n, _ = x.shape
            qkv = x @ Wqkv
            q, k, v = jnp.split(qkv, 3, -1)
            sh = lambda t: t.reshape(b, n, HEADS, DIM_HEAD).transpose(0, 2, 1, 3)
            q, k, v = (sh(q), sh(k), sh(v))
            q = l2norm(q) * qs
            k = l2norm(k) * ksc
            freqs, scale = rotary_tables(n)
            cos, sin = (jnp.cos(freqs), jnp.sin(freqs))
            q = q * cos * scale + rotate_half(q) * sin * scale
            inv = 1.0 / scale
            k = k * cos * inv + rotate_half(k) * sin * inv
            out = local_attention(q, k, v)
            out = out.transpose(0, 2, 1, 3).reshape(b, n, INNER)
            return out @ Wo

        def ffn_layer(x, g, bln, W1, b1, W2, b2):
            mu = x.mean(-1, keepdims=True)
            var = ((x - mu) ** 2).mean(-1, keepdims=True)
            xn = (x - mu) / jnp.sqrt(var + 1e-05) * g + bln
            hg = xn @ W1 + b1
            a, gate = jnp.split(hg, 2, -1)
            return a * jax.nn.gelu(gate, approximate=False) @ W2 + b2
        key = jax.random.key(seed)
        ks = jax.random.split(key, 8)
        B, N = (2, 256)
        init = lambda k, shape: jax.random.normal(k, shape, jnp.float32) * 0.02
        return {'x': jax.random.normal(ks[0], (B, N, DIM), jnp.float32), 'Wqkv': init(ks[1], (DEPTH, DIM, 3 * INNER)), 'q_scale': jnp.ones((DEPTH, DIM_HEAD), jnp.float32), 'k_scale': jnp.ones((DEPTH, DIM_HEAD), jnp.float32), 'Wo': init(ks[2], (DEPTH, INNER, DIM)), 'ln_g': jnp.ones((DEPTH, DIM), jnp.float32), 'ln_b': jnp.zeros((DEPTH, DIM), jnp.float32), 'W1': init(ks[3], (DEPTH, DIM, 2 * DIM_INNER)), 'b1': jnp.zeros((DEPTH, 2 * DIM_INNER), jnp.float32), 'W2': init(ks[4], (DEPTH, DIM_INNER, DIM)), 'b2': jnp.zeros((DEPTH, DIM), jnp.float32)}
    _L0_ffn_in = _L0_ffn_setup()

    def _L1_attn_setup():
        import jax, jax.numpy as jnp
        import numpy as np
        B, S, E = (4, 256, 128)
        H, KVH = (16, 4)
        D = E // H
        QL, KVL = (64, 32)
        ROPE_BASE = 10000.0

        def _rope(x):
            d = x.shape[-1]
            inv_freq = 1.0 / ROPE_BASE ** (jnp.arange(0, d, 2, dtype=jnp.float32) / d)
            t = jnp.arange(x.shape[1], dtype=jnp.float32)
            freqs = jnp.outer(t, inv_freq)
            cos = jnp.cos(freqs)[None, :, None, :].astype(x.dtype)
            sin = jnp.sin(freqs)[None, :, None, :].astype(x.dtype)
            x1, x2 = (x[..., ::2], x[..., 1::2])
            r1 = x1 * cos - x2 * sin
            r2 = x1 * sin + x2 * cos
            return jnp.stack([r1, r2], axis=-1).reshape(x.shape)
        key = jax.random.key(seed)
        ks = jax.random.split(key, 7)
        s = 0.02
        return {'x': jax.random.normal(ks[0], (B, S, E), dtype=jnp.float32), 'Wqa': jax.random.normal(ks[1], (E, QL), dtype=jnp.float32) * s, 'Wqb': jax.random.normal(ks[2], (QL, E), dtype=jnp.float32) * s, 'Wkva': jax.random.normal(ks[3], (E, KVL), dtype=jnp.float32) * s, 'Wkvb': jax.random.normal(ks[4], (KVL, KVH * D * 2), dtype=jnp.float32) * s, 'Wout': jax.random.normal(ks[5], (E, E), dtype=jnp.float32) * s, 'bout': jax.random.normal(ks[6], (E,), dtype=jnp.float32) * s}
    _L1_attn_in = _L1_attn_setup()

    def _L1_ffn_setup():
        import jax, jax.numpy as jnp
        import numpy as np
        B, S, D, E, K = (2, 256, 128, 8, 2)
        DFF = 4 * D
        key = jax.random.key(seed)
        ks = jax.random.split(key, 7)
        scale = 0.02
        return {'x': jax.random.normal(ks[0], (B, S, D), dtype=jnp.float32), 'W1': jax.random.normal(ks[1], (E, D, DFF), dtype=jnp.float32) * scale, 'b1': jnp.zeros((E, DFF), dtype=jnp.float32), 'W2': jax.random.normal(ks[2], (E, DFF, D), dtype=jnp.float32) * scale, 'b2': jnp.zeros((E, D), dtype=jnp.float32), 'Wg': jax.random.normal(ks[3], (D, E), dtype=jnp.float32) * scale, 'bg': jnp.zeros((E,), dtype=jnp.float32)}
    _L1_ffn_in = _L1_ffn_setup()
    _d = {'L0_attn_x': _L0_attn_in['x'], 'L0_attn_Wz': _L0_attn_in['Wz'], 'L0_attn_bz': _L0_attn_in['bz'], 'L0_attn_Wh': _L0_attn_in['Wh'], 'L0_attn_bh': _L0_attn_in['bh'], 'L0_ffn_Wqkv': _L0_ffn_in['Wqkv'], 'L0_ffn_q_scale': _L0_ffn_in['q_scale'], 'L0_ffn_k_scale': _L0_ffn_in['k_scale'], 'L0_ffn_Wo': _L0_ffn_in['Wo'], 'L0_ffn_ln_g': _L0_ffn_in['ln_g'], 'L0_ffn_ln_b': _L0_ffn_in['ln_b'], 'L0_ffn_W1': _L0_ffn_in['W1'], 'L0_ffn_b1': _L0_ffn_in['b1'], 'L0_ffn_W2': _L0_ffn_in['W2'], 'L0_ffn_b2': _L0_ffn_in['b2'], 'L1_attn_Wqa': _L1_attn_in['Wqa'], 'L1_attn_Wqb': _L1_attn_in['Wqb'], 'L1_attn_Wkva': _L1_attn_in['Wkva'], 'L1_attn_Wkvb': _L1_attn_in['Wkvb'], 'L1_attn_Wout': _L1_attn_in['Wout'], 'L1_attn_bout': _L1_attn_in['bout'], 'L1_ffn_W1': _L1_ffn_in['W1'], 'L1_ffn_b1': _L1_ffn_in['b1'], 'L1_ffn_W2': _L1_ffn_in['W2'], 'L1_ffn_b2': _L1_ffn_in['b2'], 'L1_ffn_Wg': _L1_ffn_in['Wg'], 'L1_ffn_bg': _L1_ffn_in['bg']}
    _x0 = _d['L0_attn_x']
    _d['L0_attn_x'] = jax.random.normal(jax.random.fold_in(jax.random.key(seed), 1), (8, 256, 128), dtype=_x0.dtype)
    del _x0
    return _d

def reference(L0_attn_x, L0_attn_Wz, L0_attn_bz, L0_attn_Wh, L0_attn_bh, L0_ffn_Wqkv, L0_ffn_q_scale, L0_ffn_k_scale, L0_ffn_Wo, L0_ffn_ln_g, L0_ffn_ln_b, L0_ffn_W1, L0_ffn_b1, L0_ffn_W2, L0_ffn_b2, L1_attn_Wqa, L1_attn_Wqb, L1_attn_Wkva, L1_attn_Wkvb, L1_attn_Wout, L1_attn_bout, L1_ffn_W1, L1_ffn_b1, L1_ffn_W2, L1_ffn_b2, L1_ffn_Wg, L1_ffn_bg):

    def _L0_attn_ref(x, Wz, bz, Wh, bh):
        import jax, jax.numpy as jnp
        import numpy as np
        from jax import lax
        D_MODEL = 128
        BATCH, SEQ = (4, 1024)

        def _binary_operator_diag(q_i, q_j):
            a_i, b_i = q_i
            a_j, b_j = q_j
            return (a_i * a_j, a_j * b_i + b_j)

        def _parallel_scan(a, b):
            a = jnp.moveaxis(a, 1, 0)
            b = jnp.moveaxis(b, 1, 0)
            _, h = lax.associative_scan(_binary_operator_diag, (a, b))
            return jnp.moveaxis(h, 0, 1)
        z_pre = jnp.einsum('bsd,de->bse', x, Wz) + bz
        h_tilde = jnp.einsum('bsd,de->bse', x, Wh) + bh
        z = jax.nn.sigmoid(z_pre)
        a = 1.0 - z
        b = z * h_tilde
        return _parallel_scan(a, b)

    def _L0_ffn_ref(x, Wqkv, q_scale, k_scale, Wo, ln_g, ln_b, W1, b1, W2, b2):
        import jax, jax.numpy as jnp
        import numpy as np
        DIM = 128
        DEPTH = 6
        HEADS = 16
        DIM_HEAD = 64
        WINDOW = 32
        INNER = HEADS * DIM_HEAD
        DIM_INNER = int(DIM * 4 * 2 / 3)
        QK_SCALE = 8.0

        def shift_tokens(t):
            a, s = jnp.split(t, 2, -1)
            s = jnp.pad(s, ((0, 0), (1, 0), (0, 0)))[:, :-1]
            return jnp.concatenate([a, s], -1)

        def l2norm(t):
            return t / jnp.maximum(jnp.linalg.norm(t, axis=-1, keepdims=True), 1e-12)

        def rotate_half(x):
            x1, x2 = jnp.split(x, 2, -1)
            return jnp.concatenate([-x2, x1], -1)

        def rotary_tables(n):
            half = jnp.arange(0, DIM_HEAD, 2, dtype=jnp.float32)
            inv_freq = 1.0 / 10000.0 ** (half / DIM_HEAD)
            t = jnp.arange(n, dtype=jnp.float32)
            freqs = t[:, None] * inv_freq[None, :]
            freqs = jnp.concatenate([freqs, freqs], -1)
            base_scale = (half + 0.4 * DIM_HEAD) / (1.4 * DIM_HEAD)
            power = (t - n // 2) / (WINDOW // 2)
            scale = base_scale[None, :] ** power[:, None]
            scale = jnp.concatenate([scale, scale], -1)
            return (freqs, scale)

        def local_attention(q, k, v):
            b, h, n, d = q.shape
            w = WINDOW
            nw = n // w
            bq = q.reshape(b, h, nw, w, d)
            bk = k.reshape(b, h, nw, w, d)
            bv = v.reshape(b, h, nw, w, d)

            def look(t):
                p = jnp.pad(t, ((0, 0), (0, 0), (1, 0), (0, 0), (0, 0)))
                return jnp.concatenate([p[:, :, :nw], p[:, :, 1:]], axis=3)
            bk2, bv2 = (look(bk), look(bv))
            seq = jnp.arange(n).reshape(nw, w)
            seq_p = jnp.pad(seq, ((1, 0), (0, 0)), constant_values=-1)
            jt = jnp.concatenate([seq_p[:nw], seq_p[1:]], axis=1)
            it = seq[:, :, None]
            jb = jt[:, None, :]
            mask = (it < jb) | (it > jb + w) | (jb == -1)
            sim = jnp.einsum('bhwie,bhwje->bhwij', bq, bk2) * QK_SCALE
            sim = jnp.where(mask, -jnp.finfo(sim.dtype).max, sim)
            attn = jax.nn.softmax(sim, -1)
            out = jnp.einsum('bhwij,bhwje->bhwie', attn, bv2)
            return out.reshape(b, h, n, d)

        def attn_layer(x, Wqkv, qs, ksc, Wo):
            b, n, _ = x.shape
            qkv = x @ Wqkv
            q, k, v = jnp.split(qkv, 3, -1)
            sh = lambda t: t.reshape(b, n, HEADS, DIM_HEAD).transpose(0, 2, 1, 3)
            q, k, v = (sh(q), sh(k), sh(v))
            q = l2norm(q) * qs
            k = l2norm(k) * ksc
            freqs, scale = rotary_tables(n)
            cos, sin = (jnp.cos(freqs), jnp.sin(freqs))
            q = q * cos * scale + rotate_half(q) * sin * scale
            inv = 1.0 / scale
            k = k * cos * inv + rotate_half(k) * sin * inv
            out = local_attention(q, k, v)
            out = out.transpose(0, 2, 1, 3).reshape(b, n, INNER)
            return out @ Wo

        def ffn_layer(x, g, bln, W1, b1, W2, b2):
            mu = x.mean(-1, keepdims=True)
            var = ((x - mu) ** 2).mean(-1, keepdims=True)
            xn = (x - mu) / jnp.sqrt(var + 1e-05) * g + bln
            hg = xn @ W1 + b1
            a, gate = jnp.split(hg, 2, -1)
            return a * jax.nn.gelu(gate, approximate=False) @ W2 + b2
        for i in range(DEPTH):
            x = attn_layer(shift_tokens(x), Wqkv[i], q_scale[i], k_scale[i], Wo[i]) + x
            x = ffn_layer(shift_tokens(x), ln_g[i], ln_b[i], W1[i], b1[i], W2[i], b2[i]) + x
        return x

    def _L1_attn_ref(x, Wqa, Wqb, Wkva, Wkvb, Wout, bout):
        import jax, jax.numpy as jnp
        import numpy as np
        B, S, E = (4, 256, 128)
        H, KVH = (16, 4)
        D = E // H
        QL, KVL = (64, 32)
        ROPE_BASE = 10000.0

        def _rope(x):
            d = x.shape[-1]
            inv_freq = 1.0 / ROPE_BASE ** (jnp.arange(0, d, 2, dtype=jnp.float32) / d)
            t = jnp.arange(x.shape[1], dtype=jnp.float32)
            freqs = jnp.outer(t, inv_freq)
            cos = jnp.cos(freqs)[None, :, None, :].astype(x.dtype)
            sin = jnp.sin(freqs)[None, :, None, :].astype(x.dtype)
            x1, x2 = (x[..., ::2], x[..., 1::2])
            r1 = x1 * cos - x2 * sin
            r2 = x1 * sin + x2 * cos
            return jnp.stack([r1, r2], axis=-1).reshape(x.shape)
        b, s, _ = x.shape
        scale = D ** (-0.5)
        q = (x @ Wqa @ Wqb).reshape(b, s, H, D)
        kv = (x @ Wkva @ Wkvb).reshape(b, s, KVH, D, 2)
        k, v = (kv[..., 0], kv[..., 1])
        q = _rope(q)
        k = _rope(k)
        g = H // KVH
        k = jnp.repeat(k, g, axis=2)
        v = jnp.repeat(v, g, axis=2)
        scores = jnp.einsum('bqhd,bkhd->bhqk', q, k) * scale
        causal = jnp.triu(jnp.ones((s, s), dtype=bool), k=1)
        scores = jnp.where(causal[None, None], -jnp.inf, scores)
        w = jax.nn.softmax(scores, axis=-1)
        out = jnp.einsum('bhqk,bkhd->bqhd', w, v).reshape(b, s, E)
        return out @ Wout + bout

    def _L1_ffn_ref(x, W1, b1, W2, b2, Wg, bg):
        import jax, jax.numpy as jnp
        import numpy as np
        B, S, D, E, K = (2, 256, 128, 8, 2)
        DFF = 4 * D
        num_experts = W1.shape[0]
        gate_logits = jnp.einsum('bsd,de->bse', x, Wg) + bg
        topk_w, topk_i = jax.lax.top_k(gate_logits, K)
        topk_w = jax.nn.softmax(topk_w, axis=-1)
        w = jnp.sum(jax.nn.one_hot(topk_i, num_experts, dtype=x.dtype) * topk_w[..., None], axis=-2)
        h = jax.nn.gelu(jnp.einsum('bsd,edf->bsef', x, W1) + b1, approximate=False)
        out = jnp.einsum('bsef,efd,bse->bsd', h, W2, w)
        out = out + jnp.einsum('bse,ed->bsd', w, b2)
        return out
    x = L0_attn_x
    x = x + _L0_attn_ref(_layernorm(x, axis=-1), L0_attn_Wz, L0_attn_bz, L0_attn_Wh, L0_attn_bh)
    x = x + _L0_ffn_ref(_layernorm(x, axis=-1), L0_ffn_Wqkv, L0_ffn_q_scale, L0_ffn_k_scale, L0_ffn_Wo, L0_ffn_ln_g, L0_ffn_ln_b, L0_ffn_W1, L0_ffn_b1, L0_ffn_W2, L0_ffn_b2)
    x = x + _L1_attn_ref(_layernorm(x, axis=-1), L1_attn_Wqa, L1_attn_Wqb, L1_attn_Wkva, L1_attn_Wkvb, L1_attn_Wout, L1_attn_bout)
    x = x + _L1_ffn_ref(_layernorm(x, axis=-1), L1_ffn_W1, L1_ffn_b1, L1_ffn_W2, L1_ffn_b2, L1_ffn_Wg, L1_ffn_bg)
    return x

_drawn_inputs = setup_inputs


def setup_inputs(seed=0):
    import zlib

    import numpy as np

    out = dict(_drawn_inputs(seed))
    spreads = {'L0_attn_bz': (0.0, 0.332),
     'L0_attn_bh': (0.0, 0.1),
     'L0_ffn_q_scale': (1.0, 0.6),
     'L0_ffn_k_scale': (1.0, 0.6),
     'L0_ffn_ln_g': (1.0, 0.6),
     'L0_ffn_ln_b': (0.0, 0.8),
     'L0_ffn_b1': (0.0, 0.8),
     'L0_ffn_b2': (0.0, 0.1),
     'L1_ffn_b1': (0.0, 0.8),
     'L1_ffn_b2': (0.0, 0.8),
     'L1_ffn_bg': (0.0, 0.316)}
    factors = {'L0_ffn_W1': 3.864,
     'L0_ffn_W2': 3.821,
     'L1_attn_Wqa': 8.0,
     'L1_attn_Wqb': 8.0,
     'L1_attn_Wkva': 8.0,
     'L1_attn_Wkvb': 8.0,
     'L1_attn_Wout': 8.0,
     'L1_attn_bout': 16.826,
     'L1_ffn_W1': 3.316,
     'L1_ffn_W2': 2.957}
    for name, (base, spread) in spreads.items():
        noise = np.random.default_rng([zlib.crc32(name.encode()), seed]).standard_normal(out[name].shape)
        drawn = base * np.exp(spread * noise) if base else spread * noise
        out[name] = jnp.asarray(drawn.astype(out[name].dtype))
    for name, factor in factors.items():
        out[name] = (out[name] * factor).astype(out[name].dtype)
    return out
```

```python
import math
from contextlib import ExitStack

import numpy as np

import concourse.bass as bass
from concourse import mybir
from concourse.bass import ds

F32 = mybir.dt.float32
BF16 = mybir.dt.bfloat16
I32 = mybir.dt.int32
U32 = mybir.dt.uint32
ALU = mybir.AluOpType
ACT = mybir.ActivationFunctionType
AX = mybir.AxisListType

P = 128
D = 128
NB, SEQ = 8, 256
NT = SEQ // P
DEPTH = 6
HEADS, DH = 16, 64
INNER = HEADS * DH
WIN = 32
NWT = P // WIN
NW = SEQ // WIN
HH = HEADS // 2
HP = HH // 2
UPB = NT * 2
FF = int(D * 4 * 2 / 3)
FC = math.ceil(FF / P)
FSZ = [min(P, FF - P * c) for c in range(FC)]
QH, KVH, QL, KVL, QD = 16, 4, 64, 32, 8
GRP = QH // KVH
NE, DFF = 8, 512
EC = DFF // P
EPS = 1e-5
NEG = -1e30
MAGIC = float(0x5F3759DF)
NR_STEPS = 11

CONST_COLS = {}
_at = 0
for _name, _n in (("ident", P), ("rot", NT * 4 * DH), ("rope", 2 * SEQ), ("rowmask", GRP), ("iota", NE),
                  ("band", 512), ("bandsel", NT * P), ("causal", NT * 512)):
    CONST_COLS[_name] = (_at, _at + _n)
    _at += _n
CONST_N = _at


class Signal:

    def __init__(self, sem, per=1, credit=0):
        self.sem, self.per, self.credit = sem, per, credit

    def after(self, n, k=None):
        return (n + self.credit) * self.per + (self.per if k is None else k) if self.per > 1 else n + self.credit + 1

    def start(self, eng):
        if self.credit:
            eng.sem_inc(self.sem, self.credit * self.per)


def steps(eng, count, lag):
    for s in range(lag):
        yield s, (lambda d, s=s: s >= d)
    with eng.Fori(lag, count) as s:
        yield s, (lambda d: True)
    for s in range(count, count + lag):
        yield s, (lambda d, s=s: s - d < count)


def mixed_kernel(nc, A, out):
    with ExitStack() as ctx:
        def sb(name, shape, dt=F32):
            return ctx.enter_context(nc.sbuf_tensor(name, shape, dt))

        def sig(name, per=1, credit=0):
            return Signal(ctx.enter_context(nc.semaphore(name)), per, credit)

        bank = [ctx.enter_context(nc.psum_tensor(f"bank{i}", [P, 512], F32)) for i in range(8)]

        const = sb("const", [P, CONST_N])

        def cst(name):
            a, b = CONST_COLS[name]
            return const[:, a:b]

        ident = cst("ident")
        rot_base = cst("rot").rearrange("p (t k d) -> p t k d", t=NT, k=4)
        rope = cst("rope")
        bandrhs = sb("bandrhs", [2 * WIN, 512], BF16)
        bandsel = sb("bandsel", [2 * WIN, NT, P], BF16)
        causal = sb("causal", [P, NT, 512], BF16)
        identb = sb("identb", [P, P], BF16)
        xT = sb("xT", [P, NB * SEQ])
        uT = sb("uT", [P, (NB + 1) * SEQ])
        lnin = sb("lnin", [P, SEQ])
        lns = sb("lns", [P, SEQ])
        lnx = sb("lnx", [P, NT, P])
        lnst = sb("lnst", [P, NT, 6])
        lnmv = sb("lnmv", [P, NT, 2])
        lnve = sb("lnve", [P, NT])
        lny = sb("lny", [P, NT])
        lnt = sb("lnt", [P, NT])
        xnT = sb("xnT", [P, SEQ])
        wzh = sb("wzh", [P, 2, D])
        bzh = sb("bzh", [P, 2])
        zs = sb("zs", [P, SEQ])
        za = sb("za", [P, SEQ])
        zb = sb("zb", [P, SEQ])
        hs = sb("hs", [P, SEQ])
        wqkv = sb("wqkv", [P, 3 * INNER])
        wo = sb("wo", [P, HEADS // 2, D])
        qks = sb("qks", [P, 4, DH])
        rot = sb("rot_t", [P, NT, 4, DH])
        xs = sb("xs", [P, SEQ])
        sq = sb("sq", [P, HEADS, DH])
        sqh = sb("sqh", [P, HEADS, DH // 2])
        ss = sb("ss", [P, HEADS])
        rn = sb("rn", [P, HEADS])
        rnt = sb("rnt", [P, HEADS])
        sc8 = sb("sc8", [P, UPB, HH])
        t1 = sb("t1", [P, 2, HH, DH])
        t2 = sb("t2", [P, 2, HH, DH])
        kr0 = sb("kr0", [P, HH, DH])
        qr = sb("qr", [P, 2, HH * DH])
        kr = sb("kr", [P, 2, HH, DH])
        qT = sb("qT", [P, HP, P])
        kBD = sb("kBD", [P, 2, HP, 2, WIN + SEQ])
        vS = sb("vS", [P, UPB, 2, HP, DH])
        vBD = sb("vBD", [P, 2, NW, 2, HP, DH])
        mx = sb("mx", [P, 2, HH])
        nbias = sb("nbias", [P, 2, HH])
        pr = sb("pr", [P, 2, HH, 2 * WIN])
        psm = sb("psm", [P, 2, HH])
        rinv = sb("rinv", [P, 2, HH])
        pT = sb("pT", [P, HP, P])
        ob = sb("ob", [P, 2, HH, DH])
        attT = sb("attT", [P, HEADS // 2, SEQ])
        w1 = sb("w1", [P, 2 * FF])
        w2 = sb("w2", [P, FC, D])
        lngb = sb("lngb", [P, 2])
        b1c = sb("b1c", [P, 2, FC])
        b2c = sb("b2c", [P, 1])
        gs = sb("gs", [P, FC, SEQ])
        hT = sb("hT", [P, FC, SEQ])

        wqa, wqb, wkva = sb("wqa", [P, QL]), sb("wqb", [QL, 2, P]), sb("wkva", [P, KVL])
        wkvn, wkb, wvb = sb("wkvn", [KVL, KVH, QD, 2]), sb("wkb", [KVL, 2, P]), sb("wvb", [KVL, KVH * QD])
        wout, boutc = sb("wout", [P, D]), sb("boutc", [P, 1])
        cqa, ckva = sb("cqa", [QL, SEQ]), sb("ckva", [KVL, SEQ])
        cq, ck = sb("cq", [P, SEQ]), sb("ck", [P, SEQ])
        cv = sb("cv", [P, NT, KVH * QD])
        late = kBD[:, :, :, :, :].rearrange("p h q e k -> p (h q e k)")
        ckm = late[:, 0:1024].rearrange("p (j k) -> p j k", j=GRP)
        ct = late[:, 1024:2048].rearrange("p (m k) -> p m k", m=2)
        cp = late[:, 2048:3584].rearrange("p (g k) -> p g k", g=3)
        cpT = late[:, 3584:4608].rearrange("p (g k) -> p g k", g=2)
        cmx, cnb = sb("cmx", [P, GRP]), sb("cnb", [P, 3, GRP])
        csum, crc = sb("csum", [P, NT, QH]), sb("crc", [P, NT, QH])
        co, coT = sb("co", [P, NT, P]), sb("coT", [P, SEQ])
        wg, bgb, b2e = sb("wg", [P, NE]), sb("bgb", [P, NE]), sb("b2e", [NE, D])
        dlg, dmx = sb("dlg", [P, NT, NE]), sb("dmx", [P, NT, 8])
        dix, dixf = sb("dix", [P, NT, 8], U32), sb("dixf", [P, NT, 2])
        ddiff, dexp, dden, dp = sb("ddiff", [P, NT]), sb("dexp", [P, NT]), sb("dden", [P, NT]), sb("dp", [P, 2, NT])
        dw1, dw2, dwT = sb("dw1", [P, NT, NE]), sb("dw2", [P, NT, NE]), sb("dwT", [NE, SEQ])
        xnA = uT
        wA = sb("wA", [P, NB * NT, NE])
        acc = sb("acc", [P, NB * SEQ])
        late = vBD[:, :, :, :, :, :].rearrange("p h w e q d -> p (h w e q d)")
        w1e = late[:, 0:NE * DFF].rearrange("p (e f) -> p e f", e=NE)
        w2e = late[:, NE * DFF:2 * NE * DFF].rearrange("p (e c d) -> p e c d", e=NE, c=EC)
        eh = wqkv[:, 0:2 * EC * SEQ].rearrange("p (m c k) -> p m c k", m=2, c=EC)
        b1e = sb("b1e", [P, NE * EC])
        xtok = acc[:, :].rearrange("p (t d) -> p t d", d=D)

        ld_const, ld_x, ld_gru = sig("ld_const"), sig("ld_x"), sig("ld_gru")
        held = sig("held")
        ld_exp = sig("ld_exp")
        ld_tail, st_out = sig("ld_tail"), sig("st_out")
        cast_done = sig("cast_done")
        zeroed, zeroed_dve = sig("zeroed"), sig("zeroed_dve")
        x_turned, x_kept = sig("x_turned"), sig("x_kept")
        ln_in = sig("ln_in", credit=1)
        ln_t1 = sig("ln_t1", credit=1)
        ln_stats = sig("ln_stats", credit=1)
        ln_chain = sig("ln_chain", per=NR_STEPS + 3)
        ln_t2 = sig("ln_t2", credit=1)
        ln_out = sig("ln_out", credit=1)
        zh_done = sig("zh_done", credit=1)
        z_sig, gru_a, gru_b, gru_scan, gru_res = (sig(x, credit=1) for x in ("z_sig", "gru_a", "gru_b", "gru_scan", "gru_res"))
        ld_wa = sig("ld_wa")
        tabs = sig("tabs")
        xs_in = sig("xs_in")
        q_mm, k_mm, v_mm = (sig(x, credit=1) for x in ("q_mm", "k_mm", "v_mm"))
        qt_mm, kt_mm, s_mm = (sig(x, credit=4) for x in ("qt_mm", "kt_mm", "s_mm"))
        pt_mm, o_mm, ot_mm = (sig(x, credit=4) for x in ("pt_mm", "o_mm", "ot_mm"))
        y_mm = sig("y_mm", credit=2)
        q_sq, k_sq, v_ev = (sig(x, credit=2) for x in ("q_sq", "k_sq", "v_ev"))
        qt_ev, kt_ev, p_exp, pt_ev, ot_ev = (sig(x, credit=4) for x in ("qt_ev", "kt_ev", "p_exp", "pt_ev", "ot_ev"))
        q_mul, k_mul = sig("q_mul", credit=2), sig("k_mul", credit=2)
        s_max, s_nb, p_sum, p_inv, o_norm = (sig(x, credit=4) for x in ("s_max", "s_nb", "p_sum", "p_inv", "o_norm"))
        ss_red = sig("ss_red", per=2, credit=2)
        nr_chain = sig("nr_chain", per=NR_STEPS, credit=2)
        sc_done = sig("sc_done", credit=2)
        u_res = sig("u_res", credit=2)
        sq_half, q_add, k_add, k_norm = (sig(x, credit=2) for x in ("sq_half", "q_add", "k_add", "k_norm"))
        v_dma = [sig(f"v_dma{j}", per=16 * (10 if j % NT == 0 else 8), credit=1) for j in range(UPB)]
        ld_wf = sig("ld_wf")
        h_mm, f_mm = sig("h_mm", credit=2), sig("f_mm", credit=2)
        g_act, h_mul, f_res = sig("g_act", credit=1), sig("h_mul", credit=1), sig("f_res", credit=NB)
        add_u = sig("add_u")
        cswap = sig("cswap")
        (c_rope, cv_ev, c_norm, lat_mm, lat_ev, c_ot, c_otev, c_y, c_proj, c_max, c_rcp, c_s) = (
            sig(x, credit=1) for x in ("c_rope", "cv_ev", "c_norm", "lat_mm", "lat_ev", "c_ot", "c_otev", "c_y", "c_proj",
                                       "c_max", "c_rcp", "c_s"))
        c_exp, c_ptev, c_pt, c_pv, c_nb, c_sum = (sig(x, credit=3) for x in ("c_exp", "c_ptev", "c_pt", "c_pv", "c_nb", "c_sum"))
        c_rc, c_res = sig("c_rc", per=4), sig("c_res", credit=2)
        d_lmm, d_tok, d_diff = sig("d_lmm"), sig("d_tok"), sig("d_diff")
        d_logit, d_w, d_wTev, d_wT, d_acc, d_b2, d_e = (
            sig(x, credit=1) for x in ("d_logit", "d_w", "d_wTev", "d_wT", "d_acc", "d_b2", "d_e"))
        d_ch = sig("d_ch", per=13)
        e_gelu, e_up, e_down, e_acc = sig("e_gelu", credit=4), sig("e_up"), sig("e_down", credit=2), sig("e_acc", credit=2)
        TAIL_LOADS = 10


        credited = {
            "pe": (ln_t1, ln_t2, zh_done, q_mm, k_mm, v_mm, qt_mm, kt_mm, s_mm, pt_mm, o_mm, ot_mm, y_mm, h_mm, f_mm,
                   lat_mm, c_ot, c_y, c_proj, c_s, c_pt, c_pv, d_wT, d_b2, e_down),
            "act": (ln_out, z_sig, q_sq, k_sq, v_ev, qt_ev, kt_ev, p_exp, pt_ev, ot_ev, g_act,
                    cv_ev, lat_ev, c_otev, c_exp, c_ptev, d_wTev, d_e, e_gelu),
            "dve": (ln_in, ln_stats, gru_a, gru_b, gru_scan, gru_res, q_mul, k_mul, s_max, s_nb, p_sum, p_inv, o_norm,
                    ss_red, nr_chain, sc_done, u_res, h_mul, f_res,
                    c_rope, c_norm, c_max, c_rcp, c_nb, c_sum, c_res, d_logit, d_w, d_acc, e_acc),
            "pool": (sq_half, q_add, k_add, k_norm),
            "sp": tuple(v_dma),
        }
        LA_LOADS, LF_LOADS = 8, 10
        LN_A1, LN_A2, LN_F = 0, NB, 2 * NB
        LN_C = LN_F + DEPTH * NB
        LN_D = LN_C + NB

        def hold(eng):
            eng.sem_inc(held.sem, 1)

        def col(t, a):
            return t[:, a:a + 1]

        def ln_turn_in(pe, i, src):
            pe.wait_ge(ln_in.sem, ln_in.after(i))
            pe.wait_ge(ln_stats.sem, ln_stats.after(i - 1))
            for t in range(NT):
                mm = pe.transpose(bank[0][:, t * P:(t + 1) * P], src[:, t * P:(t + 1) * P], ident)
            mm.then_inc(ln_t1.sem, 1)

        def ln_turn_out(pe, i):
            pe.wait_ge(ln_stats.sem, ln_stats.after(i))
            pe.wait_ge(ln_out.sem, ln_out.after(i - 1))
            for t in range(NT):
                mm = pe.transpose(bank[1][:, t * P:(t + 1) * P], lnx[:, t, :], ident)
            mm.then_inc(ln_t2.sem, 1)

        def rsqrt(dve, y, v, tmp, chain, n, first):
            k = first

            def link(ins):
                nonlocal k
                k += 1
                ins.then_inc(chain.sem, 1)
                dve.wait_ge(chain.sem, chain.after(n, k))

            link(dve.tensor_scalar(tmp.bitcast(I32), v.bitcast(I32), 1, None, ALU.logical_shift_right))
            link(dve.tensor_scalar(y.bitcast(I32), tmp.bitcast(I32), -1.0, MAGIC, ALU.mult, ALU.add))
            for _ in range(3):
                link(dve.tensor_tensor(tmp, y, y, ALU.mult))
                link(dve.scalar_tensor_tensor(out=tmp, in0=tmp, scalar=-0.5, in1=v, op0=ALU.mult, op1=ALU.mult))
                link(dve.scalar_tensor_tensor(out=y, in0=tmp, scalar=1.5, in1=y, op0=ALU.add, op1=ALU.mult))
            return k

        def ln_normalise(dve, i):
            tok = bank[0][:, 0:NT * P].rearrange("p (t d) -> p t d", t=NT)
            dve.wait_ge(ln_t1.sem, ln_t1.after(i))
            for t in range(NT):
                ins = dve.bn_stats(lnst[:, t, :], tok[:, t, :])
            ins.then_inc(ln_chain.sem, 1)
            dve.wait_ge(ln_chain.sem, ln_chain.after(i, 1))
            hold(dve)
            for t in range(NT):
                ins = dve.bn_aggr(lnmv[:, t, :], lnst[:, t, :])
            ins.then_inc(ln_chain.sem, 1)
            dve.wait_ge(ln_chain.sem, ln_chain.after(i, 2))
            dve.tensor_scalar(lnve[:, :], lnmv[:, :, 1], EPS, None, ALU.add).then_inc(ln_chain.sem, 1)
            dve.wait_ge(ln_chain.sem, ln_chain.after(i, 3))
            rsqrt(dve, lny[:, :], lnve[:, :], lnt[:, :], ln_chain, i, 3)
            dve.wait_ge(ln_t2.sem, ln_t2.after(i - 1))
            for t in range(NT):
                ins = dve.tensor_scalar(lnx[:, t, :], tok[:, t, :], lnmv[:, t, 0:1], lny[:, t:t + 1],
                                        ALU.subtract, ALU.mult)
            ins.then_inc(ln_stats.sem, 1)

        def seq_cols(b, n=SEQ, off=0):
            return ds(b * SEQ + off, n) if not isinstance(b, int) else slice(b * SEQ + off, b * SEQ + off + n)

        def shifted_copy(dve, dst, b):
            h = D // 2
            dve.tensor_copy(dst[0:h, :], uT[0:h, seq_cols(b)])
            return dve.tensor_copy(dst[h:D, 1:SEQ], uT[h:D, seq_cols(b, SEQ - 1)])

        L_T, L_S, L_P, L_O = 1, 2, 3, 4

        def units(eng, layer):
            for bs, live in steps(eng, NB, 1):
                B = layer * NB + bs
                n0 = B * UPB
                for j in range(UPB):
                    yield bs, B, j, (lambda d, j=j, live=live: live((d - j + UPB - 1) // UPB)), (lambda d, n0=n0, j=j: n0 + j - d)

        def attention_pe(pe, layer):
            for bs, B, j, live, unit in units(pe, layer):
                if live(0):
                    n, h, t = unit(0), j // NT, j % NT
                    if j == 0:
                        pe.wait_ge(xs_in.sem, xs_in.after(layer * (NB + 1) + bs))
                    xt = xs[:, t * P:(t + 1) * P]
                    pe.wait_ge(q_mul.sem, q_mul.after(n - 1))
                    pe.matmul(bank[0][:, :], xt, wqkv[:, h * 512:(h + 1) * 512], start=True, stop=True).then_inc(q_mm.sem, 1)
                    pe.wait_ge(k_mul.sem, k_mul.after(n - 1))
                    pe.matmul(bank[1][:, :], xt, wqkv[:, INNER + h * 512:INNER + (h + 1) * 512],
                              start=True, stop=True).then_inc(k_mm.sem, 1)
                    pe.wait_ge(v_ev.sem, v_ev.after(n - 1))
                    if j == 0:
                        pe.wait_ge(u_res.sem, u_res.after(B - 2))
                        if isinstance(bs, int) and bs == 0:
                            pe.wait_ge(f_res.sem, f_res.after(B - 1))
                    pe.matmul(bank[2][:, :], xt, wqkv[:, 2 * INNER + h * 512:2 * INNER + (h + 1) * 512],
                              start=True, stop=True).then_inc(v_mm.sem, 1)
                if live(L_P):
                    n = unit(L_P)
                    pe.wait_ge(p_exp.sem, p_exp.after(n))
                    pe.wait_ge(pt_ev.sem, pt_ev.after(n - 1))
                    for p in range(HP):
                        mm = pe.transpose(bank[6][:, p * P:(p + 1) * P],
                                          pr[:, (j - L_P) % 2, 2 * p:2 * p + 2, :].rearrange("q h k -> q (h k)"), ident)
                    mm.then_inc(pt_mm.sem, 1)
                if live(L_O):
                    n = unit(L_O)
                    pe.wait_ge(o_norm.sem, o_norm.after(n))
                    if live(L_S):
                        pe.wait_ge(kt_ev.sem, kt_ev.after(unit(L_S)))
                    else:
                        pe.wait_ge(ot_ev.sem, ot_ev.after(n - 1))
                    for p in range(HP):
                        mm = pe.transpose(bank[4][:, p * P:(p + 1) * P],
                                          ob[:, (j - L_O) % 2, 2 * p:2 * p + 2, :].rearrange("q h k -> q (h k)"), ident)
                    mm.then_inc(ot_mm.sem, 1)
                if live(L_S):
                    n = unit(L_S)
                    h, t = (j - L_S) % UPB // NT, (j - L_S) % NT
                    pe.wait_ge(qt_ev.sem, qt_ev.after(n))
                    pe.wait_ge(kt_ev.sem, kt_ev.after(n))
                    pe.wait_ge(p_exp.sem, p_exp.after(n - 1))
                    pe.matmul(bank[5][:, :], bandsel[:, t, :], bandrhs[:, :], start=True, stop=False, skip_group_check=True)
                    for p in range(HP):
                        for w in range(NWT):
                            k0 = (t * NWT + w) * WIN
                            mm = pe.matmul(bank[5][w * WIN:(w + 1) * WIN, p * P:(p + 1) * P],
                                           qT[:, p, w * WIN:(w + 1) * WIN], kBD[:, h, p, :, k0:k0 + 2 * WIN],
                                           start=False, stop=True, skip_group_check=True)
                    mm.then_inc(s_mm.sem, 1)
                if live(L_T):
                    n, par = unit(L_T), (j - L_T) % 2
                    pe.wait_ge(q_add.sem, q_add.after(n))
                    pe.wait_ge(qt_ev.sem, qt_ev.after(n - 1))
                    for p in range(HP):
                        mm = pe.transpose(bank[3][:, p * P:(p + 1) * P], qr[:, par, p * P:(p + 1) * P], ident)
                    mm.then_inc(qt_mm.sem, 1)
                    pe.wait_ge(k_norm.sem, k_norm.after(n))
                    pe.wait_ge(ot_ev.sem, ot_ev.after(n - 3))
                    for p in range(HP):
                        mm = pe.transpose(bank[4][:, p * P:(p + 1) * P],
                                          kr[:, par, 2 * p:2 * p + 2, :].rearrange("q h k -> q (h k)"), ident)
                    mm.then_inc(kt_mm.sem, 1)
                if live(L_P):
                    n = unit(L_P)
                    jj = (j - L_P) % UPB
                    h, t = jj // NT, jj % NT
                    pe.wait_ge(pt_ev.sem, pt_ev.after(n))
                    pe.wait_ge(v_dma[jj].sem, v_dma[jj].after(B if j >= L_P else B - 1))
                    pe.wait_ge(o_norm.sem, o_norm.after(n - 1))
                    for p in range(HP):
                        for w in range(NWT):
                            mm = pe.matmul(bank[7][w * WIN:(w + 1) * WIN, p * P:(p + 1) * P],
                                           pT[:, p, w * WIN:(w + 1) * WIN], vBD[:, h, t * NWT + w, :, p, :],
                                           start=True, stop=True)
                    mm.then_inc(o_mm.sem, 1)
                if j == UPB - 1 and live(L_O):
                    pe.wait_ge(ot_ev.sem, ot_ev.after(unit(L_O)))
                    pe.wait_ge(v_ev.sem, v_ev.after(unit(0) if live(0) else unit(L_O)))
                    for c in range(HEADS // 2):
                        mm = pe.matmul(bank[2][:, 0:SEQ], wo[:, c, :], attT[:, c, :], start=(c == 0), stop=(c == HEADS // 2 - 1))
                    mm.then_inc(y_mm.sem, 1)

        def attention_act(act, layer):
            for bs, B, j, live, unit in units(act, layer):
                if live(0):
                    n = unit(0)
                    act.wait_ge(q_mm.sem, q_mm.after(n))
                    act.wait_ge(sq_half.sem, sq_half.after(n - 1))
                    act.activation(sq[:, 0:HH, :], bank[0][:, :].rearrange("p (h d) -> p h d", d=DH), ACT.Square).then_inc(q_sq.sem, 1)
                    act.wait_ge(k_mm.sem, k_mm.after(n))
                    act.activation(sq[:, HH:, :], bank[1][:, :].rearrange("p (h d) -> p h d", d=DH), ACT.Square).then_inc(k_sq.sem, 1)
                    act.wait_ge(v_mm.sem, v_mm.after(n))
                    act.wait_ge(v_dma[j].sem, v_dma[j].after(B - 1))
                    act.activation(vS[:, j, :, :, :].rearrange("p e q d -> p q e d"),
                                   bank[2][:, :].rearrange("p (q e d) -> p q e d", e=2, d=DH), ACT.Copy).then_inc(v_ev.sem, 1)
                if live(L_P):
                    n = unit(L_P)
                    act.wait_ge(pt_mm.sem, pt_mm.after(n))
                    act.wait_ge(o_mm.sem, o_mm.after(n - 1))
                    act.activation(pT[:, :, :].rearrange("p a b -> p (a b)"), bank[6][:, :], ACT.Copy).then_inc(pt_ev.sem, 1)
                if live(L_O):
                    n = unit(L_O)
                    jj = (j - L_O) % UPB
                    h, t = jj // NT, jj % NT
                    act.wait_ge(ot_mm.sem, ot_mm.after(n))
                    act.activation(attT[:, h * HP:(h + 1) * HP, t * P:(t + 1) * P],
                                   bank[4][:, :].rearrange("p (a b) -> p a b", a=HP), ACT.Copy).then_inc(ot_ev.sem, 1)
                if live(L_S):
                    n = unit(L_S)
                    par = (j - L_S) % 2
                    act.wait_ge(s_nb.sem, s_nb.after(n))
                    act.wait_ge(pt_mm.sem, pt_mm.after(n - 2))
                    act.wait_ge(p_sum.sem, p_sum.after(n - 2))
                    for hd in range(HH):
                        ins = act.activation(pr[:, par, hd, :], bank[5][:, hd * 64:(hd + 1) * 64], ACT.Exp,
                                             scale=sc8[:, (j - L_S) % UPB, hd:hd + 1], bias=nbias[:, par, hd:hd + 1])
                    ins.then_inc(p_exp.sem, 1)
                if live(L_T):
                    n = unit(L_T)
                    jj = (j - L_T) % UPB
                    h, t = jj // NT, jj % NT
                    act.wait_ge(qt_mm.sem, qt_mm.after(n))
                    act.activation(qT[:, :, :].rearrange("p a b -> p (a b)"), bank[3][:, :], ACT.Copy).then_inc(qt_ev.sem, 1)
                    act.wait_ge(kt_mm.sem, kt_mm.after(n))
                    for e in range(2):
                        ins = act.activation(kBD[64 * e:64 * e + 64, h, :, e, WIN + t * P:WIN + (t + 1) * P],
                                             bank[4][64 * e:64 * e + 64, :].rearrange("p (a b) -> p a b", a=HP), ACT.Copy)
                    ins.then_inc(kt_ev.sem, 1)

        def attention_dve(dve, layer):
            dve.wait_ge(tabs.sem, layer + 1)
            for bs, B, j, live, unit in units(dve, layer):
                if j == 0 and isinstance(bs, int) and bs == 0:
                    dve.wait_ge(f_res.sem, f_res.after(B - 1))
                    dve.wait_ge(v_mm.sem, v_mm.after(unit(0) - 1))
                    shifted_copy(dve, xs, 0).then_inc(xs_in.sem, 1)
                if live(0):
                    n, t = unit(0), j % NT
                    for m, (mm, sqd, mul, add) in enumerate(((q_mm, q_sq, q_mul, q_add), (k_mm, k_sq, k_mul, k_add))):
                        dve.wait_ge(sqd.sem, sqd.after(n))
                        dve.wait_ge(add.sem, add.after(n - 1))
                        src = bank[m][:, :].rearrange("p (h d) -> p h d", d=DH)
                        swp = bank[m][:, :].rearrange("p (h s d) -> p h s d", h=HH, s=2)[:, :, ::-1, :]
                        tab = rot[:, t, 2 * m:2 * m + 2, :]
                        dve.tensor_tensor(t1[:, m], src, tab[:, 0, :].unsqueeze(1).broadcast_to([P, HH, DH]), ALU.mult)
                        dve.tensor_tensor(t2[:, m].rearrange("p h (s d) -> p h s d", s=2), swp,
                                          tab[:, 1, :].rearrange("p (s d) -> p s d", s=2).unsqueeze(1).broadcast_to([P, HH, 2, DH // 2]),
                                          ALU.mult).then_inc(mul.sem, 1)
                if live(L_P):
                    n, par = unit(L_P), (j - L_P) % 2
                    dve.wait_ge(p_exp.sem, p_exp.after(n))
                    dve.tensor_reduce(psm[:, par, :], pr[:, par], AX.X, ALU.add).then_inc(p_sum.sem, 1)
                    dve.wait_ge(p_sum.sem, p_sum.after(n))
                    dve.wait_ge(o_norm.sem, o_norm.after(n - 2))
                    dve.reciprocal(rinv[:, par, :], psm[:, par, :]).then_inc(p_inv.sem, 1)
                if live(L_S):
                    n, par = unit(L_S), (j - L_S) % 2
                    dve.wait_ge(s_mm.sem, s_mm.after(n))
                    dve.tensor_reduce(mx[:, par, :], bank[5][:, :].rearrange("p (h k) -> p h k", h=HH), AX.X, ALU.max).then_inc(s_max.sem, 1)
                    dve.wait_ge(s_max.sem, s_max.after(n))
                    dve.wait_ge(sc_done.sem, sc_done.after(n))
                    dve.wait_ge(p_exp.sem, p_exp.after(n - 2))
                    dve.scalar_tensor_tensor(out=nbias[:, par, :], in0=mx[:, par, :], scalar=-1.0,
                                             in1=sc8[:, (j - L_S) % UPB, :], op0=ALU.mult, op1=ALU.mult).then_inc(s_nb.sem, 1)
                if j == UPB - 1 and live(0):
                    dve.wait_ge(v_mm.sem, v_mm.after(unit(0)))
                    shifted_copy(dve, xs, bs + 1).then_inc(xs_in.sem, 1)
                if live(0):
                    n = unit(0)
                    dve.wait_ge(sq_half.sem, sq_half.after(n))
                    dve.wait_ge(nr_chain.sem, nr_chain.after(n - 1))
                    dve.tensor_reduce(ss[:, :], sqh[:, :, :], AX.X, ALU.add).then_inc(ss_red.sem, 1)
                    dve.wait_ge(ss_red.sem, ss_red.after(n, 1))
                    dve.tensor_scalar(ss[:, :], ss[:, :], 1e-24, None, ALU.max).then_inc(ss_red.sem, 1)
                    dve.wait_ge(ss_red.sem, ss_red.after(n, 2))
                    dve.wait_ge(k_norm.sem, k_norm.after(n - 1))
                    dve.wait_ge(sc_done.sem, sc_done.after(n - 1))
                    rsqrt(dve, rn[:, :], ss[:, :], rnt[:, :], nr_chain, n, 0)
                    dve.wait_ge(p_exp.sem, p_exp.after(n - UPB))
                    dve.tensor_scalar(sc8[:, j, :], rn[:, 0:HH], 8.0, None, ALU.mult).then_inc(sc_done.sem, 1)
                if live(L_P):
                    n, par = unit(L_P), (j - L_P) % 2
                    dve.wait_ge(o_mm.sem, o_mm.after(n))
                    dve.wait_ge(p_inv.sem, p_inv.after(n))
                    dve.wait_ge(ot_mm.sem, ot_mm.after(n - 2))
                    dve.tensor_tensor(ob[:, par], bank[7][:, :].rearrange("p (h d) -> p h d", h=HH),
                                      rinv[:, par, :].unsqueeze(2).broadcast_to([P, HH, DH]), ALU.mult).then_inc(o_norm.sem, 1)
                if j == UPB - 1 and live(L_O):
                    b1 = bs - 1
                    dve.wait_ge(y_mm.sem, y_mm.after(B - 1))
                    dve.tensor_tensor(uT[:, seq_cols(b1)], uT[:, seq_cols(b1)], bank[2][:, 0:SEQ], ALU.add).then_inc(u_res.sem, 1)

        def attention_pool(pool, layer):
            pool.wait_ge(ld_wa.sem, (layer + 1) * 16 * LA_LOADS)
            pool.wait_ge(k_mul.sem, k_mul.after(layer * NB * UPB - 1))
            for t in range(NT):
                ins = pool.tensor_tensor(rot[:, t], rot_base[:, t], qks[:, :, :], ALU.mult)
            ins.then_inc(tabs.sem, 1)
            for bs, B, j, live, unit in units(pool, layer):
                if live(0):
                    n, par = unit(0), j % 2
                    pool.wait_ge(k_sq.sem, k_sq.after(n))
                    pool.wait_ge(ss_red.sem, ss_red.after(n - 1, 1))
                    pool.tensor_tensor(sqh[:, :, :], sq[:, :, 0:DH // 2], sq[:, :, DH // 2:], ALU.add).then_inc(sq_half.sem, 1)
                    pool.wait_ge(q_mul.sem, q_mul.after(n))
                    pool.wait_ge(qt_mm.sem, qt_mm.after(n - 2))
                    pool.tensor_tensor(qr[:, par, :].rearrange("p (h d) -> p h d", h=HH), t1[:, 0], t2[:, 0], ALU.add).then_inc(q_add.sem, 1)
                    pool.wait_ge(k_mul.sem, k_mul.after(n))
                    pool.wait_ge(k_norm.sem, k_norm.after(n - 1))
                    pool.tensor_tensor(kr0[:, :, :], t1[:, 1], t2[:, 1], ALU.add).then_inc(k_add.sem, 1)
                    pool.wait_ge(k_add.sem, k_add.after(n))
                    pool.wait_ge(nr_chain.sem, nr_chain.after(n))
                    pool.wait_ge(kt_mm.sem, kt_mm.after(n - 2))
                    pool.tensor_tensor(kr[:, par], kr0[:, :, :], rn[:, HH:].unsqueeze(2).broadcast_to([P, HH, DH]),
                                       ALU.mult).then_inc(k_norm.sem, 1)

        def value_moves(h, t, j):
            for e in range(2):
                base = 64 * e
                for w in range(t * NWT, (t + 1) * NWT + 1):
                    lo = w * WIN - WIN
                    a, b = max(lo, t * P), min(lo + 2 * WIN, (t + 1) * P)
                    if w < NW and a < b:
                        yield (vBD[base + a - lo:base + b - lo, h, w, e, :, :], vS[a - t * P:b - t * P, j, e, :, :])

        def attention_sp(sp, layer):
            with sp.Fori(0, NB) as b:
                B = layer * NB + b
                for j in range(UPB):
                    n = B * UPB + j
                    sp.wait_ge(v_ev.sem, v_ev.after(n))
                    hold(sp)
                    sp.wait_ge(o_mm.sem, o_mm.after(n - 3))
                    for dst, src in value_moves(j // NT, j % NT, j):
                        sp.dma_start(dst, src).then_inc(v_dma[j].sem, 16)

        def mlp_pe(pe, layer):
            pe.wait_ge(ld_wf.sem, (layer + 1) * 16 * LF_LOADS)
            for s, live in steps(pe, NB, 2):
                B = layer * NB + s
                if live(0):
                    ln_turn_in(pe, LN_F + B, lns)
                if live(2):
                    pe.wait_ge(h_mul.sem, h_mul.after(B - 2))
                    pe.wait_ge(f_res.sem, f_res.after(B - 3))
                    if isinstance(s, int) and s == 2:
                        pe.wait_ge(u_res.sem, u_res.after(layer * NB + NB - 1))
                    for c in range(FC):
                        mm = pe.matmul(bank[2][:, 0:SEQ], w2[0:FSZ[c], c, :], hT[0:FSZ[c], c, :], start=(c == 0), stop=(c == FC - 1))
                    mm.then_inc(f_mm.sem, 1)
                if live(1):
                    pe.wait_ge(ln_out.sem, ln_out.after(LN_F + B - 1))
                    pe.wait_ge(h_mul.sem, h_mul.after(B - 2))
                    for c in range(FC):
                        for m in range(2):
                            o = m * FF + c * P
                            mm = pe.matmul(bank[3 + c][0:FSZ[c], m * SEQ:(m + 1) * SEQ], w1[:, o:o + FSZ[c]], xnT[:, :],
                                           start=True, stop=True)
                    mm.then_inc(h_mm.sem, 1)
                if live(0):
                    ln_turn_out(pe, LN_F + B)

        def mlp_act(act, layer):
            act.wait_ge(ld_wf.sem, (layer + 1) * 16 * LF_LOADS)
            for s, live in steps(act, NB, 1):
                B = layer * NB + s
                if live(1):
                    act.wait_ge(h_mm.sem, h_mm.after(B - 1))
                    act.wait_ge(h_mul.sem, h_mul.after(B - 2))
                    for c in range(FC):
                        ins = act.activation(gs[0:FSZ[c], c, :], bank[3 + c][0:FSZ[c], SEQ:2 * SEQ], ACT.Gelu,
                                             bias=b1c[0:FSZ[c], 1, c:c + 1])
                    ins.then_inc(g_act.sem, 1)
                if live(0):
                    i = LN_F + B
                    act.wait_ge(ln_t2.sem, ln_t2.after(i))
                    act.activation(xnT[:, :], bank[1][:, 0:SEQ], ACT.Identity, bias=lngb[:, 1:2], scale=lngb[:, 0:1]).then_inc(ln_out.sem, 1)

        def mlp_dve(dve, layer):
            dve.wait_ge(ld_wf.sem, (layer + 1) * 16 * LF_LOADS)
            for s, live in steps(dve, NB, 2):
                B = layer * NB + s
                if live(0):
                    i = LN_F + B
                    dve.wait_ge(u_res.sem, u_res.after(B))
                    dve.wait_ge(ln_t1.sem, ln_t1.after(i - 1))
                    shifted_copy(dve, lns, s).then_inc(ln_in.sem, 1)
                    ln_normalise(dve, i)
                if live(1):
                    dve.wait_ge(g_act.sem, g_act.after(B - 1))
                    dve.wait_ge(f_mm.sem, f_mm.after(B - 2))
                    for c in range(FC):
                        ins = dve.scalar_tensor_tensor(out=hT[0:FSZ[c], c, :], in0=bank[3 + c][0:FSZ[c], 0:SEQ],
                                                       scalar=b1c[0:FSZ[c], 0, c:c + 1], in1=gs[0:FSZ[c], c, :],
                                                       op0=ALU.add, op1=ALU.mult)
                    ins.then_inc(h_mul.sem, 1)
                if live(2):
                    dve.wait_ge(f_mm.sem, f_mm.after(B - 2))
                    b2_ = s - 2
                    dve.scalar_tensor_tensor(out=uT[:, seq_cols(b2_)], in0=bank[2][:, 0:SEQ], scalar=b2c[:, 0:1],
                                             in1=uT[:, seq_cols(b2_)], op0=ALU.add, op1=ALU.add).then_inc(f_res.sem, 1)

        def load_layer(sp, layer):
            def row(name):
                return A[name][ds(layer, 1)]

            half = DH // 2
            sp.wait_ge(y_mm.sem, y_mm.after(layer * NB - 1))
            hold(sp)
            for m, name in ((0, "L0_ffn_q_scale"), (2, "L0_ffn_k_scale")):
                v = row(name)
                sp.dma_start(qks[:, m, :], v.broadcast_to([P, DH])).then_inc(ld_wa.sem, 16)
                sp.dma_start(qks[:, m + 1, 0:half], v[:, half:DH].broadcast_to([P, half])).then_inc(ld_wa.sem, 16)
                sp.dma_start(qks[:, m + 1, half:DH], v[:, 0:half].broadcast_to([P, half])).then_inc(ld_wa.sem, 16)
            sp.dma_start(wqkv[:, :], row("L0_ffn_Wqkv").rearrange("l p n -> (l p) n")).then_inc(ld_wa.sem, 16)
            sp.dma_start(wo[:, :, :], row("L0_ffn_Wo").rearrange("l (c p) n -> p (l c) n", p=P)).then_inc(ld_wa.sem, 16)
            sp.wait_ge(f_res.sem, f_res.after(layer * NB - 1))
            hold(sp)
            full = (FC - 1) * P
            sp.dma_start(w1[:, :], row("L0_ffn_W1").rearrange("l p n -> (l p) n")).then_inc(ld_wf.sem, 16)
            v = row("L0_ffn_W2")
            sp.dma_start(w2[:, 0:FC - 1, :], v[:, 0:full, :].rearrange("l (c p) n -> p (l c) n", p=P)).then_inc(ld_wf.sem, 16)
            sp.dma_start(w2[0:FF - full, FC - 1, :], v[:, full:FF, :].rearrange("l p n -> (l p) n")).then_inc(ld_wf.sem, 16)
            v = row("L0_ffn_b1")
            for m in range(2):
                o = m * FF
                sp.dma_start(b1c[:, m, 0:FC - 1], v[:, o:o + full].rearrange("l (c p) -> p (l c)", p=P), allow_slow_non_contiguous=True).then_inc(ld_wf.sem, 16)
                sp.dma_start(b1c[0:FF - full, m, FC - 1:FC], v[:, o + full:o + FF].rearrange("l p -> p l"), allow_slow_non_contiguous=True).then_inc(ld_wf.sem, 16)
            for m, name in enumerate(("L0_ffn_ln_g", "L0_ffn_ln_b")):
                sp.dma_start(lngb[:, m:m + 1], row(name).rearrange("l p -> p l"), allow_slow_non_contiguous=True).then_inc(ld_wf.sem, 16)
            sp.dma_start(b2c[:, 0:1], row("L0_ffn_b2").rearrange("l p -> p l"), allow_slow_non_contiguous=True).then_inc(ld_wf.sem, 16)

        def tail_loads(sp):
            def load(dst, src, **how):
                sp.dma_start(dst, src, **how).then_inc(ld_tail.sem, 16)

            load(wqa[:, :], A["L1_attn_Wqa"])
            load(wqb[:, 0, :], A["L1_attn_Wqb"])
            load(wkva[:, :], A["L1_attn_Wkva"])
            load(wkvn[:, :, :, :], A["L1_attn_Wkvb"].rearrange("k (r d m) -> k r d m", r=KVH, d=QD))
            load(wout[:, :], A["L1_attn_Wout"])
            load(boutc[:, :], A["L1_attn_bout"].rearrange("(p o) -> p o", o=1), allow_slow_non_contiguous=True)
            load(b1e[:, :], A["L1_ffn_b1"].rearrange("e (c p) -> p (e c)", p=P), allow_slow_non_contiguous=True)
            load(b2e[:, :], A["L1_ffn_b2"])
            load(wg[:, :], A["L1_ffn_Wg"])
            load(bgb[:, :], A["L1_ffn_bg"].rearrange("(o e) -> o e", o=1).broadcast_to([P, NE]))

        def swap_weights(dve):
            dve.wait_ge(ld_tail.sem, 16 * TAIL_LOADS)
            dve.tensor_copy(wvb[:, :].rearrange("k (r d) -> k r d", r=KVH), wkvn[:, :, :, 1])
            dve.tensor_copy(wkb[:, 0, :].rearrange("k (r j d) -> k r j d", r=KVH, j=GRP),
                            wkvn[:, :, :, 0].unsqueeze(2).broadcast_to([KVL, KVH, GRP, QD])).then_inc(cswap.sem, 1)
            dve.wait_ge(cswap.sem, 1)
            for w in (wqb, wkb):
                ins = dve.tensor_copy(w[:, 1, :].rearrange("k (c s) -> k c s", s=2),
                                      w[:, 0, :].rearrange("k (c s) -> k c s", s=2)[:, :, ::-1])
            ins.then_inc(cswap.sem, 1)

        def gru_pe(pe):
            pe.wait_ge(ld_const.sem, 16)
            pe.wait_ge(ld_x.sem, 16)
            for g in range(NB * NT // 4):
                if g >= 4:
                    pe.wait_ge(x_kept.sem, g - 3)
                for t in range(4):
                    mm = pe.transpose(bank[2 + g % 4][:, t * P:(t + 1) * P], xtok[:, 4 * g + t, :], ident)
                mm.then_inc(x_turned.sem, 1)
            pe.wait_ge(ld_gru.sem, 16 * 4)
            pe.wait_ge(x_kept.sem, NB * NT // 4)
            for s, live in steps(pe, NB, 1):
                if live(0):
                    ln_turn_in(pe, LN_A1 + s, lnin)
                if live(1):
                    pe.wait_ge(ln_out.sem, ln_out.after(LN_A1 + s - 1))
                    pe.wait_ge(gru_b.sem, gru_b.after(s - 2))
                    for m in range(2):
                        mm = pe.matmul(bank[2][:, m * SEQ:(m + 1) * SEQ], wzh[:, m, :], xnT[:, :], start=True, stop=True)
                    mm.then_inc(zh_done.sem, 1)
                if live(0):
                    ln_turn_out(pe, LN_A1 + s)
            for s, live in steps(pe, NB, 1):
                if live(0):
                    ln_turn_in(pe, LN_A2 + s, lnin)
                    ln_turn_out(pe, LN_A2 + s)

        def gru_act(act):
            act.wait_ge(ld_gru.sem, 16 * 4)
            for s, live in steps(act, NB, 1):
                if live(1):
                    act.wait_ge(zh_done.sem, zh_done.after(s - 1))
                    act.wait_ge(gru_b.sem, gru_b.after(s - 2))
                    act.activation(zs[:, :], bank[2][:, 0:SEQ], ACT.Sigmoid, bias=bzh[:, 0:1]).then_inc(z_sig.sem, 1)
                if live(0):
                    i = LN_A1 + s
                    act.wait_ge(ln_t2.sem, ln_t2.after(i))
                    act.activation(xnT[:, :], bank[1][:, 0:SEQ], ACT.Copy).then_inc(ln_out.sem, 1)
            for s, live in steps(act, NB, 1):
                if live(0):
                    i = LN_A2 + s
                    act.wait_ge(ln_t2.sem, ln_t2.after(i))
                    act.activation(uT[:, seq_cols(s)], bank[1][:, 0:SEQ], ACT.Copy).then_inc(ln_out.sem, 1)

        def gru_dve(dve):
            for g in range(NB * NT // 4):
                dve.wait_ge(x_turned.sem, g + 1)
                dve.tensor_copy(xT[:, g * 512:(g + 1) * 512], bank[2 + g % 4][:, :]).then_inc(x_kept.sem, 1)
            dve.wait_ge(x_kept.sem, NB * NT // 4)
            dve.wait_ge(ld_gru.sem, 16 * 4)
            for s, live in steps(dve, NB, 1):
                if live(0):
                    i = LN_A1 + s
                    dve.wait_ge(ln_t1.sem, ln_t1.after(i - 1))
                    dve.tensor_copy(lnin[:, :], xT[:, seq_cols(s)]).then_inc(ln_in.sem, 1)
                    ln_normalise(dve, i)
                if live(1):
                    b = s - 1
                    dve.wait_ge(z_sig.sem, z_sig.after(b))
                    dve.wait_ge(gru_scan.sem, gru_scan.after(b - 1))
                    dve.tensor_scalar(za[:, :], zs[:, :], -1.0, 1.0, ALU.mult, ALU.add).then_inc(gru_a.sem, 1)
                    dve.scalar_tensor_tensor(out=zb[:, :], in0=bank[2][:, SEQ:2 * SEQ], scalar=bzh[:, 1:2], in1=zs[:, :],
                                             op0=ALU.add, op1=ALU.mult).then_inc(gru_b.sem, 1)
                    dve.wait_ge(gru_a.sem, gru_a.after(b))
                    dve.wait_ge(gru_b.sem, gru_b.after(b))
                    dve.wait_ge(gru_res.sem, gru_res.after(b - 1))
                    dve.tensor_tensor_scan(hs[:, :], za[:, :], zb[:, :], 0.0, ALU.mult, ALU.add).then_inc(gru_scan.sem, 1)
                    dve.wait_ge(gru_scan.sem, gru_scan.after(b))
                    dve.tensor_tensor(xT[:, seq_cols(b)], xT[:, seq_cols(b)], hs[:, :], ALU.add).then_inc(gru_res.sem, 1)
            for s, live in steps(dve, NB, 1):
                if live(0):
                    i = LN_A2 + s
                    dve.wait_ge(gru_res.sem, gru_res.after(s))
                    dve.wait_ge(ln_t1.sem, ln_t1.after(i - 1))
                    dve.tensor_copy(lnin[:, :], xT[:, seq_cols(s)]).then_inc(ln_in.sem, 1)
                    ln_normalise(dve, i)
            dve.wait_ge(ln_out.sem, ln_out.after(LN_A2 + NB - 1))

        GROUPS = [(0, r, 0, GRP, 1) for r in range(KVH)] + [(1, r, j, 2, 2) for r in range(KVH) for j in (0, 2)]
        NG = len(GROUPS)
        G_T, G_V = 2, 3

        def lat_pe(pe):
            pe.wait_ge(ld_tail.sem, 16 * TAIL_LOADS)
            pe.wait_ge(cast_done.sem, 4)
            pe.wait_ge(cswap.sem, 2)
            pe.wait_ge(f_res.sem, f_res.after(DEPTH * NB - 1))
            for s, live in steps(pe, NB, 1):
                b = s - 1
                if live(1):
                    for g in range(NG + G_V):
                        G = NG * b + g
                        if g < NG:
                            t, r, j0, nh, nk = GROUPS[g]
                            if g == 0:
                                pe.wait_ge(c_rope.sem, c_rope.after(b))
                                pe.wait_ge(cv_ev.sem, cv_ev.after(b))
                            pe.wait_ge(c_exp.sem, c_exp.after(G - 3))
                            sc = bank[5 + g % 3]
                            pe.matmul(sc[:, :], identb[:, :], causal[:, t, :], start=True, stop=False, skip_group_check=True)
                            pe.matmul(sc[:, :], cq[32 * r:32 * r + 32, t * P:(t + 1) * P],
                                      ckm[32 * r:32 * r + 32, j0:j0 + nh, 0:nk * P],
                                      start=False, stop=True, skip_group_check=True).then_inc(c_s.sem, 1)
                        if g >= G_V:
                            t, r, j0, nh, nk = GROUPS[g - G_V]
                            pe.wait_ge(c_ptev.sem, c_ptev.after(G - G_V))
                            if g == G_V:
                                pe.wait_ge(c_norm.sem, c_norm.after(b - 1))
                            for hh in range(nh):
                                for kb in range(nk):
                                    o = t * P + (r * GRP + j0 + hh) * QD
                                    k = (hh * nk + kb) * P
                                    mm = pe.matmul(bank[4][:, o:o + QD], cpT[:, (g - G_V) % 2, k:k + P],
                                                   cv[:, kb, r * QD:(r + 1) * QD], start=(kb == 0), stop=(kb == nk - 1))
                            mm.then_inc(c_pv.sem, 1)
                        if G_T <= g < NG + G_T:
                            pe.wait_ge(c_exp.sem, c_exp.after(G - G_T))
                            pe.wait_ge(c_ptev.sem, c_ptev.after(G - G_T - 1))
                            for k in range(4):
                                mm = pe.transpose(bank[3][:, k * P:(k + 1) * P], cp[:, (g - G_T) % 3, k * P:(k + 1) * P], ident)
                            mm.then_inc(c_pt.sem, 1)
                        if g == 3 and s_live0(s):
                            ln_turn_in(pe, LN_C + s, lnin)
                        if g == 6 and s_live0(s):
                            ln_turn_out(pe, LN_C + s)
                        if g == 8 and s_live0(s):
                            lat_down(pe, s)
                    pe.wait_ge(c_norm.sem, c_norm.after(b))
                    pe.wait_ge(lat_ev.sem, lat_ev.after(s if s_live0(s) else b))
                    for t in range(NT):
                        mm = pe.transpose(bank[2][:, t * P:(t + 1) * P], co[:, t, :], ident)
                    mm.then_inc(c_ot.sem, 1)
                    if s_live0(s):
                        lat_up(pe, s)
                    pe.wait_ge(c_otev.sem, c_otev.after(b))
                    pe.matmul(bank[2][:, SEQ:2 * SEQ], wout[:, :], coT[:, :], start=True, stop=True).then_inc(c_y.sem, 1)
                elif live(0):
                    ln_turn_in(pe, LN_C + s, lnin)
                    ln_turn_out(pe, LN_C + s)
                    lat_down(pe, s)
                    lat_up(pe, s)

        def s_live0(s):
            return not isinstance(s, int) or s < NB

        def lat_down(pe, s):
            pe.wait_ge(ln_out.sem, ln_out.after(LN_C + s))
            pe.wait_ge(c_res.sem, c_res.after(s - 2))
            pe.matmul(bank[2][0:QL, 0:SEQ], wqa[:, :], xnT[:, :], start=True, stop=True)
            pe.matmul(bank[2][0:KVL, SEQ:2 * SEQ], wkva[:, :], xnT[:, :], start=True, stop=True).then_inc(lat_mm.sem, 1)

        def lat_up(pe, s):
            pe.wait_ge(lat_ev.sem, lat_ev.after(s))
            pe.wait_ge(c_norm.sem, c_norm.after(s - 1))
            for m in range(2):
                pe.matmul(bank[3][:, m * SEQ:(m + 1) * SEQ], wqb[:, m, :], cqa[:, :], start=True, stop=True)
                pe.matmul(bank[4][:, m * SEQ:(m + 1) * SEQ], wkb[:, m, :], ckva[:, :], start=True, stop=True)
            for t in range(NT):
                mm = pe.matmul(bank[0][:, t * 32:(t + 1) * 32], ckva[:, t * P:(t + 1) * P], wvb[:, :], start=True, stop=True)
            mm.then_inc(c_proj.sem, 1)

        def lat_act(act):
            act.preload_act_table(ACT.Exp)
            for s, live in steps(act, NB, 1):
                b = s - 1

                def prefix(part):
                    if part == 0:
                        act.wait_ge(ln_t2.sem, ln_t2.after(LN_C + s))
                        act.activation(xnT[:, :], bank[1][:, 0:SEQ], ACT.Copy).then_inc(ln_out.sem, 1)
                    if part == 1:
                        act.wait_ge(lat_mm.sem, lat_mm.after(s))
                        act.wait_ge(c_proj.sem, c_proj.after(s - 1))
                        act.activation(cqa[:, :], bank[2][0:QL, 0:SEQ], ACT.Copy)
                        act.activation(ckva[:, :], bank[2][0:KVL, SEQ:2 * SEQ], ACT.Copy).then_inc(lat_ev.sem, 1)
                    if part == 2:
                        act.wait_ge(c_proj.sem, c_proj.after(s))
                        act.activation(cv[:, :, :].rearrange("p t d -> p (t d)"), bank[0][:, 0:NT * 32], ACT.Copy).then_inc(cv_ev.sem, 1)

                if live(1):
                    for g in range(NG + G_V):
                        G = NG * b + g
                        if g >= G_V:
                            act.wait_ge(c_pt.sem, c_pt.after(G - G_V))
                            act.wait_ge(c_pv.sem, c_pv.after(G - G_V - 2))
                            act.activation(cpT[:, (g - G_V) % 2, :], bank[3][:, :], ACT.Copy).then_inc(c_ptev.sem, 1)
                        if g < NG:
                            t, r, j0, nh, nk = GROUPS[g]
                            act.wait_ge(c_nb.sem, c_nb.after(G))
                            act.wait_ge(c_pt.sem, c_pt.after(G - 3))
                            act.wait_ge(c_sum.sem, c_sum.after(G - 3))
                            n = nk * P
                            for hh in range(nh):
                                ins = act.activation(cp[:, g % 3, hh * n:(hh + 1) * n], bank[5 + g % 3][:, hh * n:(hh + 1) * n],
                                                     ACT.Exp, scale=QD ** -0.5, bias=cnb[:, g % 3, hh:hh + 1])
                            ins.then_inc(c_exp.sem, 1)
                        if g == 7 and s_live0(s):
                            prefix(0)
                        if g == 9 and s_live0(s):
                            prefix(1)
                    act.wait_ge(c_ot.sem, c_ot.after(b))
                    act.wait_ge(c_y.sem, c_y.after(b - 1))
                    act.activation(coT[:, :], bank[2][:, 0:SEQ], ACT.Copy).then_inc(c_otev.sem, 1)
                    if s_live0(s):
                        prefix(2)
                elif live(0):
                    prefix(0)
                    prefix(1)
                    prefix(2)

        def lat_dve(dve):
            dve.wait_ge(f_res.sem, f_res.after(DEPTH * NB - 1))
            dve.tensor_tensor(xT[:, :], xT[:, :], uT[:, 0:NB * SEQ], ALU.add).then_inc(add_u.sem, 1)
            dve.wait_ge(add_u.sem, 1)
            dve.wait_ge(ld_tail.sem, 16 * TAIL_LOADS)
            for s, live in steps(dve, NB, 1):
                b = s - 1

                def norm_in():
                    i = LN_C + s
                    dve.wait_ge(ln_t1.sem, ln_t1.after(i - 1))
                    dve.tensor_copy(lnin[:, :], xT[:, seq_cols(s)]).then_inc(ln_in.sem, 1)

                def rotate():
                    dve.wait_ge(c_proj.sem, c_proj.after(s))
                    dve.wait_ge(c_s.sem, c_s.after(NG * s - 1))
                    chain = lambda k: dve.wait_ge(c_rc.sem, c_rc.after(s, k))
                    dve.tensor_tensor(ct[:, 0, :], bank[3][:, :], rope, ALU.mult).then_inc(c_rc.sem, 1)
                    dve.tensor_tensor(ct[:, 1, :], bank[4][:, :], rope, ALU.mult).then_inc(c_rc.sem, 1)
                    chain(2)
                    dve.tensor_tensor(ck[:, :], ct[:, 1, 0:SEQ], ct[:, 1, SEQ:], ALU.add).then_inc(c_rc.sem, 1)
                    dve.tensor_tensor(cq[:, :], ct[:, 0, 0:SEQ], ct[:, 0, SEQ:], ALU.add).then_inc(c_rc.sem, 1)
                    chain(4)
                    for j in range(GRP):
                        ins = dve.tensor_scalar(ckm[:, j, :], ck[:, :], col(cst("rowmask"), j), None, ALU.mult)
                    ins.then_inc(c_rope.sem, 1)

                if live(1):
                    for g in range(NG + 1):
                        G = NG * b + g
                        if g < NG:
                            t, r, j0, nh, nk = GROUPS[g]
                            dve.wait_ge(c_s.sem, c_s.after(G))
                            dve.wait_ge(c_nb.sem, c_nb.after(G - 1))
                            dve.tensor_reduce(cmx[:, 0:nh], bank[5 + g % 3][:, :].rearrange("p (h k) -> p h k", h=nh), AX.X,
                                              ALU.max).then_inc(c_max.sem, 1)
                            dve.wait_ge(c_max.sem, c_max.after(G))
                            dve.wait_ge(c_exp.sem, c_exp.after(G - 3))
                            dve.tensor_scalar(cnb[:, g % 3, 0:nh], cmx[:, 0:nh], -(QD ** -0.5), None, ALU.mult).then_inc(c_nb.sem, 1)
                        if g >= 1:
                            t, r, j0, nh, nk = GROUPS[g - 1]
                            dve.wait_ge(c_exp.sem, c_exp.after(G - 1))
                            if g == 1:
                                dve.wait_ge(c_rcp.sem, c_rcp.after(b - 1))
                            dve.tensor_reduce(csum[:, t, r * GRP + j0:r * GRP + j0 + nh],
                                              cp[:, (g - 1) % 3, :].rearrange("p (h k) -> p h k", h=nh), AX.X,
                                              ALU.add).then_inc(c_sum.sem, 1)
                        if g == 2 and s_live0(s):
                            norm_in()
                        if g == 4 and s_live0(s):
                            ln_normalise(dve, LN_C + s)
                    dve.wait_ge(c_sum.sem, c_sum.after(NG * b + NG - 1))
                    dve.wait_ge(c_norm.sem, c_norm.after(b - 1))
                    dve.reciprocal(crc[:, :, :], csum[:, :, :]).then_inc(c_rcp.sem, 1)
                    dve.wait_ge(c_rcp.sem, c_rcp.after(b))
                    dve.wait_ge(c_pv.sem, c_pv.after(NG * b + NG - 1))
                    dve.wait_ge(c_ot.sem, c_ot.after(b - 1))
                    dve.tensor_tensor(co[:, :, :].rearrange("p t (h d) -> p (t h) d", d=QD),
                                      bank[4][:, 0:NT * P].rearrange("p (h d) -> p h d", d=QD),
                                      crc[:, :, :].rearrange("p t h -> p (t h)").unsqueeze(2).broadcast_to([P, NT * QH, QD]),
                                      ALU.mult).then_inc(c_norm.sem, 1)
                    if s_live0(s):
                        rotate()
                    dve.wait_ge(c_y.sem, c_y.after(b))
                    dve.scalar_tensor_tensor(out=xT[:, seq_cols(b)], in0=bank[2][:, SEQ:2 * SEQ], scalar=boutc[:, 0:1],
                                             in1=xT[:, seq_cols(b)], op0=ALU.add, op1=ALU.add).then_inc(c_res.sem, 1)
                elif live(0):
                    norm_in()
                    ln_normalise(dve, LN_C + s)
                    rotate()

        def gate_pe(pe):
            pe.wait_ge(c_res.sem, c_res.after(NB - 1))
            for s, live in steps(pe, NB, 1):
                if live(0):
                    ln_turn_in(pe, LN_D + s, lnin)
                if live(1):
                    b = s - 1
                    pe.wait_ge(ln_out.sem, ln_out.after(LN_D + b))
                    pe.wait_ge(d_logit.sem, d_logit.after(b - 1))
                    for t in range(NT):
                        mm = pe.matmul(bank[2][:, t * NE:(t + 1) * NE], xnT[:, t * P:(t + 1) * P], wg[:, :], start=True, stop=True)
                    mm.then_inc(d_lmm.sem, 1)
                    pe.wait_ge(d_w.sem, d_w.after(b))
                    pe.wait_ge(d_wTev.sem, d_wTev.after(b - 1))
                    for t in range(NT):
                        mm = pe.transpose(bank[3][0:NE, t * P:(t + 1) * P], dw1[:, t, :], ident)
                    mm.then_inc(d_wT.sem, 1)
                    pe.wait_ge(d_wTev.sem, d_wTev.after(b))
                    pe.wait_ge(d_acc.sem, d_acc.after(b - 1))
                    for t in range(NT):
                        mm = pe.matmul(bank[4][:, t * P:(t + 1) * P], dwT[:, t * P:(t + 1) * P], b2e[:, :], start=True, stop=True)
                    mm.then_inc(d_b2.sem, 1)
                if live(0):
                    ln_turn_out(pe, LN_D + s)

        def gate_act(act):
            for s, live in steps(act, NB, 1):
                if live(1):
                    b = s - 1
                    act.wait_ge(d_diff.sem, d_diff.after(b))
                    act.wait_ge(d_w.sem, d_w.after(b - 1))
                    act.activation(dexp[:, :], ddiff[:, :], ACT.Exp).then_inc(d_e.sem, 1)
                    act.wait_ge(d_wT.sem, d_wT.after(b))
                    act.wait_ge(d_b2.sem, d_b2.after(b - 1))
                    act.activation(dwT[:, :], bank[3][0:NE, 0:SEQ], ACT.Copy).then_inc(d_wTev.sem, 1)
                if live(0):
                    i = LN_D + s
                    act.wait_ge(ln_t2.sem, ln_t2.after(i))
                    act.activation(xnT[:, :], bank[1][:, 0:SEQ], ACT.Copy)
                    act.activation(xnA[:, seq_cols(s)], bank[1][:, 0:SEQ], ACT.Copy).then_inc(ln_out.sem, 1)

        def gate_dve(dve):
            dve.wait_ge(c_res.sem, c_res.after(NB - 1))
            for s, live in steps(dve, NB, 1):
                if live(0):
                    i = LN_D + s
                    dve.wait_ge(ln_t1.sem, ln_t1.after(i - 1))
                    dve.tensor_copy(lnin[:, :], xT[:, seq_cols(s)]).then_inc(ln_in.sem, 1)
                    dve.wait_ge(ln_t1.sem, ln_t1.after(i))
                    dve.tensor_copy(acc[:, seq_cols(s)], bank[0][:, 0:SEQ]).then_inc(d_tok.sem, 1)
                    ln_normalise(dve, i)
                if live(1):
                    b = s - 1
                    k = 0

                    def link(ins):
                        nonlocal k
                        k += 1
                        ins.then_inc(d_ch.sem, 1)
                        dve.wait_ge(d_ch.sem, d_ch.after(b, k))
                        hold(dve)

                    dve.wait_ge(d_lmm.sem, d_lmm.after(b))
                    dve.wait_ge(d_w.sem, d_w.after(b - 1))
                    dve.tensor_tensor(dlg[:, :, :], bank[2][:, 0:NT * NE].rearrange("p (t e) -> p t e", t=NT),
                                      bgb[:, :].unsqueeze(1).broadcast_to([P, NT, NE]), ALU.add).then_inc(d_logit.sem, 1)
                    dve.wait_ge(d_logit.sem, d_logit.after(b))
                    hold(dve)
                    for t in range(NT):
                        link(dve.max(dmx[:, t, :], dlg[:, t, :]))
                    for t in range(NT):
                        link(dve.max_index(dix[:, t, :], dmx[:, t, :], dlg[:, t, :]))
                    link(dve.tensor_copy(dixf[:, :, :], dix[:, :, 0:2]))
                    dve.wait_ge(d_e.sem, d_e.after(b - 1))
                    dve.tensor_tensor(ddiff[:, :], dmx[:, :, 1], dmx[:, :, 0], ALU.subtract).then_inc(d_diff.sem, 1)
                    dve.wait_ge(d_e.sem, d_e.after(b))
                    link(dve.tensor_scalar(dden[:, :], dexp[:, :], 1.0, None, ALU.add))
                    link(dve.reciprocal(dp[:, 0, :], dden[:, :]))
                    link(dve.tensor_tensor(dp[:, 1, :], dexp[:, :], dp[:, 0, :], ALU.mult))
                    dve.wait_ge(d_wT.sem, d_wT.after(b - 1))
                    for t in range(NT):
                        link(dve.tensor_scalar(dw1[:, t, :], cst("iota"), dixf[:, t, 0:1], dp[:, 0, t:t + 1], ALU.is_equal, ALU.mult))
                        link(dve.tensor_scalar(dw2[:, t, :], cst("iota"), dixf[:, t, 1:2], dp[:, 1, t:t + 1], ALU.is_equal, ALU.mult))
                    link(dve.tensor_tensor(dw1[:, :, :], dw1[:, :, :], dw2[:, :, :], ALU.add))
                    dve.tensor_copy(wA[:, ds(b * NT, NT) if not isinstance(b, int) else slice(b * NT, b * NT + NT), :],
                                    dw1[:, :, :]).then_inc(d_w.sem, 1)
                    dve.wait_ge(d_b2.sem, d_b2.after(b))
                    dve.wait_ge(d_tok.sem, d_tok.after(b))
                    dve.tensor_tensor(acc[:, seq_cols(b)], acc[:, seq_cols(b)], bank[4][:, 0:SEQ], ALU.add).then_inc(d_acc.sem, 1)

        def expert_slots(eng):
            for s, live in steps(eng, NB, 1):
                for e in range(NE):
                    yield s, e, live(0), (live(0) if e else live(1)), NE * s + e

        def experts_pe(pe):
            pe.wait_ge(d_acc.sem, d_acc.after(NB - 1))
            pe.wait_ge(ld_exp.sem, 32)
            for s, e, first, second, n in expert_slots(pe):
                if first:
                    for hb in range(2):
                        pe.wait_ge(e_gelu.sem, e_gelu.after(2 * (n - 2) + hb))
                        for c in range(2):
                            ch = 2 * hb + c
                            mm = pe.matmul(bank[2 * (e % 2) + hb][:, c * SEQ:(c + 1) * SEQ], w1e[:, e, ch * P:(ch + 1) * P],
                                           xnA[:, seq_cols(s)], start=True, stop=True)
                        mm.then_inc(e_up.sem, 1)
                if second:
                    m, pe_e = n - 1, (e - 1) % NE
                    pe.wait_ge(e_gelu.sem, e_gelu.after(2 * m + 1))
                    pe.wait_ge(e_acc.sem, e_acc.after(m - 2))
                    for t in range(NT):
                        for c in range(EC):
                            mm = pe.matmul(bank[4 + pe_e % 2][:, t * P:(t + 1) * P], eh[:, pe_e % 2, c, t * P:(t + 1) * P],
                                           w2e[:, pe_e, c, :], start=(c == 0), stop=(c == EC - 1))
                    mm.then_inc(e_down.sem, 1)

        def experts_act(act):
            act.preload_act_table(ACT.Gelu)
            for s, e, first, second, n in expert_slots(act):
                if first:
                    act.wait_ge(e_down.sem, e_down.after(n - 2))
                    for hb in range(2):
                        act.wait_ge(e_up.sem, e_up.after(2 * n + hb))
                        for c in range(2):
                            ch = 2 * hb + c
                            ins = act.activation(eh[:, e % 2, ch, :], bank[2 * (e % 2) + hb][:, c * SEQ:(c + 1) * SEQ], ACT.Gelu,
                                                 bias=b1e[:, e * EC + ch:e * EC + ch + 1])
                        ins.then_inc(e_gelu.sem, 1)

        def experts_dve(dve):
            dve.wait_ge(d_acc.sem, d_acc.after(NB - 1))
            for s, e, first, second, n in expert_slots(dve):
                if second:
                    m, pe_e = n - 1, (e - 1) % NE
                    b = s if e else s - 1
                    dve.wait_ge(e_down.sem, e_down.after(m))
                    dve.wait_ge(e_acc.sem, e_acc.after(m - 1))
                    for t in range(NT):
                        if isinstance(b, int):
                            w = wA[:, b * NT + t, pe_e:pe_e + 1]
                        else:
                            w = wA[:, ds(b * NT + t, 1), pe_e:pe_e + 1].rearrange("p t e -> p (t e)")
                        a = acc[:, seq_cols(b, P, t * P)]
                        ins = dve.scalar_tensor_tensor(out=a, in0=bank[4 + pe_e % 2][:, t * P:(t + 1) * P], scalar=w, in1=a,
                                                       op0=ALU.mult, op1=ALU.add)
                    ins.then_inc(e_acc.sem, 1)

        block = ctx.enter_context(nc.Block())

        @block.sync
        def _(sp):
            for x in credited["sp"]:
                x.start(sp)
            sp.dma_start(const[:, :], A["const"]).then_inc(ld_const.sem, 16)
            sp.dma_start(xtok[:, :, :], A["L0_attn_x"].rearrange("b (t p) d -> p (b t) d", p=P)).then_inc(ld_x.sem, 16)
            for m, (w, b) in enumerate((("L0_attn_Wz", "L0_attn_bz"), ("L0_attn_Wh", "L0_attn_bh"))):
                sp.dma_start(wzh[:, m, :], A[w]).then_inc(ld_gru.sem, 16)
                sp.dma_start(bzh[:, m:m + 1], A[b].rearrange("(p o) -> p o", o=1), allow_slow_non_contiguous=True).then_inc(ld_gru.sem, 16)
            tail_loads(sp)
            sp.wait_ge(zeroed.sem, 2)
            with sp.Fori(0, DEPTH) as layer:
                load_layer(sp, layer)
                attention_sp(sp, layer)
            sp.wait_ge(y_mm.sem, y_mm.after(DEPTH * NB - 1))
            sp.dma_start(w1e, A["L1_ffn_W1"].rearrange("e p f -> p e f")).then_inc(ld_exp.sem, 16)
            sp.dma_start(w2e, A["L1_ffn_W2"].rearrange("e (c p) d -> p e c d", p=P)).then_inc(ld_exp.sem, 16)
            with sp.Fori(0, NB) as b:
                sp.wait_ge(e_acc.sem, e_acc.after(NE * b + NE - 1))
                hold(sp)
                sp.dma_start(out[ds(b, 1)].rearrange("b (t p) d -> p (b t) d", p=P),
                             acc[:, seq_cols(b)].rearrange("p (t d) -> p t d", t=NT)).then_inc(st_out.sem, 16)
            sp.wait_ge(st_out.sem, 16 * NB)

        @block.gpsimd
        def _(pool):
            for x in credited["pool"]:
                x.start(pool)
            pool.memset(vBD[:, 0], 0.0).then_inc(zeroed.sem, 1)
            pool.memset(vBD[:, 1], 0.0).then_inc(zeroed.sem, 1)
            pool.wait_ge(ld_const.sem, 16)
            pool.tensor_copy(bandrhs[:, :], cst("band")[0:2 * WIN, :]).then_inc(cast_done.sem, 1)
            pool.tensor_copy(bandsel[:, :, :], cst("bandsel")[0:2 * WIN, :].rearrange("p (t q) -> p t q", t=NT)).then_inc(cast_done.sem, 1)
            pool.tensor_copy(causal[:, :, :], cst("causal").rearrange("p (t q) -> p t q", t=NT)).then_inc(cast_done.sem, 1)
            pool.tensor_copy(identb[:, :], ident).then_inc(cast_done.sem, 1)
            with pool.Fori(0, DEPTH) as layer:
                attention_pool(pool, layer)

        @block.scalar
        def _(act):
            for x in credited["act"]:
                x.start(act)
            gru_act(act)
            act.wait_ge(zeroed_dve.sem, 1)
            with act.Fori(0, DEPTH) as layer:
                act.preload_act_table(ACT.Exp)
                attention_act(act, layer)
                act.preload_act_table(ACT.Gelu)
                mlp_act(act, layer)
            lat_act(act)
            gate_act(act)
            experts_act(act)

        @block.vector
        def _(dve):
            for x in credited["dve"]:
                x.start(dve)
            dve.memset(kBD[:, :, :, :, :], 0.0)
            dve.memset(uT[:, NB * SEQ:], 0.0)
            dve.memset(lns[:, 0:1], 0.0)
            dve.memset(xs[:, 0:1], 0.0).then_inc(zeroed_dve.sem, 1)
            dve.wait_ge(zeroed_dve.sem, 1)
            gru_dve(dve)
            swap_weights(dve)
            with dve.Fori(0, DEPTH) as layer:
                attention_dve(dve, layer)
                mlp_dve(dve, layer)
            lat_dve(dve)
            gate_dve(dve)
            experts_dve(dve)

        @block.tensor
        def _(pe):
            for x in credited["pe"]:
                x.start(pe)
            gru_pe(pe)
            pe.wait_ge(cast_done.sem, 4)
            pe.wait_ge(zeroed_dve.sem, 1)
            with pe.Fori(0, DEPTH) as layer:
                pe.wait_ge(ld_wa.sem, (layer + 1) * 16 * LA_LOADS)
                attention_pe(pe, layer)
                mlp_pe(pe, layer)
            lat_pe(pe)
            gate_pe(pe)
            experts_pe(pe)


def constants():
    c = np.zeros((P, CONST_N), np.float32)

    def put(name, v):
        a, b = CONST_COLS[name]
        c[:v.shape[0], a:b] = v.reshape(v.shape[0], b - a)

    f32 = np.float32
    put("ident", np.eye(P, dtype=f32))
    half = np.arange(0, DH, 2, dtype=f32)
    inv_freq = (f32(1.0) / f32(10000.0) ** (half / f32(DH))).astype(f32)
    tok = np.arange(SEQ, dtype=f32)
    freqs = (tok[:, None] * inv_freq[None, :]).astype(np.float64)
    base = ((half + f32(0.4 * DH)) / f32(1.4 * DH)).astype(np.float64)
    power = ((tok - SEQ // 2) / f32(WIN // 2)).astype(np.float64)
    scale = base[None, :] ** power[:, None]
    cos, sin = np.cos(freqs), np.sin(freqs)
    rot = np.zeros((SEQ, 4, DH))
    for m, s in ((0, scale), (2, 1.0 / scale)):
        rot[:, m] = np.concatenate([cos * s, cos * s], -1)
        rot[:, m + 1] = np.concatenate([-sin * s, sin * s], -1)
    put("rot", rot.reshape(NT, P, 4, DH).transpose(1, 0, 2, 3).astype(f32))
    inv8 = (f32(1.0) / f32(10000.0) ** (np.arange(0, QD, 2, dtype=f32) / f32(QD))).astype(f32)
    ang = (tok[:, None] * inv8[None, :]).astype(np.float64)
    pair = (np.arange(P) % QD) // 2
    sign = np.where(np.arange(P) % 2 == 0, -1.0, 1.0)[:, None]
    put("rope", np.concatenate([np.cos(ang)[:, pair].T, np.sin(ang)[:, pair].T * sign], 1).astype(f32))
    rows = np.arange(P)
    put("rowmask", (rows[:, None] % (GRP * QD) // QD == np.arange(GRP)[None, :]).astype(f32))
    put("iota", np.tile(np.arange(NE, dtype=f32), (P, 1)))
    i, j = np.arange(WIN)[:, None], np.arange(2 * WIN)[None, :]
    band = np.where((i <= j) & (j <= i + WIN), 0.0, NEG)
    edge = np.where(j < WIN, NEG, 0.0) + 0.0 * i
    put("band", np.tile(np.concatenate([band, edge], 0), (1, HH)).astype(f32))
    sel = np.zeros((2 * WIN, NT, P), f32)
    for w in range(NWT):
        sel[np.arange(WIN), :, w * WIN + np.arange(WIN)] = 1.0
    sel[WIN + np.arange(WIN), 0, np.arange(WIN)] = 1.0
    put("bandsel", sel)
    tri = np.where(rows[None, :] <= rows[:, None], 0.0, NEG)
    put("causal", np.stack([np.tile(tri, (1, 4)), np.tile(np.concatenate([0.0 * tri, tri], 1), (1, 2))], 1).astype(f32))
    return c


_INS = ['L0_attn_x', 'L0_attn_Wz', 'L0_attn_bz', 'L0_attn_Wh', 'L0_attn_bh', 'L0_ffn_Wqkv', 'L0_ffn_q_scale',
        'L0_ffn_k_scale', 'L0_ffn_Wo', 'L0_ffn_ln_g', 'L0_ffn_ln_b', 'L0_ffn_W1', 'L0_ffn_b1', 'L0_ffn_W2', 'L0_ffn_b2',
        'L1_attn_Wqa', 'L1_attn_Wqb', 'L1_attn_Wkva', 'L1_attn_Wkvb', 'L1_attn_Wout', 'L1_attn_bout', 'L1_ffn_W1',
        'L1_ffn_b1', 'L1_ffn_W2', 'L1_ffn_b2', 'L1_ffn_Wg', 'L1_ffn_bg']


def kernel(**inputs):
    import concourse.bacc as _bacc
    from concourse.bass_utils import run_bass_kernel_spmd as _run

    nc = _bacc.Bacc("TRN2", target_bir_lowering=False, num_devices=1)
    arrays = {name: np.ascontiguousarray(inputs[name]) for name in _INS}
    arrays["const"] = constants()
    A = {}
    for name, a in arrays.items():
        A[name] = nc.dram_tensor(f"in_{name}_dram", a.shape, mybir.dt.from_np(a.dtype), kind="ExternalInput").ap()
    out = nc.dram_tensor("out_0_dram", (NB, SEQ, D), F32, kind="ExternalOutput").ap()
    mixed_kernel(nc, A, out)
    r = _run(nc, [{f"in_{name}_dram": a for name, a in arrays.items()}], core_ids=[0])
    return r.results[0]["out_0_dram"]
```

```python
import math
from contextlib import ExitStack

import numpy as np

import concourse.bass as bass
from concourse import mybir
from concourse.bass import ds

F32 = mybir.dt.float32
BF16 = mybir.dt.bfloat16
I32 = mybir.dt.int32
U32 = mybir.dt.uint32
ALU = mybir.AluOpType
ACT = mybir.ActivationFunctionType
AX = mybir.AxisListType

P = 128
D = 128
NB, SEQ = 8, 256
NT = SEQ // P
DEPTH = 6
HEADS, DH = 16, 64
INNER = HEADS * DH
WIN = 32
NWT = P // WIN
NW = SEQ // WIN
HH = HEADS // 2
HP = HH // 2
UPB = NT * 2
FF = int(D * 4 * 2 / 3)
FC = math.ceil(FF / P)
FSZ = [min(P, FF - P * c) for c in range(FC)]
QH, KVH, QL, KVL, QD = 16, 4, 64, 32, 8
GRP = QH // KVH
NE, DFF = 8, 512
EC = DFF // P
EPS = 1e-5
NEG = -1e30
MAGIC = float(0x5F3759DF)
NR_STEPS = 11
GATE_STEPS = 12
LN_STEPS = NR_STEPS + 4

CONST_COLS = {}
_at = 0
for _name, _n in (("ident", P), ("rot", NT * 4 * DH), ("rope", 2 * SEQ), ("rowmask", GRP), ("zsel", P), ("iota", NE),
                  ("band", 512), ("bandsel", NT * P), ("causal", NT * 512)):
    CONST_COLS[_name] = (_at, _at + _n)
    _at += _n
CONST_N = _at


class Signal:

    def __init__(self, sem, per=1, credit=0):
        self.sem, self.per, self.credit = sem, per, credit

    def after(self, n, k=None):
        return (n + self.credit) * self.per + (self.per if k is None else k) if self.per > 1 else n + self.credit + 1

    def start(self, eng):
        if self.credit:
            eng.sem_inc(self.sem, self.credit * self.per)


def steps(eng, count, lag):
    for s in range(lag):
        yield s, (lambda d, s=s: s >= d)
    with eng.Fori(lag, count) as s:
        yield s, (lambda d: True)
    for s in range(count, count + lag):
        yield s, (lambda d, s=s: s - d < count)


def mixed_kernel(nc, A, out):
    with ExitStack() as ctx:
        def sb(name, shape, dt=F32):
            return ctx.enter_context(nc.sbuf_tensor(name, shape, dt))

        def sig(name, per=1, credit=0):
            return Signal(ctx.enter_context(nc.semaphore(name)), per, credit)

        bank = [ctx.enter_context(nc.psum_tensor(f"bank{i}", [P, 512], F32)) for i in range(8)]

        const = sb("const", [P, CONST_N])

        def cst(name):
            a, b = CONST_COLS[name]
            return const[:, a:b]

        ident = cst("ident")
        rot_base = cst("rot").rearrange("p (t k d) -> p t k d", t=NT, k=4)
        rope = cst("rope")
        bandrhs = sb("bandrhs", [2 * WIN, 512], BF16)
        bandsel = sb("bandsel", [2 * WIN, NT, P], BF16)
        causal = sb("causal", [P, NT, 512], BF16)
        identb = sb("identb", [P, P], BF16)
        xT = sb("xT", [P, NB * SEQ])
        uT = sb("uT", [P, (NB + 1) * SEQ])
        lnin = sb("lnin", [P, SEQ])
        lns = sb("lns", [P, SEQ])
        lnk = sb("lnk", [P, NT, P])
        lnx = sb("lnx", [P, NT, P])
        lnst = sb("lnst", [P, NT, 6])
        lnmv = sb("lnmv", [P, NT, 2])
        lnve = sb("lnve", [P, NT])
        lny = sb("lny", [P, NT])
        lnt = sb("lnt", [P, NT])
        xnT = sb("xnT", [P, SEQ])
        wzh = sb("wzh", [P, 2, D])
        bzh = sb("bzh", [P, 2])
        zs = sb("zs", [P, SEQ])
        za = sb("za", [P, SEQ])
        zb = sb("zb", [P, SEQ])
        hs = sb("hs", [P, SEQ])
        wqkv = sb("wqkv", [P, 3 * INNER])
        wo = sb("wo", [P, HEADS // 2, D])
        qks = sb("qks", [P, 4, DH])
        rot = sb("rot_t", [P, NT, 4, DH])
        xs = sb("xs", [P, SEQ])
        sq = sb("sq", [P, HEADS, DH])
        sqh = sb("sqh", [P, HEADS, DH // 2])
        ss = sb("ss", [P, HEADS])
        rn = sb("rn", [P, HEADS])
        rnt = sb("rnt", [P, HEADS])
        sc8 = sb("sc8", [P, UPB, HH])
        t1 = sb("t1", [P, 2, HH, DH])
        t2 = sb("t2", [P, 2, HH, DH])
        kr0 = sb("kr0", [P, HH, DH])
        qr = sb("qr", [P, 2, HH * DH])
        kr = sb("kr", [P, 2, HH, DH])
        qT = sb("qT", [P, HP, P])
        kBD = sb("kBD", [P, 2, HP, 2, WIN + SEQ])
        vS = sb("vS", [P, UPB, 2, HP, DH])
        vBD = sb("vBD", [P, 2, NW, 2, HP, DH])
        mx = sb("mx", [P, 2, HH])
        nbias = sb("nbias", [P, 2, HH])
        pr = sb("pr", [P, 2, HH, 2 * WIN])
        psm = sb("psm", [P, 2, HH])
        rinv = sb("rinv", [P, 2, HH])
        pT = sb("pT", [P, HP, P])
        ob = sb("ob", [P, 2, HH, DH])
        attT = sb("attT", [P, HEADS // 2, SEQ])
        w1 = sb("w1", [P, 2 * FF])
        w2 = sb("w2", [P, FC, D])
        lngb = sb("lngb", [P, 2])
        b1c = sb("b1c", [P, 2, FC])
        b2c = sb("b2c", [P, 1])
        gs = sb("gs", [P, FC, SEQ])
        hT = sb("hT", [P, 2, FC, SEQ])

        wqa, wqb, wkva = sb("wqa", [P, QL]), sb("wqb", [QL, 2, P]), sb("wkva", [P, KVL])
        wkvn, wkb, wvb = sb("wkvn", [KVL, KVH, QD, 2]), sb("wkb", [KVL, 2, P]), sb("wvb", [KVL, KVH * QD])
        woutp, boutc = sb("woutp", [P, GRP, D]), sb("boutc", [P, 1])
        cqa, ckva = sb("cqa", [QL, SEQ]), sb("ckva", [KVL, SEQ])
        cq, ck = sb("cq", [P, SEQ]), sb("ck", [P, SEQ])
        cvn = sb("cvn", [P, NT, KVH, QD])
        cvp = sb("cvp", [P, NT, KVH, 32])
        zsel = cst("zsel")
        ZK = GRP * P // 32
        crs = sb("crs", [P, NT, 2, ZK])
        cmx, cnb = sb("cmx", [P, GRP]), sb("cnb", [P, 3, GRP])
        late = kBD[:, :, :, :, :].rearrange("p h q e k -> p (h q e k)")
        ckm = late[:, 0:1024].rearrange("p (j k) -> p j k", j=GRP)
        ct = late[:, 2048:3072].rearrange("p (m k) -> p m k", m=2)
        cp = late[:, 3072:4608].rearrange("p (g k) -> p g k", g=3)
        cpT = [vS[:, i].rearrange("p e q d -> p (e q d)") for i in range(UPB)] + [t1[:, i].rearrange("p h d -> p (h d)") for i in range(2)]
        NTB = len(cpT)
        cos_ = t2[:, :, :, :].rearrange("p m h d -> p m (h d)")
        late = attT[:, :, :].rearrange("p c k -> p (c k)")
        con = late[:, 0:1024].rearrange("p (t k) -> p t k", t=NT)
        wg, bgb, b2e = sb("wg", [P, NE]), sb("bgb", [P, NE]), sb("b2e", [NE, D])
        dlg, dmx = sb("dlg", [P, NT, NE]), sb("dmx", [P, NT, 8])
        dix, dixf = sb("dix", [P, NT, 8], U32), sb("dixf", [P, NT, 2])
        ddiff, dexp, dden, dp = sb("ddiff", [P, NT]), sb("dexp", [P, NT]), sb("dden", [P, NT]), sb("dp", [P, 2, NT])
        dw1, dw2, dwT = sb("dw1", [P, NT, NE]), sb("dw2", [P, NT, NE]), sb("dwT", [NE, SEQ])
        xnA = uT
        wA = sb("wA", [P, NB * NT, NE])
        acc = sb("acc", [P, NB * SEQ])
        late = vBD[:, :, :, :, :, :].rearrange("p h w e q d -> p (h w e q d)")
        w1e = late[:, 0:NE * DFF].rearrange("p (e f) -> p e f", e=NE)
        w2e = late[:, NE * DFF:2 * NE * DFF].rearrange("p (e c d) -> p e c d", e=NE, c=EC)
        eh = wqkv[:, 0:2 * EC * SEQ].rearrange("p (m c k) -> p m c k", m=2, c=EC)
        b1e = sb("b1e", [P, NE * EC])
        xtok = acc[:, :].rearrange("p (t d) -> p t d", d=D)

        ld_const, ld_x, ld_gru = sig("ld_const"), sig("ld_x"), sig("ld_gru")
        held = sig("held")
        ld_exp = sig("ld_exp")
        ld_tail, st_out = sig("ld_tail"), sig("st_out")
        cast_done = sig("cast_done")
        zeroed, zeroed_dve = sig("zeroed"), sig("zeroed_dve")
        x_turned, x_kept = sig("x_turned"), sig("x_kept")
        ln_in = sig("ln_in", credit=1)
        ln_t1 = sig("ln_t1", credit=1)
        ln_tok = sig("ln_tok", credit=1)
        ln_stats = sig("ln_stats", credit=1)
        ln_chain = sig("ln_chain", per=NR_STEPS + 3)
        ln_t2 = sig("ln_t2", credit=1)
        ln_out = sig("ln_out", credit=1)
        zh_done = sig("zh_done", credit=1)
        z_sig, gru_a, gru_b, gru_scan, gru_res = (sig(x, credit=1) for x in ("z_sig", "gru_a", "gru_b", "gru_scan", "gru_res"))
        ld_wa = sig("ld_wa")
        tabs = sig("tabs")
        xs_in = sig("xs_in")
        q_mm, k_mm, v_mm = (sig(x, credit=1) for x in ("q_mm", "k_mm", "v_mm"))
        qt_mm, kt_mm, s_mm = (sig(x, credit=4) for x in ("qt_mm", "kt_mm", "s_mm"))
        pt_mm, o_mm, ot_mm = (sig(x, credit=4) for x in ("pt_mm", "o_mm", "ot_mm"))
        y_mm = sig("y_mm", credit=6)
        q_sq, k_sq, v_ev = (sig(x, credit=2) for x in ("q_sq", "k_sq", "v_ev"))
        qt_ev, kt_ev, p_exp, pt_ev, ot_ev = (sig(x, credit=4) for x in ("qt_ev", "kt_ev", "p_exp", "pt_ev", "ot_ev"))
        q_mul, k_mul = sig("q_mul", credit=2), sig("k_mul", credit=2)
        s_max, s_nb, p_sum, p_inv, o_norm = (sig(x, credit=4) for x in ("s_max", "s_nb", "p_sum", "p_inv", "o_norm"))
        ss_red = sig("ss_red", per=2, credit=2)
        nr_chain = sig("nr_chain", per=NR_STEPS, credit=2)
        sc_done = sig("sc_done", credit=2)
        u_res = sig("u_res", credit=6)
        sq_half, q_add, k_add, k_norm = (sig(x, credit=2) for x in ("sq_half", "q_add", "k_add", "k_norm"))
        v_dma = [sig(f"v_dma{j}", per=16 * (10 if j % NT == 0 else 8), credit=1) for j in range(UPB)]
        ld_wf = sig("ld_wf")
        f_in = sig("f_in")
        h_mm, f_mm = sig("h_mm", per=FC, credit=2), sig("f_mm", credit=3)
        g_act, h_mul = sig("g_act", per=FC, credit=1), sig("h_mul", per=FC, credit=2)
        f_res = sig("f_res", credit=NB)
        add_u = sig("add_u")
        cswap, cvones = sig("cswap"), sig("cvones")
        lat_mm, lat_ev, c_pq, c_pk, c_pv = (sig(x, credit=2) for x in ("lat_mm", "lat_ev", "c_pq", "c_pk", "c_pv"))
        c_mq, c_mk, c_cq, c_ck, cv_ev, c_cv = (sig(x, credit=2) for x in ("c_mq", "c_mk", "c_cq", "c_ck", "cv_ev", "c_cv"))
        c_ckm = sig("c_ckm", per=3)
        c_s, c_max, c_nb, c_exp, c_pt, c_ptev = (sig(x, credit=24) for x in ("c_s", "c_max", "c_nb", "c_exp", "c_pt", "c_ptev"))
        c_o = sig("c_o", credit=6)
        c_oev, c_z, c_rz, c_nrm = (sig(x, credit=4) for x in ("c_oev", "c_z", "c_rz", "c_nrm"))
        c_out = [sig(f"c_out{t}", per=16 * KVH) for t in range(NT)]
        c_back = [sig(f"c_back{t}", per=16 * KVH, credit=1) for t in range(NT)]
        c_y, c_res = sig("c_y", credit=3), sig("c_res", credit=3)
        d_lmm, d_tok = sig("d_lmm"), sig("d_tok")
        d_w, d_wTev, d_wT, d_acc, d_b2, d_e = (
            sig(x, credit=1) for x in ("d_w", "d_wTev", "d_wT", "d_acc", "d_b2", "d_e"))
        d_ch = sig("d_ch", per=GATE_STEPS, credit=1)
        e_gelu, e_up, e_down, e_acc = sig("e_gelu", credit=4), sig("e_up"), sig("e_down", credit=2), sig("e_acc", credit=2)
        TAIL_LOADS = 9 + KVH


        credited = {
            "pe": (ln_t1, ln_t2, zh_done, q_mm, k_mm, v_mm, qt_mm, kt_mm, s_mm, pt_mm, o_mm, ot_mm, y_mm, h_mm, f_mm,
                   lat_mm, c_pq, c_pk, c_pv, c_s, c_pt, c_o, c_z, c_y, d_wT, d_b2, e_down),
            "act": (ln_out, ln_tok, z_sig, q_sq, k_sq, v_ev, qt_ev, kt_ev, p_exp, pt_ev, ot_ev, g_act,
                    cv_ev, lat_ev, c_oev, c_exp, c_ptev, d_wTev, d_e, e_gelu),
            "dve": (ln_in, ln_stats, gru_a, gru_b, gru_scan, gru_res, q_mul, k_mul, s_max, s_nb, p_sum, p_inv, o_norm,
                    ss_red, nr_chain, sc_done, u_res, h_mul, f_res,
                    c_mq, c_mk, c_max, c_nb, c_rz, c_nrm, c_res, d_ch, d_w, d_acc, e_acc),
            "pool": (sq_half, q_add, k_add, k_norm, c_cq, c_ck, c_cv),
            "sp": tuple(v_dma) + tuple(c_back),
        }
        LA_LOADS, LF_LOADS = 8, 10
        LN_A1, LN_A2, LN_F = 0, NB, 2 * NB
        LN_C = LN_F + DEPTH * NB
        LN_D = LN_C + NB

        def hold(eng):
            eng.sem_inc(held.sem, 1)

        def col(t, a):
            return t[:, a:a + 1]

        def ln_turn_in(pe, i, src, filled):
            pe.wait_ge(filled[0].sem, filled[0].after(filled[1]))
            pe.wait_ge(ln_tok.sem, ln_tok.after(i - 1))
            for t in range(NT):
                mm = pe.transpose(bank[0][:, t * P:(t + 1) * P], src[:, t * P:(t + 1) * P], ident)
            mm.then_inc(ln_t1.sem, 1)

        def ln_keep(act, i):
            act.wait_ge(ln_chain.sem, ln_chain.after(i, 1))
            act.wait_ge(ln_stats.sem, ln_stats.after(i - 1))
            act.activation(lnk[:, :, :].rearrange("p t d -> p (t d)"), bank[0][:, 0:SEQ], ACT.Copy).then_inc(ln_tok.sem, 1)

        def ln_turn_out(pe, i, dst=None):
            dst = bank[1][:, 0:SEQ] if dst is None else dst
            pe.wait_ge(ln_stats.sem, ln_stats.after(i))
            pe.wait_ge(ln_out.sem, ln_out.after(i - 1))
            for t in range(NT):
                mm = pe.transpose(dst[:, t * P:(t + 1) * P], lnx[:, t, :], ident)
            mm.then_inc(ln_t2.sem, 1)

        def rsqrt(dve, y, v, tmp, chain, n, first, lo=0, hi=NR_STEPS):
            for k in range(lo, hi):
                if first + k:
                    dve.wait_ge(chain.sem, chain.after(n, first + k))
                if k == 0:
                    ins = dve.tensor_scalar(tmp.bitcast(I32), v.bitcast(I32), 1, None, ALU.logical_shift_right)
                elif k == 1:
                    ins = dve.tensor_scalar(y.bitcast(I32), tmp.bitcast(I32), -1.0, MAGIC, ALU.mult, ALU.add)
                elif k % 3 == 2:
                    ins = dve.tensor_tensor(tmp, y, y, ALU.mult)
                elif k % 3 == 0:
                    ins = dve.scalar_tensor_tensor(out=tmp, in0=tmp, scalar=-0.5, in1=v, op0=ALU.mult, op1=ALU.mult)
                else:
                    ins = dve.scalar_tensor_tensor(out=y, in0=tmp, scalar=1.5, in1=y, op0=ALU.add, op1=ALU.mult)
                ins.then_inc(chain.sem, 1)

        def ln_normalise(dve, i, lo=0, hi=LN_STEPS):
            tok = bank[0][:, 0:NT * P].rearrange("p (t d) -> p t d", t=NT)
            for k in range(lo, hi):
                if k == 0:
                    dve.wait_ge(ln_t1.sem, ln_t1.after(i))
                    for t in range(NT):
                        ins = dve.bn_stats(lnst[:, t, :], tok[:, t, :])
                    ins.then_inc(ln_chain.sem, 1)
                elif k == 1:
                    dve.wait_ge(ln_chain.sem, ln_chain.after(i, 1))
                    hold(dve)
                    for t in range(NT):
                        ins = dve.bn_aggr(lnmv[:, t, :], lnst[:, t, :])
                    ins.then_inc(ln_chain.sem, 1)
                elif k == 2:
                    dve.wait_ge(ln_chain.sem, ln_chain.after(i, 2))
                    dve.tensor_scalar(lnve[:, :], lnmv[:, :, 1], EPS, None, ALU.add).then_inc(ln_chain.sem, 1)
                elif k < 3 + NR_STEPS:
                    rsqrt(dve, lny[:, :], lnve[:, :], lnt[:, :], ln_chain, i, 3, k - 3, k - 2)
                else:
                    dve.wait_ge(ln_chain.sem, ln_chain.after(i))
                    dve.wait_ge(ln_t2.sem, ln_t2.after(i - 1))
                    dve.wait_ge(ln_tok.sem, ln_tok.after(i))
                    for t in range(NT):
                        ins = dve.tensor_scalar(lnx[:, t, :], lnk[:, t, :], lnmv[:, t, 0:1], lny[:, t:t + 1],
                                                ALU.subtract, ALU.mult)
                    ins.then_inc(ln_stats.sem, 1)

        def seq_cols(b, n=SEQ, off=0):
            return ds(b * SEQ + off, n) if not isinstance(b, int) else slice(b * SEQ + off, b * SEQ + off + n)

        def shifted_copy(dve, dst, b):
            h = D // 2
            dve.tensor_copy(dst[0:h, :], uT[0:h, seq_cols(b)])
            return dve.tensor_copy(dst[h:D, 1:SEQ], uT[h:D, seq_cols(b, SEQ - 1)])

        L_T, L_S, L_P, L_O = 1, 2, 3, 4

        def units(eng, layer):
            for bs, live in steps(eng, NB, 1):
                B = layer * NB + bs
                n0 = B * UPB
                for j in range(UPB):
                    yield bs, B, j, (lambda d, j=j, live=live: live((d - j + UPB - 1) // UPB)), (lambda d, n0=n0, j=j: n0 + j - d)

        def attention_pe(pe, layer):
            for bs, B, j, live, unit in units(pe, layer):
                if live(0):
                    n, h, t = unit(0), j // NT, j % NT
                    if j == 0:
                        pe.wait_ge(xs_in.sem, xs_in.after(layer * (NB + 1) + bs))
                    xt = xs[:, t * P:(t + 1) * P]
                    pe.wait_ge(q_sq.sem, q_sq.after(n - 1))
                    pe.matmul(bank[0][:, :], xt, wqkv[:, h * 512:(h + 1) * 512], start=True, stop=True).then_inc(q_mm.sem, 1)
                    pe.wait_ge(k_mul.sem, k_mul.after(n - 1))
                    pe.matmul(bank[1][:, :], xt, wqkv[:, INNER + h * 512:INNER + (h + 1) * 512],
                              start=True, stop=True).then_inc(k_mm.sem, 1)
                    pe.wait_ge(v_ev.sem, v_ev.after(n - 1))
                    pe.wait_ge(u_res.sem, u_res.after(n - L_O - 1))
                    if j == 0:
                        if isinstance(bs, int) and bs == 0:
                            pe.wait_ge(f_res.sem, f_res.after(B - 1))
                    pe.matmul(bank[2][:, :], xt, wqkv[:, 2 * INNER + h * 512:2 * INNER + (h + 1) * 512],
                              start=True, stop=True).then_inc(v_mm.sem, 1)
                if live(L_P):
                    n = unit(L_P)
                    pe.wait_ge(p_exp.sem, p_exp.after(n))
                    pe.wait_ge(pt_ev.sem, pt_ev.after(n - 1))
                    for p in range(HP):
                        mm = pe.transpose(bank[6][:, p * P:(p + 1) * P],
                                          pr[:, (j - L_P) % 2, 2 * p:2 * p + 2, :].rearrange("q h k -> q (h k)"), ident)
                    mm.then_inc(pt_mm.sem, 1)
                if live(L_O):
                    n = unit(L_O)
                    pe.wait_ge(o_norm.sem, o_norm.after(n))
                    if live(L_S):
                        pe.wait_ge(kt_ev.sem, kt_ev.after(unit(L_S)))
                    else:
                        pe.wait_ge(ot_ev.sem, ot_ev.after(n - 1))
                    for p in range(HP):
                        mm = pe.transpose(bank[4][:, p * P:(p + 1) * P],
                                          ob[:, (j - L_O) % 2, 2 * p:2 * p + 2, :].rearrange("q h k -> q (h k)"), ident)
                    mm.then_inc(ot_mm.sem, 1)
                if live(L_S):
                    n = unit(L_S)
                    h, t = (j - L_S) % UPB // NT, (j - L_S) % NT
                    pe.wait_ge(qt_ev.sem, qt_ev.after(n))
                    pe.wait_ge(kt_ev.sem, kt_ev.after(n))
                    pe.wait_ge(p_exp.sem, p_exp.after(n - 1))
                    pe.matmul(bank[5][:, :], bandsel[:, t, :], bandrhs[:, :], start=True, stop=False, skip_group_check=True)
                    for p in range(HP):
                        for w in range(NWT):
                            k0 = (t * NWT + w) * WIN
                            mm = pe.matmul(bank[5][w * WIN:(w + 1) * WIN, p * P:(p + 1) * P],
                                           qT[:, p, w * WIN:(w + 1) * WIN], kBD[:, h, p, :, k0:k0 + 2 * WIN],
                                           start=False, stop=True, skip_group_check=True)
                    mm.then_inc(s_mm.sem, 1)
                if live(L_T):
                    n, par = unit(L_T), (j - L_T) % 2
                    pe.wait_ge(q_add.sem, q_add.after(n))
                    pe.wait_ge(qt_ev.sem, qt_ev.after(n - 1))
                    for p in range(HP):
                        mm = pe.transpose(bank[3][:, p * P:(p + 1) * P], qr[:, par, p * P:(p + 1) * P], ident)
                    mm.then_inc(qt_mm.sem, 1)
                if live(L_P):
                    n = unit(L_P)
                    jj = (j - L_P) % UPB
                    h, t = jj // NT, jj % NT
                    pe.wait_ge(pt_ev.sem, pt_ev.after(n))
                    pe.wait_ge(v_dma[jj].sem, v_dma[jj].after(B if j >= L_P else B - 1))
                    pe.wait_ge(o_norm.sem, o_norm.after(n - 1))
                    for p in range(HP):
                        for w in range(NWT):
                            mm = pe.matmul(bank[7][w * WIN:(w + 1) * WIN, p * P:(p + 1) * P],
                                           pT[:, p, w * WIN:(w + 1) * WIN], vBD[:, h, t * NWT + w, :, p, :],
                                           start=True, stop=True)
                    mm.then_inc(o_mm.sem, 1)
                if live(L_T):
                    n, par = unit(L_T), (j - L_T) % 2
                    pe.wait_ge(k_norm.sem, k_norm.after(n))
                    pe.wait_ge(ot_ev.sem, ot_ev.after(n - 3))
                    for p in range(HP):
                        mm = pe.transpose(bank[4][:, p * P:(p + 1) * P],
                                          kr[:, par, 2 * p:2 * p + 2, :].rearrange("q h k -> q (h k)"), ident)
                    mm.then_inc(kt_mm.sem, 1)
                if live(L_O):
                    n, jj = unit(L_O), (j - L_O) % UPB
                    h, t = jj // NT, jj % NT
                    pe.wait_ge(ot_ev.sem, ot_ev.after(n))
                    pe.wait_ge(v_ev.sem, v_ev.after(unit(0) if live(0) else n))
                    pe.wait_ge(u_res.sem, u_res.after(n - 1))
                    for c in range(HP):
                        mm = pe.matmul(bank[2][:, 0:P], wo[:, h * HP + c, :], attT[:, h * HP + c, t * P:(t + 1) * P],
                                       start=(c == 0), stop=(c == HP - 1))
                    mm.then_inc(y_mm.sem, 1)

        def attention_act(act, layer):
            for bs, B, j, live, unit in units(act, layer):
                if live(0):
                    n = unit(0)
                    act.wait_ge(k_mm.sem, k_mm.after(n))
                    act.wait_ge(sq_half.sem, sq_half.after(n - 1))
                    act.activation(sq[:, HH:, :], bank[1][:, :].rearrange("p (h d) -> p h d", d=DH), ACT.Square).then_inc(k_sq.sem, 1)
                    act.wait_ge(q_mul.sem, q_mul.after(n))
                    act.activation(sq[:, 0:HH, :], bank[0][:, :].rearrange("p (h d) -> p h d", d=DH), ACT.Square).then_inc(q_sq.sem, 1)
                    act.wait_ge(v_mm.sem, v_mm.after(n))
                    act.wait_ge(v_dma[j].sem, v_dma[j].after(B - 1))
                    act.activation(vS[:, j, :, :, :].rearrange("p e q d -> p q e d"),
                                   bank[2][:, :].rearrange("p (q e d) -> p q e d", e=2, d=DH), ACT.Copy).then_inc(v_ev.sem, 1)
                if live(L_P):
                    n = unit(L_P)
                    act.wait_ge(pt_mm.sem, pt_mm.after(n))
                    act.wait_ge(o_mm.sem, o_mm.after(n - 1))
                    act.activation(pT[:, :, :].rearrange("p a b -> p (a b)"), bank[6][:, :], ACT.Copy).then_inc(pt_ev.sem, 1)
                if live(L_O):
                    n = unit(L_O)
                    jj = (j - L_O) % UPB
                    h, t = jj // NT, jj % NT
                    act.wait_ge(ot_mm.sem, ot_mm.after(n))
                    act.activation(attT[:, h * HP:(h + 1) * HP, t * P:(t + 1) * P],
                                   bank[4][:, :].rearrange("p (a b) -> p a b", a=HP), ACT.Copy).then_inc(ot_ev.sem, 1)
                if live(L_S):
                    n = unit(L_S)
                    par = (j - L_S) % 2
                    act.wait_ge(s_nb.sem, s_nb.after(n))
                    act.wait_ge(pt_mm.sem, pt_mm.after(n - 2))
                    act.wait_ge(p_sum.sem, p_sum.after(n - 2))
                    for hd in range(HH):
                        ins = act.activation(pr[:, par, hd, :], bank[5][:, hd * 64:(hd + 1) * 64], ACT.Exp,
                                             scale=sc8[:, (j - L_S) % UPB, hd:hd + 1], bias=nbias[:, par, hd:hd + 1])
                    ins.then_inc(p_exp.sem, 1)
                if live(L_T):
                    n = unit(L_T)
                    jj = (j - L_T) % UPB
                    h, t = jj // NT, jj % NT
                    act.wait_ge(qt_mm.sem, qt_mm.after(n))
                    act.activation(qT[:, :, :].rearrange("p a b -> p (a b)"), bank[3][:, :], ACT.Copy).then_inc(qt_ev.sem, 1)
                    act.wait_ge(kt_mm.sem, kt_mm.after(n))
                    for e in range(2):
                        ins = act.activation(kBD[64 * e:64 * e + 64, h, :, e, WIN + t * P:WIN + (t + 1) * P],
                                             bank[4][64 * e:64 * e + 64, :].rearrange("p (a b) -> p a b", a=HP), ACT.Copy)
                    ins.then_inc(kt_ev.sem, 1)

        def attention_dve(dve, layer):
            dve.wait_ge(tabs.sem, layer + 1)
            for bs, B, j, live, unit in units(dve, layer):
                if j == 0 and isinstance(bs, int) and bs == 0:
                    dve.wait_ge(f_res.sem, f_res.after(B - 1))
                    dve.wait_ge(v_mm.sem, v_mm.after(unit(0) - 1))
                    shifted_copy(dve, xs, 0).then_inc(xs_in.sem, 1)
                def factors(lag, lo, hi):
                    if live(lag):
                        if lo == 0:
                            n = unit(lag)
                            dve.wait_ge(ss_red.sem, ss_red.after(n, 2))
                            dve.wait_ge(k_norm.sem, k_norm.after(n - 1))
                            dve.wait_ge(sc_done.sem, sc_done.after(n - 1))
                        rsqrt(dve, rn[:, :], ss[:, :], rnt[:, :], nr_chain, unit(lag), 0, lo, hi)

                t = j % NT
                for m, (mm, mul, add) in enumerate(((q_mm, q_mul, q_add), (k_sq, k_mul, k_add))):
                    if live(0):
                        n = unit(0)
                        src = bank[m][:, :].rearrange("p (h d) -> p h d", d=DH)
                        swp = bank[m][:, :].rearrange("p (h s d) -> p h s d", h=HH, s=2)[:, :, ::-1, :]
                        tab = rot[:, t, 2 * m:2 * m + 2, :]
                        dve.wait_ge(mm.sem, mm.after(n))
                        dve.wait_ge(add.sem, add.after(n - 1))
                        dve.tensor_tensor(t1[:, m], src, tab[:, 0, :].unsqueeze(1).broadcast_to([P, HH, DH]), ALU.mult)
                    factors(L_T, 4 + 2 * m, 5 + 2 * m)
                    if live(0):
                        dve.tensor_tensor(t2[:, m].rearrange("p h (s d) -> p h s d", s=2), swp,
                                          tab[:, 1, :].rearrange("p (s d) -> p s d", s=2).unsqueeze(1).broadcast_to([P, HH, 2, DH // 2]),
                                          ALU.mult).then_inc(mul.sem, 1)
                    factors(L_T, 5 + 2 * m, 6 + 2 * m)
                if live(L_P):
                    n, par = unit(L_P), (j - L_P) % 2
                    dve.wait_ge(p_exp.sem, p_exp.after(n))
                    dve.tensor_reduce(psm[:, par, :], pr[:, par], AX.X, ALU.add).then_inc(p_sum.sem, 1)
                factors(L_T, 8, 9)
                if live(L_P):
                    dve.wait_ge(p_sum.sem, p_sum.after(n))
                    dve.wait_ge(o_norm.sem, o_norm.after(n - 2))
                    dve.reciprocal(rinv[:, par, :], psm[:, par, :]).then_inc(p_inv.sem, 1)
                factors(L_T, 9, NR_STEPS)
                if live(L_S):
                    n, par = unit(L_S), (j - L_S) % 2
                    dve.wait_ge(s_mm.sem, s_mm.after(n))
                    dve.tensor_reduce(mx[:, par, :], bank[5][:, :].rearrange("p (h k) -> p h k", h=HH), AX.X, ALU.max).then_inc(s_max.sem, 1)
                if live(L_S):
                    dve.wait_ge(s_max.sem, s_max.after(n))
                    dve.wait_ge(sc_done.sem, sc_done.after(n))
                    dve.wait_ge(p_exp.sem, p_exp.after(n - 2))
                    dve.scalar_tensor_tensor(out=nbias[:, par, :], in0=mx[:, par, :], scalar=-1.0,
                                             in1=sc8[:, (j - L_S) % UPB, :], op0=ALU.mult, op1=ALU.mult).then_inc(s_nb.sem, 1)
                if live(L_T):
                    n, jj = unit(L_T), (j - L_T) % UPB
                    dve.wait_ge(nr_chain.sem, nr_chain.after(n))
                    dve.wait_ge(p_exp.sem, p_exp.after(n - UPB))
                    dve.tensor_scalar(sc8[:, jj, :], rn[:, 0:HH], 8.0, None, ALU.mult).then_inc(sc_done.sem, 1)
                if live(0):
                    n = unit(0)
                    dve.wait_ge(sq_half.sem, sq_half.after(n))
                    dve.wait_ge(nr_chain.sem, nr_chain.after(n - 1))
                    dve.tensor_reduce(ss[:, :], sqh[:, :, :], AX.X, ALU.add).then_inc(ss_red.sem, 1)
                if j == UPB - 1 and live(0):
                    dve.wait_ge(v_mm.sem, v_mm.after(unit(0)))
                    shifted_copy(dve, xs, bs + 1).then_inc(xs_in.sem, 1)
                if live(0):
                    dve.wait_ge(ss_red.sem, ss_red.after(n, 1))
                    dve.tensor_scalar(ss[:, :], ss[:, :], 1e-24, None, ALU.max).then_inc(ss_red.sem, 1)
                if live(L_P):
                    n, par = unit(L_P), (j - L_P) % 2
                    dve.wait_ge(o_mm.sem, o_mm.after(n))
                    dve.wait_ge(p_inv.sem, p_inv.after(n))
                    dve.wait_ge(ot_mm.sem, ot_mm.after(n - 2))
                    dve.tensor_tensor(ob[:, par], bank[7][:, :].rearrange("p (h d) -> p h d", h=HH),
                                      rinv[:, par, :].unsqueeze(2).broadcast_to([P, HH, DH]), ALU.mult).then_inc(o_norm.sem, 1)
                factors(0, 0, 4)
                if live(L_O):
                    n = unit(L_O)
                    u = uT[:, seq_cols(bs if j >= L_O else bs - 1, P, (j - L_O) % NT * P)]
                    dve.wait_ge(y_mm.sem, y_mm.after(n))
                    dve.wait_ge(u_res.sem, u_res.after(n - NT))
                    dve.tensor_tensor(u, u, bank[2][:, 0:P], ALU.add).then_inc(u_res.sem, 1)

        def attention_pool(pool, layer):
            pool.wait_ge(ld_wa.sem, (layer + 1) * 16 * LA_LOADS)
            pool.wait_ge(k_mul.sem, k_mul.after(layer * NB * UPB - 1))
            for t in range(NT):
                ins = pool.tensor_tensor(rot[:, t], rot_base[:, t], qks[:, :, :], ALU.mult)
            ins.then_inc(tabs.sem, 1)
            for bs, B, j, live, unit in units(pool, layer):
                if live(0):
                    n, par = unit(0), j % 2
                    pool.wait_ge(q_mul.sem, q_mul.after(n))
                    pool.wait_ge(qt_mm.sem, qt_mm.after(n - 2))
                    pool.tensor_tensor(qr[:, par, :].rearrange("p (h d) -> p h d", h=HH), t1[:, 0], t2[:, 0], ALU.add).then_inc(q_add.sem, 1)
                    pool.wait_ge(k_sq.sem, k_sq.after(n))
                    pool.wait_ge(q_sq.sem, q_sq.after(n))
                    pool.wait_ge(ss_red.sem, ss_red.after(n - 1, 1))
                    pool.tensor_tensor(sqh[:, :, :], sq[:, :, 0:DH // 2], sq[:, :, DH // 2:], ALU.add).then_inc(sq_half.sem, 1)
                if live(L_T):
                    n, par = unit(L_T), (j - L_T) % 2
                    pool.wait_ge(k_add.sem, k_add.after(n))
                    pool.wait_ge(nr_chain.sem, nr_chain.after(n))
                    pool.wait_ge(kt_mm.sem, kt_mm.after(n - 2))
                    pool.tensor_tensor(kr[:, par], kr0[:, :, :], rn[:, HH:].unsqueeze(2).broadcast_to([P, HH, DH]),
                                       ALU.mult).then_inc(k_norm.sem, 1)
                if live(0):
                    n = unit(0)
                    pool.wait_ge(k_mul.sem, k_mul.after(n))
                    pool.wait_ge(k_norm.sem, k_norm.after(n - 1))
                    pool.tensor_tensor(kr0[:, :, :], t1[:, 1], t2[:, 1], ALU.add).then_inc(k_add.sem, 1)

        def value_moves(h, t, j):
            for e in range(2):
                base = 64 * e
                for w in range(t * NWT, (t + 1) * NWT + 1):
                    lo = w * WIN - WIN
                    a, b = max(lo, t * P), min(lo + 2 * WIN, (t + 1) * P)
                    if w < NW and a < b:
                        yield (vBD[base + a - lo:base + b - lo, h, w, e, :, :], vS[a - t * P:b - t * P, j, e, :, :])

        def attention_sp(sp, layer):
            with sp.Fori(0, NB) as b:
                B = layer * NB + b
                for j in range(UPB):
                    n = B * UPB + j
                    sp.wait_ge(v_ev.sem, v_ev.after(n))
                    hold(sp)
                    sp.wait_ge(o_mm.sem, o_mm.after(n - 3))
                    for dst, src in value_moves(j // NT, j % NT, j):
                        sp.dma_start(dst, src).then_inc(v_dma[j].sem, 16)

        def gated_cols(s, c):
            if isinstance(s, int):
                return hT[0:FSZ[c], s % 2, c, :]
            return hT[0:FSZ[c], ds(s % 2, 1), c, :].rearrange("p m k -> p (m k)")

        def mlp_pe(pe, layer):
            pe.wait_ge(ld_wf.sem, (layer + 1) * 16 * LF_LOADS)
            for s, live in steps(pe, NB, 2):
                B = layer * NB + s
                if live(0):
                    ln_turn_in(pe, LN_F + B, lns, (f_in, layer * (NB + 1) + s))
                if live(1):
                    ln_turn_out(pe, LN_F + B - 1)
                    pe.wait_ge(ln_out.sem, ln_out.after(LN_F + B - 1))
                    for c in range(FC):
                        pe.wait_ge(h_mul.sem, h_mul.after(B - 2, c + 1))
                        for m in range(2):
                            o = m * FF + c * P
                            mm = pe.matmul(bank[3 + c][0:FSZ[c], m * SEQ:(m + 1) * SEQ], w1[:, o:o + FSZ[c]], xnT[:, :],
                                           start=True, stop=True)
                        mm.then_inc(h_mm.sem, 1)
                if live(2):
                    pe.wait_ge(h_mul.sem, h_mul.after(B - 2))
                    pe.wait_ge(f_res.sem, f_res.after(B - 3))
                    if isinstance(s, int) and s == 2:
                        pe.wait_ge(u_res.sem, u_res.after((layer + 1) * NB * UPB - 1))
                    for c in range(FC):
                        mm = pe.matmul(bank[2][:, 0:SEQ], w2[0:FSZ[c], c, :], gated_cols(s - 2, c), start=(c == 0), stop=(c == FC - 1))
                    mm.then_inc(f_mm.sem, 1)

        def mlp_act(act, layer):
            act.wait_ge(ld_wf.sem, (layer + 1) * 16 * LF_LOADS)
            for s, live in steps(act, NB, 1):
                B = layer * NB + s
                if live(1):
                    act.wait_ge(ln_t2.sem, ln_t2.after(LN_F + B - 1))
                    act.activation(xnT[:, :], bank[1][:, 0:SEQ], ACT.Identity, bias=lngb[:, 1:2], scale=lngb[:, 0:1]).then_inc(ln_out.sem, 1)
                if live(0):
                    ln_keep(act, LN_F + B)
                if live(1):
                    for c in range(FC):
                        act.wait_ge(h_mm.sem, h_mm.after(B - 1, c + 1))
                        act.wait_ge(h_mul.sem, h_mul.after(B - 2, c + 1))
                        act.activation(gs[0:FSZ[c], c, :], bank[3 + c][0:FSZ[c], SEQ:2 * SEQ], ACT.Gelu,
                                       bias=b1c[0:FSZ[c], 1, c:c + 1]).then_inc(g_act.sem, 1)

        def mlp_dve(dve, layer):
            dve.wait_ge(ld_wf.sem, (layer + 1) * 16 * LF_LOADS)
            dve.wait_ge(u_res.sem, u_res.after((layer + 1) * NB * UPB - 1))
            dve.wait_ge(ln_t1.sem, ln_t1.after(LN_F + layer * NB - 1))
            shifted_copy(dve, lns, 0).then_inc(f_in.sem, 1)
            for s, live in steps(dve, NB, 2):
                B = layer * NB + s
                i = LN_F + B

                def gated(c):
                    dve.wait_ge(g_act.sem, g_act.after(B - 1, c + 1))
                    dve.wait_ge(f_mm.sem, f_mm.after(B - 3))
                    dve.scalar_tensor_tensor(out=gated_cols(s - 1, c), in0=bank[3 + c][0:FSZ[c], 0:SEQ],
                                             scalar=b1c[0:FSZ[c], 0, c:c + 1], in1=gs[0:FSZ[c], c, :],
                                             op0=ALU.add, op1=ALU.mult).then_inc(h_mul.sem, 1)

                if live(0):
                    ln_normalise(dve, i, 0, 1)
                    shifted_copy(dve, lns, s + 1).then_inc(f_in.sem, 1)
                    ln_normalise(dve, i, 1, 10)
                if live(1):
                    gated(0)
                if live(0):
                    ln_normalise(dve, i, 10, 12)
                if live(1):
                    gated(1)
                if live(0):
                    ln_normalise(dve, i, 12, 14)
                if live(1):
                    gated(2)
                if live(0):
                    ln_normalise(dve, i, 14, LN_STEPS)
                if live(2):
                    b = s - 2
                    dve.wait_ge(f_mm.sem, f_mm.after(B - 2))
                    dve.scalar_tensor_tensor(out=uT[:, seq_cols(b)], in0=bank[2][:, 0:SEQ], scalar=b2c[:, 0:1],
                                             in1=uT[:, seq_cols(b)], op0=ALU.add, op1=ALU.add).then_inc(f_res.sem, 1)

        def load_layer(sp, layer):
            def row(name):
                return A[name][ds(layer, 1)]

            half = DH // 2
            sp.wait_ge(y_mm.sem, y_mm.after(layer * NB * UPB - 1))
            hold(sp)
            for m, name in ((0, "L0_ffn_q_scale"), (2, "L0_ffn_k_scale")):
                v = row(name)
                sp.dma_start(qks[:, m, :], v.broadcast_to([P, DH])).then_inc(ld_wa.sem, 16)
                sp.dma_start(qks[:, m + 1, 0:half], v[:, half:DH].broadcast_to([P, half])).then_inc(ld_wa.sem, 16)
                sp.dma_start(qks[:, m + 1, half:DH], v[:, 0:half].broadcast_to([P, half])).then_inc(ld_wa.sem, 16)
            sp.dma_start(wqkv[:, :], row("L0_ffn_Wqkv").rearrange("l p n -> (l p) n")).then_inc(ld_wa.sem, 16)
            sp.dma_start(wo[:, :, :], row("L0_ffn_Wo").rearrange("l (c p) n -> p (l c) n", p=P)).then_inc(ld_wa.sem, 16)
            sp.wait_ge(f_res.sem, f_res.after(layer * NB - 1))
            hold(sp)
            full = (FC - 1) * P
            sp.dma_start(w1[:, :], row("L0_ffn_W1").rearrange("l p n -> (l p) n")).then_inc(ld_wf.sem, 16)
            v = row("L0_ffn_W2")
            sp.dma_start(w2[:, 0:FC - 1, :], v[:, 0:full, :].rearrange("l (c p) n -> p (l c) n", p=P)).then_inc(ld_wf.sem, 16)
            sp.dma_start(w2[0:FF - full, FC - 1, :], v[:, full:FF, :].rearrange("l p n -> (l p) n")).then_inc(ld_wf.sem, 16)
            v = row("L0_ffn_b1")
            for m in range(2):
                o = m * FF
                sp.dma_start(b1c[:, m, 0:FC - 1], v[:, o:o + full].rearrange("l (c p) -> p (l c)", p=P), allow_slow_non_contiguous=True).then_inc(ld_wf.sem, 16)
                sp.dma_start(b1c[0:FF - full, m, FC - 1:FC], v[:, o + full:o + FF].rearrange("l p -> p l"), allow_slow_non_contiguous=True).then_inc(ld_wf.sem, 16)
            for m, name in enumerate(("L0_ffn_ln_g", "L0_ffn_ln_b")):
                sp.dma_start(lngb[:, m:m + 1], row(name).rearrange("l p -> p l"), allow_slow_non_contiguous=True).then_inc(ld_wf.sem, 16)
            sp.dma_start(b2c[:, 0:1], row("L0_ffn_b2").rearrange("l p -> p l"), allow_slow_non_contiguous=True).then_inc(ld_wf.sem, 16)

        def tail_loads(sp):
            def load(dst, src, **how):
                sp.dma_start(dst, src, **how).then_inc(ld_tail.sem, 16)

            load(wqa[:, :], A["L1_attn_Wqa"])
            load(wqb[:, 0, :], A["L1_attn_Wqb"])
            load(wkva[:, :], A["L1_attn_Wkva"])
            load(wkvn[:, :, :, :], A["L1_attn_Wkvb"].rearrange("k (r d m) -> k r d m", r=KVH, d=QD))
            sp.wait_ge(zeroed_dve.sem, 1)
            for r in range(KVH):
                load(woutp[32 * r:32 * r + QD, :, :],
                     A["L1_attn_Wout"][r * GRP * QD:(r + 1) * GRP * QD, :].rearrange("(j d) n -> d j n", j=GRP))
            load(boutc[:, :], A["L1_attn_bout"].rearrange("(p o) -> p o", o=1), allow_slow_non_contiguous=True)
            load(b1e[:, :], A["L1_ffn_b1"].rearrange("e (c p) -> p (e c)", p=P), allow_slow_non_contiguous=True)
            load(b2e[:, :], A["L1_ffn_b2"])
            load(wg[:, :], A["L1_ffn_Wg"])
            load(bgb[:, :], A["L1_ffn_bg"].rearrange("(o e) -> o e", o=1).broadcast_to([P, NE]))

        def swap_weights(dve):
            dve.wait_ge(ld_tail.sem, 16 * TAIL_LOADS)
            dve.tensor_copy(wvb[:, :].rearrange("k (r d) -> k r d", r=KVH), wkvn[:, :, :, 1])
            dve.tensor_copy(wkb[:, 0, :].rearrange("k (r j d) -> k r j d", r=KVH, j=GRP),
                            wkvn[:, :, :, 0].unsqueeze(2).broadcast_to([KVL, KVH, GRP, QD])).then_inc(cswap.sem, 1)
            dve.wait_ge(cswap.sem, 1)
            for w in (wqb, wkb):
                ins = dve.tensor_copy(w[:, 1, :].rearrange("k (c s) -> k c s", s=2),
                                      w[:, 0, :].rearrange("k (c s) -> k c s", s=2)[:, :, ::-1])
            ins.then_inc(cswap.sem, 1)

        def gru_pe(pe):
            pe.wait_ge(ld_const.sem, 16)
            pe.wait_ge(ld_x.sem, 16)
            for g in range(NB * NT // 4):
                if g >= 4:
                    pe.wait_ge(x_kept.sem, g - 3)
                for t in range(4):
                    mm = pe.transpose(bank[2 + g % 4][:, t * P:(t + 1) * P], xtok[:, 4 * g + t, :], ident)
                mm.then_inc(x_turned.sem, 1)
            pe.wait_ge(ld_gru.sem, 16 * 4)
            pe.wait_ge(x_kept.sem, NB * NT // 4)
            for s, live in steps(pe, NB, 1):
                if live(0):
                    ln_turn_in(pe, LN_A1 + s, lnin, (ln_in, LN_A1 + s))
                if live(1):
                    ln_turn_out(pe, LN_A1 + s - 1)
                    pe.wait_ge(ln_out.sem, ln_out.after(LN_A1 + s - 1))
                    pe.wait_ge(gru_b.sem, gru_b.after(s - 2))
                    for m in range(2):
                        mm = pe.matmul(bank[2][:, m * SEQ:(m + 1) * SEQ], wzh[:, m, :], xnT[:, :], start=True, stop=True)
                    mm.then_inc(zh_done.sem, 1)
            for s, live in steps(pe, NB, 1):
                if live(0):
                    ln_turn_in(pe, LN_A2 + s, lnin, (ln_in, LN_A2 + s))
                if live(1):
                    ln_turn_out(pe, LN_A2 + s - 1)

        def gru_act(act):
            act.wait_ge(ld_gru.sem, 16 * 4)
            for s, live in steps(act, NB, 1):
                if live(1):
                    act.wait_ge(ln_t2.sem, ln_t2.after(LN_A1 + s - 1))
                    act.activation(xnT[:, :], bank[1][:, 0:SEQ], ACT.Copy).then_inc(ln_out.sem, 1)
                if live(0):
                    ln_keep(act, LN_A1 + s)
                if live(1):
                    act.wait_ge(zh_done.sem, zh_done.after(s - 1))
                    act.wait_ge(gru_b.sem, gru_b.after(s - 2))
                    act.activation(zs[:, :], bank[2][:, 0:SEQ], ACT.Sigmoid, bias=bzh[:, 0:1]).then_inc(z_sig.sem, 1)
            for s, live in steps(act, NB, 1):
                if live(1):
                    act.wait_ge(ln_t2.sem, ln_t2.after(LN_A2 + s - 1))
                    act.activation(uT[:, seq_cols(s - 1)], bank[1][:, 0:SEQ], ACT.Copy).then_inc(ln_out.sem, 1)
                if live(0):
                    ln_keep(act, LN_A2 + s)

        def gru_dve(dve):
            for g in range(NB * NT // 4):
                dve.wait_ge(x_turned.sem, g + 1)
                dve.tensor_copy(xT[:, g * 512:(g + 1) * 512], bank[2 + g % 4][:, :]).then_inc(x_kept.sem, 1)
            dve.wait_ge(x_kept.sem, NB * NT // 4)
            dve.wait_ge(ld_gru.sem, 16 * 4)
            for s, live in steps(dve, NB, 1):
                i = LN_A1 + s
                if live(0):
                    dve.wait_ge(ln_t1.sem, ln_t1.after(i - 1))
                    dve.tensor_copy(lnin[:, :], xT[:, seq_cols(s)]).then_inc(ln_in.sem, 1)
                    ln_normalise(dve, i, 0, 10)
                if live(1):
                    b = s - 1
                    dve.wait_ge(z_sig.sem, z_sig.after(b))
                    dve.wait_ge(gru_scan.sem, gru_scan.after(b - 1))
                    dve.tensor_scalar(za[:, :], zs[:, :], -1.0, 1.0, ALU.mult, ALU.add).then_inc(gru_a.sem, 1)
                    dve.scalar_tensor_tensor(out=zb[:, :], in0=bank[2][:, SEQ:2 * SEQ], scalar=bzh[:, 1:2], in1=zs[:, :],
                                             op0=ALU.add, op1=ALU.mult).then_inc(gru_b.sem, 1)
                if live(0):
                    ln_normalise(dve, i, 10, 11)
                if live(1):
                    dve.wait_ge(gru_a.sem, gru_a.after(b))
                    dve.wait_ge(gru_b.sem, gru_b.after(b))
                    dve.wait_ge(gru_res.sem, gru_res.after(b - 1))
                    dve.tensor_tensor_scan(hs[:, :], za[:, :], zb[:, :], 0.0, ALU.mult, ALU.add).then_inc(gru_scan.sem, 1)
                if live(0):
                    ln_normalise(dve, i, 11, 13)
                if live(1):
                    dve.wait_ge(gru_scan.sem, gru_scan.after(b))
                    dve.tensor_tensor(xT[:, seq_cols(b)], xT[:, seq_cols(b)], hs[:, :], ALU.add).then_inc(gru_res.sem, 1)
                if live(0):
                    ln_normalise(dve, i, 13, LN_STEPS)
            dve.wait_ge(gru_res.sem, gru_res.after(NB - 1))
            for s, live in steps(dve, NB, 1):
                if live(0):
                    i = LN_A2 + s
                    dve.wait_ge(ln_t1.sem, ln_t1.after(i - 1))
                    dve.tensor_copy(lnin[:, :], xT[:, seq_cols(s)]).then_inc(ln_in.sem, 1)
                    ln_normalise(dve, i)
            dve.wait_ge(ln_out.sem, ln_out.after(LN_A2 + NB - 1))

        GROUPS = ([(0, r, 0, GRP, 1) for r in range(KVH)] + [(1, r, j, 2, 2) for j in (0, 2) for r in range(KVH)])
        NG = len(GROUPS)
        G_T = 2
        O_SLOT = KVH + 2
        obank = (bank[4], bank[1])

        def lagged(g, lag, live):
            k = g - lag
            return (live(1), 1, k) if k >= 0 else (live(2), 2, k + NG)

        def lat_pe(pe):
            pe.wait_ge(ld_tail.sem, 16 * TAIL_LOADS)
            pe.wait_ge(cast_done.sem, 4)
            pe.wait_ge(cswap.sem, 2)
            pe.wait_ge(f_res.sem, f_res.after(DEPTH * NB - 1))
            low, high = bank[0][:, 0:SEQ], bank[0][:, SEQ:2 * SEQ]
            for s, live in steps(pe, NB, 2):
                for g in range(NG):
                    if live(1):
                        b, G = s - 1, NG * (s - 1) + g
                        t, r, j0, nh, nk = GROUPS[g]
                        if g == 0:
                            pe.wait_ge(c_ckm.sem, c_ckm.after(b, 2))
                        if g == KVH:
                            pe.wait_ge(c_ckm.sem, c_ckm.after(b))
                            pe.wait_ge(c_cq.sem, c_cq.after(b))
                        pe.wait_ge(c_exp.sem, c_exp.after(G - 3))
                        sc = bank[5 + g % 3]
                        keys = ckm[32 * r:32 * r + 32, j0:j0 + nh, 0:nk * P]
                        pe.matmul(sc[:, :], cq[32 * r:32 * r + 32, t * P:(t + 1) * P], keys, start=True, stop=False,
                                  skip_group_check=True)
                        tri = causal[:, t, :].rearrange("p (h b k) -> p h b k", h=nh, b=nk)[:, :, nk - 1, :]
                        diag = sc[:, :].rearrange("p (h b k) -> p h b k", h=nh, b=nk)[:, :, nk - 1, :]
                        pe.matmul(diag, identb[:, :], tri, start=False, stop=True, skip_group_check=True).then_inc(c_s.sem, 1)
                    ok, lag, k = lagged(g, G_T, live)
                    if ok:
                        G = NG * (s - lag) + k
                        pe.wait_ge(c_exp.sem, c_exp.after(G))
                        pe.wait_ge(c_ptev.sem, c_ptev.after(G - 1))
                        for q in range(4):
                            mm = pe.transpose(bank[3][:, q * P:(q + 1) * P], cp[:, k % 3, q * P:(q + 1) * P], ident)
                        mm.then_inc(c_pt.sem, 1)
                    for n in range(3):
                        first = O_SLOT + KVH * n
                        c, ok = (s - 1, live(1)) if first < NG else (s - 2, live(2))
                        if g == first % NG and ok:
                            if n == 0:
                                pe.wait_ge(c_cv.sem, c_cv.after(c))
                            if n < 2:
                                pe.wait_ge(c_oev.sem, c_oev.after(2 * (c - 1) + n))
                            pe.wait_ge(c_ptev.sem, c_ptev.after(NG * c + KVH * n + KVH - 1))
                            set_ = GROUPS[KVH * n:KVH * n + KVH]
                            for kb in range(set_[0][4]):
                                for i, (t, r, j0, nh, nk) in enumerate(set_):
                                    probs = cpT[(KVH * n + i) % NTB].rearrange("p (h b k) -> p h b k", h=nh, b=nk)[:, :, kb, :]
                                    mm = pe.matmul(obank[t][32 * r:32 * r + 32, j0 * P:(j0 + nh) * P], cvp[:, kb, r, :], probs,
                                                   start=(kb == 0), stop=(kb == nk - 1))
                            mm.then_inc(c_o.sem, 1)
                    for t, slot in ((0, 0), (1, 8)):
                        c = s - 2
                        if g == slot and live(2):
                            pe.wait_ge(c_back[t].sem, c_back[t].after(c))
                            if t == 0:
                                pe.wait_ge(c_res.sem, c_res.after(c - 1))
                            else:
                                pe.wait_ge(c_nrm.sem, c_nrm.after(2 * c))
                                if live(1):
                                    pe.wait_ge(cv_ev.sem, cv_ev.after(s - 1))
                            pe.matmul(bank[2][:, :], zsel, cos_[:, t, :], start=True, stop=True).then_inc(c_z.sem, 1)
                    if g == 10 and live(2):
                        c = s - 2
                        pe.wait_ge(c_nrm.sem, c_nrm.after(2 * c + 1))
                        for j in range(GRP):
                            mm = pe.matmul(bank[2][:, 0:SEQ], woutp[:, j, :], con[:, :, j * P:(j + 1) * P],
                                           start=(j == 0), stop=(j == GRP - 1))
                        mm.then_inc(c_y.sem, 1)
                    if g == 3 and live(1):
                        b = s - 1
                        if live(2):
                            pe.wait_ge(c_nrm.sem, c_nrm.after(2 * (s - 2)))
                        for t in range(NT):
                            mm = pe.matmul(bank[2][:, t * 32:(t + 1) * 32], ckva[:, t * P:(t + 1) * P], wvb[:, :], start=True, stop=True)
                        mm.then_inc(c_pv.sem, 1)
                    if live(0):
                        if g == 0:
                            pe.wait_ge(c_mq.sem, c_mq.after(s - 1))
                            ln_turn_in(pe, LN_C + s, lnin, (ln_in, LN_C + s - DEPTH * NB))
                        if g == 6:
                            ln_turn_out(pe, LN_C + s, high)
                        if g == 7:
                            pe.wait_ge(ln_out.sem, ln_out.after(LN_C + s))
                            pe.matmul(low[0:QL, :], wqa[:, :], xnT[:, :], start=True, stop=True)
                            pe.matmul(high[0:KVL, :], wkva[:, :], xnT[:, :], start=True, stop=True).then_inc(lat_mm.sem, 1)
                        if g == 8:
                            pe.wait_ge(lat_ev.sem, lat_ev.after(s))
                            for m in range(2):
                                mm = pe.matmul(bank[0][:, m * SEQ:(m + 1) * SEQ], wkb[:, m, :], ckva[:, :], start=True, stop=True)
                            mm.then_inc(c_pk.sem, 1)
                        if g == 9:
                            pe.wait_ge(c_mk.sem, c_mk.after(s))
                            for m in range(2):
                                mm = pe.matmul(bank[0][:, m * SEQ:(m + 1) * SEQ], wqb[:, m, :], cqa[:, :], start=True, stop=True)
                            mm.then_inc(c_pq.sem, 1)

        def lat_act(act):
            act.preload_act_table(ACT.Exp)
            for s, live in steps(act, NB, 2):
                for g in range(NG):
                    ok, lag, k = lagged(g, G_T, live)
                    if ok:
                        G = NG * (s - lag) + k
                        act.wait_ge(c_pt.sem, c_pt.after(G))
                        used = (k - NTB) // KVH
                        act.wait_ge(c_o.sem, c_o.after(3 * (s - lag) + used))
                        act.activation(cpT[k % NTB], bank[3][:, :], ACT.Copy).then_inc(c_ptev.sem, 1)
                    if live(1):
                        G = NG * (s - 1) + g
                        t, r, j0, nh, nk = GROUPS[g]
                        act.wait_ge(c_nb.sem, c_nb.after(G))
                        act.wait_ge(c_pt.sem, c_pt.after(G - 3))
                        n = nk * P
                        for hh in range(nh):
                            ins = act.activation(cp[:, g % 3, hh * n:(hh + 1) * n], bank[5 + g % 3][:, hh * n:(hh + 1) * n],
                                                 ACT.Exp, scale=QD ** -0.5, bias=cnb[:, g % 3, hh:hh + 1])
                        ins.then_inc(c_exp.sem, 1)
                    for t, slot in ((0, 7), (1, 3)):
                        c, ok = (s - 1, live(1)) if t == 0 else (s - 2, live(2))
                        if g == slot and ok:
                            act.wait_ge(c_o.sem, c_o.after(3 * c + 2 * t))
                            act.wait_ge(c_nrm.sem, c_nrm.after(2 * (c - 1) + t))
                            act.activation(cos_[:, t, :], obank[t][:, :], ACT.Copy).then_inc(c_oev.sem, 1)
                    if live(0):
                        if g == 1:
                            ln_keep(act, LN_C + s)
                        if g == 6:
                            act.wait_ge(ln_t2.sem, ln_t2.after(LN_C + s))
                            act.wait_ge(lat_mm.sem, lat_mm.after(s - 1))
                            act.activation(xnT[:, :], bank[0][:, SEQ:2 * SEQ], ACT.Copy).then_inc(ln_out.sem, 1)
                        if g == 7:
                            act.wait_ge(lat_mm.sem, lat_mm.after(s))
                            act.wait_ge(c_pq.sem, c_pq.after(s - 1))
                            act.wait_ge(c_pv.sem, c_pv.after(s - 1))
                            act.activation(cqa[:, :], bank[0][0:QL, 0:SEQ], ACT.Copy)
                            act.activation(ckva[:, :], bank[0][0:KVL, SEQ:2 * SEQ], ACT.Copy).then_inc(lat_ev.sem, 1)
                    if live(1) and g == 3:
                        b = s - 1
                        act.wait_ge(c_pv.sem, c_pv.after(b))
                        act.wait_ge(c_cv.sem, c_cv.after(b - 1))
                        act.activation(cvn[:, :, :, :].rearrange("p t r d -> p (t r d)"), bank[2][:, 0:NT * KVH * QD],
                                       ACT.Copy).then_inc(cv_ev.sem, 1)

        def lat_dve(dve):
            dve.wait_ge(f_res.sem, f_res.after(DEPTH * NB - 1))
            dve.tensor_tensor(xT[:, :], xT[:, :], uT[:, 0:NB * SEQ], ALU.add).then_inc(add_u.sem, 1)
            dve.wait_ge(add_u.sem, 1)
            dve.wait_ge(ld_tail.sem, 16 * TAIL_LOADS)
            for s, live in steps(dve, NB, 2):
                for g in range(NG):
                    if live(0) and g == 0:
                        dve.wait_ge(ln_t1.sem, ln_t1.after(LN_C + s - 1))
                        dve.tensor_copy(lnin[:, :], xT[:, seq_cols(s)]).then_inc(ln_in.sem, 1)
                    i = LN_C + s
                    norm = live(0) and 1 <= g <= 5
                    if live(1):
                        G = NG * (s - 1) + g
                        t, r, j0, nh, nk = GROUPS[g]
                        dve.wait_ge(c_s.sem, c_s.after(G))
                        dve.wait_ge(c_nb.sem, c_nb.after(G - 1))
                        dve.tensor_reduce(cmx[:, 0:nh], bank[5 + g % 3][:, :].rearrange("p (h k) -> p h k", h=nh), AX.X,
                                          ALU.max).then_inc(c_max.sem, 1)
                    if norm:
                        ln_normalise(dve, i, 3 * g - 3, 3 * g - 2)
                    if live(1):
                        dve.wait_ge(c_max.sem, c_max.after(G))
                        dve.wait_ge(c_exp.sem, c_exp.after(G - 3))
                        dve.tensor_scalar(cnb[:, g % 3, 0:nh], cmx[:, 0:nh], -(QD ** -0.5), None, ALU.mult).then_inc(c_nb.sem, 1)
                    if norm:
                        ln_normalise(dve, i, 3 * g - 2, 3 * g)
                    for t, slot in ((0, 9), (1, 5)):
                        c, ok = (s - 1, live(1)) if t == 0 else (s - 2, live(2))
                        if g == slot and ok:
                            dve.wait_ge(c_out[t].sem, c_out[t].after(c))
                            dve.wait_ge(c_back[t].sem, c_back[t].after(c - 1))
                            dve.reciprocal(crs[:, t, 1, :], crs[:, t, 0, :]).then_inc(c_rz.sem, 1)
                    for t, slot in ((0, 1), (1, 9)):
                        c = s - 2
                        if g == slot and live(2):
                            dve.wait_ge(c_z.sem, c_z.after(2 * c + t))
                            dve.wait_ge(c_y.sem, c_y.after(c - 1))
                            dve.tensor_tensor(con[:, t, :], cos_[:, t, :], bank[2][:, :], ALU.mult).then_inc(c_nrm.sem, 1)
                    if g == 11 and live(2):
                        c = s - 2
                        dve.wait_ge(c_y.sem, c_y.after(c))
                        dve.scalar_tensor_tensor(out=xT[:, seq_cols(c)], in0=bank[2][:, 0:SEQ], scalar=boutc[:, 0:1],
                                                 in1=xT[:, seq_cols(c)], op0=ALU.add, op1=ALU.add).then_inc(c_res.sem, 1)
                    if live(0):
                        if g == 8:
                            dve.wait_ge(c_pk.sem, c_pk.after(s))
                            dve.wait_ge(c_ck.sem, c_ck.after(s - 1))
                            dve.tensor_tensor(ct[:, 1, :], bank[0][:, :], rope, ALU.mult).then_inc(c_mk.sem, 1)
                        if g == 9:
                            dve.wait_ge(c_pq.sem, c_pq.after(s))
                            dve.wait_ge(c_cq.sem, c_cq.after(s - 1))
                            dve.tensor_tensor(ct[:, 0, :], bank[0][:, :], rope, ALU.mult).then_inc(c_mq.sem, 1)

        def lat_pool(pool):
            pool.wait_ge(add_u.sem, 1)
            def prepare(s):
                def mask_keys(j, k0, k1):
                    pool.tensor_tensor(ckm[:, j:j + 2, k0:k1], ck[:, k0:k1].unsqueeze(1).broadcast_to([P, 2, k1 - k0]),
                                       cst("rowmask")[:, j:j + 2].unsqueeze(2).broadcast_to([P, 2, k1 - k0]),
                                       ALU.mult).then_inc(c_ckm.sem, 1)

                pool.wait_ge(c_mk.sem, c_mk.after(s))
                pool.tensor_tensor(ck[:, :], ct[:, 1, 0:SEQ], ct[:, 1, SEQ:], ALU.add).then_inc(c_ck.sem, 1)
                pool.wait_ge(c_ck.sem, c_ck.after(s))
                pool.wait_ge(c_s.sem, c_s.after(NG * s - KVH - 1))
                pool.wait_ge(c_mq.sem, c_mq.after(s))
                pool.tensor_tensor(cq[:, 0:P], ct[:, 0, 0:P], ct[:, 0, SEQ:SEQ + P], ALU.add)
                mask_keys(0, 0, SEQ)
                pool.wait_ge(c_s.sem, c_s.after(NG * s - 1))
                mask_keys(2, 0, P)
                mask_keys(2, P, SEQ)
                pool.tensor_tensor(cq[:, P:SEQ], ct[:, 0, P:SEQ], ct[:, 0, SEQ + P:], ALU.add).then_inc(c_cq.sem, 1)

            def values(s):
                pool.wait_ge(cv_ev.sem, cv_ev.after(s))
                hold(pool)
                pool.wait_ge(c_o.sem, c_o.after(3 * s - 1))
                hold(pool)
                pool.tensor_copy(cvp[:, :, :, 0:QD], cvn[:, :, :, :]).then_inc(c_cv.sem, 1)

            prepare(0)
            with pool.Fori(1, NB) as s:
                values(s - 1)
                prepare(s)
            values(NB - 1)

        def lat_sp(sp):
            def rows(t, r):
                return cos_[32 * r + QD:32 * r + QD + 1, t, :]

            def spread(t, r, m):
                return crs[32 * r:32 * r + 32, t, m, :]

            with sp.Fori(0, NB) as c:
                for t in range(NT):
                    sp.wait_ge(c_oev.sem, c_oev.after(2 * c + t))
                    hold(sp)
                    sp.wait_ge(c_rz.sem, c_rz.after(2 * (c - 1) + t))
                    hold(sp)
                    for r in range(KVH):
                        sp.dma_start(spread(t, r, 0), rows(t, r)).then_inc(c_out[t].sem, 16)
                    sp.wait_ge(c_rz.sem, c_rz.after(2 * c + t))
                    hold(sp)
                    for r in range(KVH):
                        sp.dma_start(rows(t, r), spread(t, r, 1)).then_inc(c_back[t].sem, 16)

        def gate_pe(pe):
            pe.wait_ge(c_res.sem, c_res.after(NB - 1))
            for s, live in steps(pe, NB, 2):
                if live(0):
                    ln_turn_in(pe, LN_D + s, lnin, (ln_in, LN_D + s - DEPTH * NB))
                if live(1):
                    b = s - 1
                    ln_turn_out(pe, LN_D + b)
                    pe.wait_ge(ln_out.sem, ln_out.after(LN_D + b))
                    pe.wait_ge(d_ch.sem, d_ch.after(b - 1, 1))
                    for t in range(NT):
                        mm = pe.matmul(bank[2][:, t * NE:(t + 1) * NE], xnT[:, t * P:(t + 1) * P], wg[:, :], start=True, stop=True)
                    mm.then_inc(d_lmm.sem, 1)
                if live(2):
                    b = s - 2
                    pe.wait_ge(d_w.sem, d_w.after(b))
                    pe.wait_ge(d_wTev.sem, d_wTev.after(b - 1))
                    for t in range(NT):
                        mm = pe.transpose(bank[3][0:NE, t * P:(t + 1) * P], dw1[:, t, :], ident)
                    mm.then_inc(d_wT.sem, 1)
                    pe.wait_ge(d_wTev.sem, d_wTev.after(b))
                    pe.wait_ge(d_acc.sem, d_acc.after(b - 1))
                    for t in range(NT):
                        mm = pe.matmul(bank[4][:, t * P:(t + 1) * P], dwT[:, t * P:(t + 1) * P], b2e[:, :], start=True, stop=True)
                    mm.then_inc(d_b2.sem, 1)

        def gate_act(act):
            for s, live in steps(act, NB, 2):
                if live(1):
                    i = LN_D + s - 1
                    act.wait_ge(ln_t2.sem, ln_t2.after(i))
                    act.activation(xnT[:, :], bank[1][:, 0:SEQ], ACT.Copy)
                    act.activation(xnA[:, seq_cols(s - 1)], bank[1][:, 0:SEQ], ACT.Copy).then_inc(ln_out.sem, 1)
                if live(0):
                    ln_keep(act, LN_D + s)
                if live(2):
                    b = s - 2
                    act.wait_ge(d_ch.sem, d_ch.after(b, 2 + NT))
                    act.wait_ge(d_w.sem, d_w.after(b - 1))
                    act.activation(dexp[:, :], ddiff[:, :], ACT.Exp).then_inc(d_e.sem, 1)
                    act.wait_ge(d_wT.sem, d_wT.after(b))
                    act.wait_ge(d_b2.sem, d_b2.after(b - 1))
                    act.activation(dwT[:, :], bank[3][0:NE, 0:SEQ], ACT.Copy).then_inc(d_wTev.sem, 1)

        def gate_dve(dve):
            dve.wait_ge(c_res.sem, c_res.after(NB - 1))
            for s, live in steps(dve, NB, 3):
                b = s - 2

                def gate(k):
                    if k:
                        dve.wait_ge(d_ch.sem, d_ch.after(b, k))
                        if 1 <= k < 1 + NT or 2 + NT <= k < 2 + 2 * NT:
                            hold(dve)
                    if k == 0:
                        dve.wait_ge(d_lmm.sem, d_lmm.after(b))
                        dve.wait_ge(d_w.sem, d_w.after(b - 1))
                        ins = dve.tensor_tensor(dlg[:, :, :], bank[2][:, 0:NT * NE].rearrange("p (t e) -> p t e", t=NT),
                                                bgb[:, :].unsqueeze(1).broadcast_to([P, NT, NE]), ALU.add)
                    elif k < 1 + NT:
                        ins = dve.max(dmx[:, k - 1, :], dlg[:, k - 1, :])
                    elif k == 1 + NT:
                        dve.wait_ge(d_e.sem, d_e.after(b - 1))
                        ins = dve.tensor_tensor(ddiff[:, :], dmx[:, :, 1], dmx[:, :, 0], ALU.subtract)
                    elif k < 2 + 2 * NT:
                        t = k - 2 - NT
                        ins = dve.max_index(dix[:, t, :], dmx[:, t, :], dlg[:, t, :])
                    elif k == 2 + 2 * NT:
                        ins = dve.tensor_copy(dixf[:, :, :], dix[:, :, 0:2])
                    elif k == 3 + 2 * NT:
                        dve.wait_ge(d_e.sem, d_e.after(b))
                        ins = dve.tensor_scalar(dden[:, :], dexp[:, :], 1.0, None, ALU.add)
                    elif k == 4 + 2 * NT:
                        ins = dve.reciprocal(dp[:, 0, :], dden[:, :])
                    elif k == 5 + 2 * NT:
                        ins = dve.tensor_tensor(dp[:, 1, :], dexp[:, :], dp[:, 0, :], ALU.mult)
                    elif k == 6 + 2 * NT:
                        dve.wait_ge(d_wT.sem, d_wT.after(b - 1))
                        for t in range(NT):
                            dve.tensor_scalar(dw1[:, t, :], cst("iota"), dixf[:, t, 0:1], dp[:, 0, t:t + 1], ALU.is_equal, ALU.mult)
                            ins = dve.tensor_scalar(dw2[:, t, :], cst("iota"), dixf[:, t, 1:2], dp[:, 1, t:t + 1], ALU.is_equal, ALU.mult)
                    elif k == 7 + 2 * NT:
                        ins = dve.tensor_tensor(dw1[:, :, :], dw1[:, :, :], dw2[:, :, :], ALU.add)
                    else:
                        dve.tensor_copy(wA[:, ds(b * NT, NT) if not isinstance(b, int) else slice(b * NT, b * NT + NT), :],
                                        dw1[:, :, :]).then_inc(d_w.sem, 1)
                        return
                    ins.then_inc(d_ch.sem, 1)

                if live(0):
                    i = LN_D + s
                    dve.wait_ge(ln_t1.sem, ln_t1.after(i - 1))
                    dve.tensor_copy(lnin[:, :], xT[:, seq_cols(s)]).then_inc(ln_in.sem, 1)
                if live(3):
                    c = s - 3
                    dve.wait_ge(d_b2.sem, d_b2.after(c))
                    dve.wait_ge(d_tok.sem, d_tok.after(c))
                    dve.tensor_tensor(acc[:, seq_cols(c)], acc[:, seq_cols(c)], bank[4][:, 0:SEQ], ALU.add).then_inc(d_acc.sem, 1)
                for k in range(LN_STEPS):
                    if live(2) and k <= GATE_STEPS:
                        gate(k)
                    if live(0):
                        ln_normalise(dve, i, k, k + 1)
                if live(0):
                    dve.tensor_copy(acc[:, seq_cols(s)], lnk[:, :, :].rearrange("p t d -> p (t d)")).then_inc(d_tok.sem, 1)

        def expert_slots(eng):
            for s, live in steps(eng, NB, 1):
                for e in range(NE):
                    yield s, e, live(0), (live(0) if e else live(1)), NE * s + e

        def experts_pe(pe):
            pe.wait_ge(d_acc.sem, d_acc.after(NB - 1))
            pe.wait_ge(ld_exp.sem, 32)
            for s, e, first, second, n in expert_slots(pe):
                if first:
                    for hb in range(2):
                        pe.wait_ge(e_gelu.sem, e_gelu.after(2 * (n - 2) + hb))
                        for c in range(2):
                            ch = 2 * hb + c
                            mm = pe.matmul(bank[2 * (e % 2) + hb][:, c * SEQ:(c + 1) * SEQ], w1e[:, e, ch * P:(ch + 1) * P],
                                           xnA[:, seq_cols(s)], start=True, stop=True)
                        mm.then_inc(e_up.sem, 1)
                if second:
                    m, pe_e = n - 1, (e - 1) % NE
                    pe.wait_ge(e_gelu.sem, e_gelu.after(2 * m + 1))
                    pe.wait_ge(e_acc.sem, e_acc.after(m - 2))
                    for t in range(NT):
                        for c in range(EC):
                            mm = pe.matmul(bank[4 + pe_e % 2][:, t * P:(t + 1) * P], eh[:, pe_e % 2, c, t * P:(t + 1) * P],
                                           w2e[:, pe_e, c, :], start=(c == 0), stop=(c == EC - 1))
                    mm.then_inc(e_down.sem, 1)

        def experts_act(act):
            act.preload_act_table(ACT.Gelu)
            for s, e, first, second, n in expert_slots(act):
                if first:
                    act.wait_ge(e_down.sem, e_down.after(n - 2))
                    for hb in range(2):
                        act.wait_ge(e_up.sem, e_up.after(2 * n + hb))
                        for c in range(2):
                            ch = 2 * hb + c
                            ins = act.activation(eh[:, e % 2, ch, :], bank[2 * (e % 2) + hb][:, c * SEQ:(c + 1) * SEQ], ACT.Gelu,
                                                 bias=b1e[:, e * EC + ch:e * EC + ch + 1])
                        ins.then_inc(e_gelu.sem, 1)

        def experts_dve(dve):
            dve.wait_ge(d_acc.sem, d_acc.after(NB - 1))
            for s, e, first, second, n in expert_slots(dve):
                if second:
                    m, pe_e = n - 1, (e - 1) % NE
                    b = s if e else s - 1
                    dve.wait_ge(e_down.sem, e_down.after(m))
                    dve.wait_ge(e_acc.sem, e_acc.after(m - 1))
                    for t in range(NT):
                        if isinstance(b, int):
                            w = wA[:, b * NT + t, pe_e:pe_e + 1]
                        else:
                            w = wA[:, ds(b * NT + t, 1), pe_e:pe_e + 1].rearrange("p t e -> p (t e)")
                        a = acc[:, seq_cols(b, P, t * P)]
                        ins = dve.scalar_tensor_tensor(out=a, in0=bank[4 + pe_e % 2][:, t * P:(t + 1) * P], scalar=w, in1=a,
                                                       op0=ALU.mult, op1=ALU.add)
                    ins.then_inc(e_acc.sem, 1)

        block = ctx.enter_context(nc.Block())

        @block.sync
        def _(sp):
            for x in credited["sp"]:
                x.start(sp)
            sp.dma_start(const[:, :], A["const"]).then_inc(ld_const.sem, 16)
            sp.dma_start(xtok[:, :, :], A["L0_attn_x"].rearrange("b (t p) d -> p (b t) d", p=P)).then_inc(ld_x.sem, 16)
            for m, (w, b) in enumerate((("L0_attn_Wz", "L0_attn_bz"), ("L0_attn_Wh", "L0_attn_bh"))):
                sp.dma_start(wzh[:, m, :], A[w]).then_inc(ld_gru.sem, 16)
                sp.dma_start(bzh[:, m:m + 1], A[b].rearrange("(p o) -> p o", o=1), allow_slow_non_contiguous=True).then_inc(ld_gru.sem, 16)
            tail_loads(sp)
            sp.wait_ge(zeroed.sem, 2)
            with sp.Fori(0, DEPTH) as layer:
                load_layer(sp, layer)
                attention_sp(sp, layer)
            sp.wait_ge(y_mm.sem, y_mm.after(DEPTH * NB * UPB - 1))
            sp.dma_start(w1e, A["L1_ffn_W1"].rearrange("e p f -> p e f")).then_inc(ld_exp.sem, 16)
            sp.dma_start(w2e, A["L1_ffn_W2"].rearrange("e (c p) d -> p e c d", p=P)).then_inc(ld_exp.sem, 16)
            lat_sp(sp)
            with sp.Fori(0, NB) as b:
                sp.wait_ge(e_acc.sem, e_acc.after(NE * b + NE - 1))
                hold(sp)
                sp.dma_start(out[ds(b, 1)].rearrange("b (t p) d -> p (b t) d", p=P),
                             acc[:, seq_cols(b)].rearrange("p (t d) -> p t d", t=NT)).then_inc(st_out.sem, 16)
            sp.wait_ge(st_out.sem, 16 * NB)

        @block.gpsimd
        def _(pool):
            for x in credited["pool"]:
                x.start(pool)
            pool.memset(vBD[:, 0], 0.0).then_inc(zeroed.sem, 1)
            pool.memset(vBD[:, 1], 0.0).then_inc(zeroed.sem, 1)
            pool.wait_ge(ld_const.sem, 16)
            pool.tensor_copy(bandrhs[:, :], cst("band")[0:2 * WIN, :]).then_inc(cast_done.sem, 1)
            pool.tensor_copy(bandsel[:, :, :], cst("bandsel")[0:2 * WIN, :].rearrange("p (t q) -> p t q", t=NT)).then_inc(cast_done.sem, 1)
            pool.tensor_copy(causal[:, :, :], cst("causal").rearrange("p (t q) -> p t q", t=NT)).then_inc(cast_done.sem, 1)
            pool.tensor_copy(identb[:, :], ident).then_inc(cast_done.sem, 1)
            with pool.Fori(0, DEPTH) as layer:
                attention_pool(pool, layer)
            lat_pool(pool)

        @block.scalar
        def _(act):
            for x in credited["act"]:
                x.start(act)
            gru_act(act)
            act.wait_ge(zeroed_dve.sem, 1)
            with act.Fori(0, DEPTH) as layer:
                act.preload_act_table(ACT.Exp)
                attention_act(act, layer)
                act.preload_act_table(ACT.Gelu)
                mlp_act(act, layer)
            lat_act(act)
            gate_act(act)
            experts_act(act)

        @block.vector
        def _(dve):
            for x in credited["dve"]:
                x.start(dve)
            dve.memset(kBD[:, :, :, :, :], 0.0)
            dve.memset(woutp[:, :, :], 0.0)
            dve.memset(cvp[:, :, :, :], 0.0)
            dve.memset(uT[:, NB * SEQ:], 0.0)
            dve.memset(lns[:, 0:1], 0.0)
            dve.memset(xs[:, 0:1], 0.0).then_inc(zeroed_dve.sem, 1)
            dve.wait_ge(zeroed_dve.sem, 1)
            dve.memset(cvp[:, :, :, QD:QD + 1], 1.0)
            gru_dve(dve)
            swap_weights(dve)
            with dve.Fori(0, DEPTH) as layer:
                attention_dve(dve, layer)
                mlp_dve(dve, layer)
            lat_dve(dve)
            gate_dve(dve)
            experts_dve(dve)

        @block.tensor
        def _(pe):
            for x in credited["pe"]:
                x.start(pe)
            gru_pe(pe)
            pe.wait_ge(cast_done.sem, 4)
            pe.wait_ge(zeroed_dve.sem, 1)
            with pe.Fori(0, DEPTH) as layer:
                pe.wait_ge(ld_wa.sem, (layer + 1) * 16 * LA_LOADS)
                attention_pe(pe, layer)
                mlp_pe(pe, layer)
            lat_pe(pe)
            gate_pe(pe)
            experts_pe(pe)


def constants():
    c = np.zeros((P, CONST_N), np.float32)

    def put(name, v):
        a, b = CONST_COLS[name]
        c[:v.shape[0], a:b] = v.reshape(v.shape[0], b - a)

    f32 = np.float32
    put("ident", np.eye(P, dtype=f32))
    half = np.arange(0, DH, 2, dtype=f32)
    inv_freq = (f32(1.0) / f32(10000.0) ** (half / f32(DH))).astype(f32)
    tok = np.arange(SEQ, dtype=f32)
    freqs = (tok[:, None] * inv_freq[None, :]).astype(np.float64)
    base = ((half + f32(0.4 * DH)) / f32(1.4 * DH)).astype(np.float64)
    power = ((tok - SEQ // 2) / f32(WIN // 2)).astype(np.float64)
    scale = base[None, :] ** power[:, None]
    cos, sin = np.cos(freqs), np.sin(freqs)
    rot = np.zeros((SEQ, 4, DH))
    for m, s in ((0, scale), (2, 1.0 / scale)):
        rot[:, m] = np.concatenate([cos * s, cos * s], -1)
        rot[:, m + 1] = np.concatenate([-sin * s, sin * s], -1)
    put("rot", rot.reshape(NT, P, 4, DH).transpose(1, 0, 2, 3).astype(f32))
    inv8 = (f32(1.0) / f32(10000.0) ** (np.arange(0, QD, 2, dtype=f32) / f32(QD))).astype(f32)
    ang = (tok[:, None] * inv8[None, :]).astype(np.float64)
    pair = (np.arange(P) % QD) // 2
    sign = np.where(np.arange(P) % 2 == 0, -1.0, 1.0)[:, None]
    put("rope", np.concatenate([np.cos(ang)[:, pair].T, np.sin(ang)[:, pair].T * sign], 1).astype(f32))
    rows = np.arange(P)
    put("rowmask", (rows[:, None] % (GRP * QD) // QD == np.arange(GRP)[None, :]).astype(f32))
    put("zsel", ((rows[:, None] % 32 == QD) & (rows[:, None] // 32 == rows[None, :] // 32)).astype(f32))
    put("iota", np.tile(np.arange(NE, dtype=f32), (P, 1)))
    i, j = np.arange(WIN)[:, None], np.arange(2 * WIN)[None, :]
    band = np.where((i <= j) & (j <= i + WIN), 0.0, NEG)
    edge = np.where(j < WIN, NEG, 0.0) + 0.0 * i
    put("band", np.tile(np.concatenate([band, edge], 0), (1, HH)).astype(f32))
    sel = np.zeros((2 * WIN, NT, P), f32)
    for w in range(NWT):
        sel[np.arange(WIN), :, w * WIN + np.arange(WIN)] = 1.0
    sel[WIN + np.arange(WIN), 0, np.arange(WIN)] = 1.0
    put("bandsel", sel)
    tri = np.where(rows[None, :] <= rows[:, None], 0.0, NEG)
    put("causal", np.stack([np.tile(tri, (1, 4)), np.tile(np.concatenate([0.0 * tri, tri], 1), (1, 2))], 1).astype(f32))
    return c


_INS = ['L0_attn_x', 'L0_attn_Wz', 'L0_attn_bz', 'L0_attn_Wh', 'L0_attn_bh', 'L0_ffn_Wqkv', 'L0_ffn_q_scale',
        'L0_ffn_k_scale', 'L0_ffn_Wo', 'L0_ffn_ln_g', 'L0_ffn_ln_b', 'L0_ffn_W1', 'L0_ffn_b1', 'L0_ffn_W2', 'L0_ffn_b2',
        'L1_attn_Wqa', 'L1_attn_Wqb', 'L1_attn_Wkva', 'L1_attn_Wkvb', 'L1_attn_Wout', 'L1_attn_bout', 'L1_ffn_W1',
        'L1_ffn_b1', 'L1_ffn_W2', 'L1_ffn_b2', 'L1_ffn_Wg', 'L1_ffn_bg']


def kernel(**inputs):
    import concourse.bacc as _bacc
    from concourse.bass_utils import run_bass_kernel_spmd as _run

    nc = _bacc.Bacc("TRN2", target_bir_lowering=False, num_devices=1)
    arrays = {name: np.ascontiguousarray(inputs[name]) for name in _INS}
    arrays["const"] = constants()
    A = {}
    for name, a in arrays.items():
        A[name] = nc.dram_tensor(f"in_{name}_dram", a.shape, mybir.dt.from_np(a.dtype), kind="ExternalInput").ap()
    out = nc.dram_tensor("out_0_dram", (NB, SEQ, D), F32, kind="ExternalOutput").ap()
    mixed_kernel(nc, A, out)
    r = _run(nc, [{f"in_{name}_dram": a for name, a in arrays.items()}], core_ids=[0])
    return r.results[0]["out_0_dram"]
```

```python
import math
from contextlib import ExitStack

import numpy as np

import concourse.bass as bass
from concourse import mybir
from concourse.bass import ds

F32 = mybir.dt.float32
BF16 = mybir.dt.bfloat16
I32 = mybir.dt.int32
U32 = mybir.dt.uint32
ALU = mybir.AluOpType
ACT = mybir.ActivationFunctionType
AX = mybir.AxisListType

P = 128
D = 128
NB, SEQ = 8, 256
NT = SEQ // P
DEPTH = 6
HEADS, DH = 16, 64
INNER = HEADS * DH
WIN = 32
NWT = P // WIN
NW = SEQ // WIN
HH = HEADS // 2
HP = HH // 2
UPB = NT * 2
FF = int(D * 4 * 2 / 3)
FC = math.ceil(FF / P)
FSZ = [min(P, FF - P * c) for c in range(FC)]
QH, KVH, QL, KVL, QD = 16, 4, 64, 32, 8
GRP = QH // KVH
NE, DFF = 8, 512
EC = DFF // P
TILES = NB * NT
TG = 4
NGR = TILES // TG
GW = TG * P
EPS = 1e-5
NEG = -1e30
MAGIC = float(0x5F3759DF)
NR_STEPS = 11
WL_STEPS = NR_STEPS + 3
LN_STEPS = NR_STEPS + 4

CONST_COLS = {}
_at = 0
for _name, _n in (("ident", P), ("rot", NT * 4 * DH), ("rope", 2 * SEQ), ("rowmask", GRP), ("zsel", P), ("iota", NE),
                  ("band", 512), ("bandsel", NT * P), ("causal", NT * 512)):
    CONST_COLS[_name] = (_at, _at + _n)
    _at += _n
CONST_N = _at


class Signal:

    def __init__(self, sem, per=1, credit=0):
        self.sem, self.per, self.credit = sem, per, credit

    def after(self, n, k=None):
        return (n + self.credit) * self.per + (self.per if k is None else k) if self.per > 1 else n + self.credit + 1

    def start(self, eng):
        if self.credit:
            eng.sem_inc(self.sem, self.credit * self.per)


def steps(eng, count, lag):
    for s in range(lag):
        yield s, (lambda d, s=s: s >= d)
    with eng.Fori(lag, count) as s:
        yield s, (lambda d: True)
    for s in range(count, count + lag):
        yield s, (lambda d, s=s: s - d < count)


def mixed_kernel(nc, A, out):
    with ExitStack() as ctx:
        def sb(name, shape, dt=F32):
            return ctx.enter_context(nc.sbuf_tensor(name, shape, dt))

        def sig(name, per=1, credit=0):
            return Signal(ctx.enter_context(nc.semaphore(name)), per, credit)

        bank = [ctx.enter_context(nc.psum_tensor(f"bank{i}", [P, 512], F32)) for i in range(8)]

        const = sb("const", [P, CONST_N])

        def cst(name):
            a, b = CONST_COLS[name]
            return const[:, a:b]

        ident = cst("ident")
        rot_base = cst("rot").rearrange("p (t k d) -> p t k d", t=NT, k=4)
        rope = cst("rope")
        bandrhs = sb("bandrhs", [2 * WIN, 512], BF16)
        bandsel = sb("bandsel", [2 * WIN, NT, P], BF16)
        causal = sb("causal", [P, NT, 512], BF16)
        identb = sb("identb", [P, P], BF16)
        xT = sb("xT", [P, NB * SEQ])
        uT = sb("uT", [P, (NB + 1) * SEQ])
        lnin = sb("lnin", [P, SEQ])
        lns = sb("lns", [P, SEQ])
        lnk = sb("lnk", [P, NT, P])
        lnx = sb("lnx", [P, NT, P])
        lnst = sb("lnst", [P, NT, 6])
        lnmv = sb("lnmv", [P, NT, 2])
        lnve = sb("lnve", [P, NT])
        lny = sb("lny", [P, NT])
        lnt = sb("lnt", [P, NT])
        xnF = sb("xnF", [P, NB * SEQ])
        xnT = xnF[:, 0:SEQ]
        wzh = sb("wzh", [P, 2, D])
        bzh = sb("bzh", [P, 2])
        wqkv = sb("wqkv", [P, 3 * INNER])
        wo = sb("wo", [P, HEADS // 2, D])
        qks = sb("qks", [P, 4, DH])
        rot = sb("rot_t", [P, NT, 4, DH])
        xs = sb("xs", [P, SEQ])
        sq = sb("sq", [P, HEADS, DH])
        sqh = sb("sqh", [P, HEADS, DH // 2])
        ss = sb("ss", [P, HEADS])
        rn = sb("rn", [P, HEADS])
        rnt = sb("rnt", [P, HEADS])
        sc8 = sb("sc8", [P, UPB, HH])
        t1 = sb("t1", [P, 2, HH, DH])
        t2 = sb("t2", [P, 2, HH, DH])
        kr0 = sb("kr0", [P, HH, DH])
        qr = sb("qr", [P, 2, HH * DH])
        kr = sb("kr", [P, 2, HH, DH])
        qT = sb("qT", [P, HP, P])
        kBD = sb("kBD", [P, 2, HP, 2, WIN + SEQ])
        vS = sb("vS", [P, UPB, 2, HP, DH])
        vBD = sb("vBD", [P, 2, NW, 2, HP, DH])
        mx = sb("mx", [P, 2, HH])
        nbias = sb("nbias", [P, 2, HH])
        pr = sb("pr", [P, 2, HH, 2 * WIN])
        psm = sb("psm", [P, 2, HH])
        rinv = sb("rinv", [P, 2, HH])
        pT = sb("pT", [P, HP, P])
        ob = sb("ob", [P, 2, HH, DH])
        attT = sb("attT", [P, HEADS // 2, SEQ])
        w1 = sb("w1", [P, 2 * FF])
        w2 = sb("w2", [P, FC, D])
        lngb = sb("lngb", [P, 2])
        b1c = sb("b1c", [P, 2, FC])
        b2c = sb("b2c", [P, 1])
        gs = sb("gs", [P, FC, SEQ])
        hT = sb("hT", [P, 2, FC, SEQ])

        wqa, wqb, wkva = sb("wqa", [P, QL]), sb("wqb", [QL, 2, P]), sb("wkva", [P, KVL])
        wkvn, wkb, wvb = sb("wkvn", [KVL, KVH, QD, 2]), sb("wkb", [KVL, 2, P]), sb("wvb", [KVL, KVH * QD])
        woutp, boutc = sb("woutp", [P, GRP, D]), sb("boutc", [P, 1])
        cqa, ckva = sb("cqa", [QL, SEQ]), sb("ckva", [KVL, SEQ])
        cq, ck = sb("cq", [P, SEQ]), sb("ck", [P, SEQ])
        cvn = sb("cvn", [P, NT, KVH, QD])
        cvp = sb("cvp", [P, NT, KVH, 32])
        zsel = cst("zsel")
        ZK = GRP * P // 32
        crs = sb("crs", [P, NT, 2, ZK])
        cmx, cnb = sb("cmx", [P, GRP]), sb("cnb", [P, 3, GRP])
        late = kBD[:, :, :, :, :].rearrange("p h q e k -> p (h q e k)")
        ckm = late[:, 0:1024].rearrange("p (j k) -> p j k", j=GRP)
        ct = late[:, 2048:3072].rearrange("p (m k) -> p m k", m=2)
        cp = late[:, 3072:4608].rearrange("p (g k) -> p g k", g=3)
        cpT = [vS[:, i].rearrange("p e q d -> p (e q d)") for i in range(UPB)] + [t1[:, i].rearrange("p h d -> p (h d)") for i in range(2)]
        NTB = len(cpT)
        cout = t2[:, :, :, :].rearrange("p m h d -> p m (h d)")
        late = attT[:, :, :].rearrange("p c k -> p (c k)")
        con = late[:, 0:1024].rearrange("p (t k) -> p t k", t=NT)
        zs, za = (t1[:, i].rearrange("p h d -> p (h d)") for i in range(2))
        zb, hs = (t2[:, i].rearrange("p h d -> p (h d)") for i in range(2))
        wst, wmv = sb("wst", [P, TILES, 6]), sb("wmv", [P, TILES, 2])
        wve, wy, wt = sb("wve", [P, TILES]), sb("wy", [P, TILES]), sb("wt", [P, TILES])
        wnorm = attT[:, :, :].rearrange("p c k -> p (c k)").rearrange("p (t d) -> p t d", d=P)
        xn1 = vS[:, :, :, :, :].rearrange("p j e q d -> p (j e q d)")
        wg, bgb, b2e = sb("wg", [P, NE]), sb("bgb", [P, NE]), sb("b2e", [NE, D])
        dlg, dmx = sb("dlg", [P, TILES, NE]), sb("dmx", [P, TILES, 8])
        dix, dixf = sb("dix", [P, TILES, 8], U32), sb("dixf", [P, TILES, 2])
        ddiff, dexp, dden, dp = sb("ddiff", [P, TILES]), sb("dexp", [P, TILES]), sb("dden", [P, TILES]), sb("dp", [P, 2, TILES])
        dw = sb("dw", [P, 2, TILES, NE])
        dwT = xn1[0:NE, :]
        xnA = uT
        wA = sb("wA", [P, NB * NT, NE])
        acc = sb("acc", [P, NB * SEQ])
        late = vBD[:, :, :, :, :, :].rearrange("p h w e q d -> p (h w e q d)")
        w1e = late[:, 0:NE * DFF].rearrange("p (e f) -> p e f", e=NE)
        w2e = late[:, NE * DFF:2 * NE * DFF].rearrange("p (e c d) -> p e c d", e=NE, c=EC)
        eh = wqkv[:, 0:2 * EC * SEQ].rearrange("p (m c k) -> p m c k", m=2, c=EC)
        b1e = sb("b1e", [P, NE * EC])
        xtok = acc[:, :].rearrange("p (t d) -> p t d", d=D)

        ld_const, ld_x, ld_gru = sig("ld_const"), sig("ld_x"), sig("ld_gru")
        held = sig("held")
        ld_exp = sig("ld_exp")
        ld_tail, st_out = sig("ld_tail"), sig("st_out")
        cast_done = sig("cast_done")
        zeroed, zeroed_dve = sig("zeroed"), sig("zeroed_dve")
        x_turned, x_kept = sig("x_turned"), sig("x_kept")
        ln_in = sig("ln_in", credit=1)
        ln_t1 = sig("ln_t1", credit=1)
        ln_tok = sig("ln_tok", credit=1)
        ln_stats = sig("ln_stats", credit=1)
        ln_chain = sig("ln_chain", per=NR_STEPS + 3)
        ln_t2 = sig("ln_t2", credit=1)
        ln_out = sig("ln_out", credit=1)
        w_turn, w_keep, w_norm, w_back, w_out = (sig(x) for x in ("w_turn", "w_keep", "w_norm", "w_back", "w_out"))
        w_chain = sig("w_chain", per=WL_STEPS)
        zh_done, z_sig, gru_a, gru_b, gru_scan, gru_res = (
            sig(x) for x in ("zh_done", "z_sig", "gru_a", "gru_b", "gru_scan", "gru_res"))
        ld_wa = sig("ld_wa")
        tabs = sig("tabs")
        xs_in = sig("xs_in")
        q_mm, k_mm, v_mm = (sig(x, credit=1) for x in ("q_mm", "k_mm", "v_mm"))
        qt_mm, kt_mm, s_mm = (sig(x, credit=4) for x in ("qt_mm", "kt_mm", "s_mm"))
        pt_mm, o_mm, ot_mm = (sig(x, credit=4) for x in ("pt_mm", "o_mm", "ot_mm"))
        y_mm = sig("y_mm", credit=6)
        q_sq, k_sq, v_ev = (sig(x, credit=2) for x in ("q_sq", "k_sq", "v_ev"))
        qt_ev, kt_ev, p_exp, pt_ev, ot_ev = (sig(x, credit=4) for x in ("qt_ev", "kt_ev", "p_exp", "pt_ev", "ot_ev"))
        q_mul, k_mul = sig("q_mul", credit=2), sig("k_mul", credit=2)
        s_max, s_nb, p_sum, p_inv, o_norm = (sig(x, credit=4) for x in ("s_max", "s_nb", "p_sum", "p_inv", "o_norm"))
        ss_red = sig("ss_red", per=2, credit=2)
        nr_chain = sig("nr_chain", per=NR_STEPS, credit=2)
        sc_done = sig("sc_done", credit=2)
        u_res = sig("u_res", credit=6)
        sq_half, q_add, k_add, k_norm = (sig(x, credit=2) for x in ("sq_half", "q_add", "k_add", "k_norm"))
        v_dma = [sig(f"v_dma{j}", per=16 * (10 if j % NT == 0 else 8), credit=1) for j in range(UPB)]
        ld_wf = sig("ld_wf")
        h_mm, f_mm = sig("h_mm", per=FC, credit=2), sig("f_mm", credit=3)
        g_act, h_mul = sig("g_act", per=FC, credit=1), sig("h_mul", per=FC, credit=2)
        f_res = sig("f_res", credit=NB)
        add_u = sig("add_u")
        cswap = sig("cswap")
        lat_mm, lat_ev, c_pq, c_pk, c_pv = (sig(x, credit=2) for x in ("lat_mm", "lat_ev", "c_pq", "c_pk", "c_pv"))
        c_mq, c_mk, c_cq, c_ck, cv_ev, c_cv = (sig(x, credit=2) for x in ("c_mq", "c_mk", "c_cq", "c_ck", "cv_ev", "c_cv"))
        c_ckm = sig("c_ckm", per=3)
        c_s, c_max, c_nb, c_exp, c_pt, c_ptev = (sig(x, credit=24) for x in ("c_s", "c_max", "c_nb", "c_exp", "c_pt", "c_ptev"))
        c_o = sig("c_o", credit=6)
        c_oev, c_z, c_rz, c_nrm = (sig(x, credit=4) for x in ("c_oev", "c_z", "c_rz", "c_nrm"))
        c_out = [sig(f"c_out{t}", per=16 * KVH) for t in range(NT)]
        c_back = [sig(f"c_back{t}", per=16 * KVH, credit=1) for t in range(NT)]
        c_y, c_res = sig("c_y", credit=3), sig("c_res", credit=3)
        d_lmm, d_e, d_ch = sig("d_lmm"), sig("d_e"), sig("d_ch")
        d_wT, d_wTev, d_b2, d_acc = (sig(x) for x in ("d_wT", "d_wTev", "d_b2", "d_acc"))
        e_gelu, e_up, e_down, e_acc = sig("e_gelu", credit=4), sig("e_up"), sig("e_down", credit=2), sig("e_acc", credit=2)
        TAIL_LOADS = 9 + KVH


        credited = {
            "pe": (ln_t1, ln_t2, q_mm, k_mm, v_mm, qt_mm, kt_mm, s_mm, pt_mm, o_mm, ot_mm, y_mm, h_mm, f_mm,
                   lat_mm, c_pq, c_pk, c_pv, c_s, c_pt, c_o, c_z, c_y, e_down),
            "act": (ln_out, ln_tok, q_sq, k_sq, v_ev, qt_ev, kt_ev, p_exp, pt_ev, ot_ev, g_act,
                    cv_ev, lat_ev, c_oev, c_exp, c_ptev, e_gelu),
            "dve": (ln_in, ln_stats, q_mul, k_mul, s_max, s_nb, p_sum, p_inv, o_norm,
                    ss_red, nr_chain, sc_done, u_res, h_mul, f_res,
                    c_mq, c_mk, c_max, c_nb, c_rz, c_nrm, c_res, e_acc),
            "pool": (sq_half, q_add, k_add, k_norm, c_cq, c_ck, c_cv),
            "sp": tuple(v_dma) + tuple(c_back),
        }
        LA_LOADS, LF_LOADS = 8, 10
        LN_F, LN_C = 0, DEPTH * NB

        def hold(eng):
            eng.sem_inc(held.sem, 1)

        def col(t, a):
            return t[:, a:a + 1]

        def wide_turn(pe, w, g, src, bank_):
            for t in range(TG):
                mm = pe.transpose(bank_[:, t * P:(t + 1) * P], src(g * TG + t), ident)
            mm.then_inc(w_turn.sem, 1)

        def wide_stats(dve, tok, g):
            for t in range(g * TG, (g + 1) * TG):
                ins = dve.bn_stats(wst[:, t, :], tok[:, t, :])
            return ins

        def wide_normalise(dve, w, tok):
            dve.wait_ge(w_chain.sem, w_chain.after(w, 1))
            for t in range(TILES):
                ins = dve.bn_aggr(wmv[:, t, :], wst[:, t, :])
            ins.then_inc(w_chain.sem, 1)
            dve.wait_ge(w_chain.sem, w_chain.after(w, 2))
            dve.tensor_scalar(wve[:, :], wmv[:, :, 1], EPS, None, ALU.add).then_inc(w_chain.sem, 1)
            rsqrt(dve, wy[:, :], wve[:, :], wt[:, :], w_chain, w, 3)
            dve.wait_ge(w_chain.sem, w_chain.after(w))
            for g in range(NGR):
                for t in range(g * TG, (g + 1) * TG):
                    ins = dve.tensor_scalar(wnorm[:, t, :], tok[:, t, :], wmv[:, t, 0:1], wy[:, t:t + 1], ALU.subtract, ALU.mult)
                ins.then_inc(w_norm.sem, 1)

        def wide_back(pe, w, g, bank_):
            pe.wait_ge(w_norm.sem, w_norm.after(NGR * w + g))
            for t in range(TG):
                mm = pe.transpose(bank_[:, t * P:(t + 1) * P], wnorm[:, g * TG + t, :], ident)
            mm.then_inc(w_back.sem, 1)

        def wide_out(act, w, g, bank_, dst):
            act.wait_ge(w_back.sem, w_back.after(NGR * w + g))
            act.activation(dst[:, g * GW:(g + 1) * GW], bank_[:, :], ACT.Copy).then_inc(w_out.sem, 1)

        def ln_turn_in(pe, i, src, dst):
            pe.wait_ge(ln_in.sem, ln_in.after(i))
            pe.wait_ge(ln_tok.sem, ln_tok.after(i - 1))
            for t in range(NT):
                mm = pe.transpose(dst[:, t * P:(t + 1) * P], src[:, t * P:(t + 1) * P], ident)
            mm.then_inc(ln_t1.sem, 1)

        def ln_keep(act, i, src):
            act.wait_ge(ln_t1.sem, ln_t1.after(i))
            act.wait_ge(ln_stats.sem, ln_stats.after(i - 1))
            act.activation(lnk[:, :, :].rearrange("p t d -> p (t d)"), src, ACT.Copy).then_inc(ln_tok.sem, 1)

        def ln_turn_out(pe, i, dst):
            pe.wait_ge(ln_stats.sem, ln_stats.after(i))
            pe.wait_ge(ln_out.sem, ln_out.after(i - 1))
            for t in range(NT):
                mm = pe.transpose(dst[:, t * P:(t + 1) * P], lnx[:, t, :], ident)
            mm.then_inc(ln_t2.sem, 1)

        def rsqrt(dve, y, v, tmp, chain, n, first, lo=0, hi=NR_STEPS):
            for k in range(lo, hi):
                if first + k:
                    dve.wait_ge(chain.sem, chain.after(n, first + k))
                if k == 0:
                    ins = dve.tensor_scalar(tmp.bitcast(I32), v.bitcast(I32), 1, None, ALU.logical_shift_right)
                elif k == 1:
                    ins = dve.tensor_scalar(y.bitcast(I32), tmp.bitcast(I32), -1.0, MAGIC, ALU.mult, ALU.add)
                elif k % 3 == 2:
                    ins = dve.tensor_tensor(tmp, y, y, ALU.mult)
                elif k % 3 == 0:
                    ins = dve.scalar_tensor_tensor(out=tmp, in0=tmp, scalar=-0.5, in1=v, op0=ALU.mult, op1=ALU.mult)
                else:
                    ins = dve.scalar_tensor_tensor(out=y, in0=tmp, scalar=1.5, in1=y, op0=ALU.add, op1=ALU.mult)
                ins.then_inc(chain.sem, 1)

        def ln_normalise(dve, i, lo=0, hi=LN_STEPS):
            for k in range(lo, hi):
                if k == 0:
                    dve.wait_ge(ln_tok.sem, ln_tok.after(i))
                    for t in range(NT):
                        ins = dve.bn_stats(lnst[:, t, :], lnk[:, t, :])
                    ins.then_inc(ln_chain.sem, 1)
                elif k == 1:
                    dve.wait_ge(ln_chain.sem, ln_chain.after(i, 1))
                    hold(dve)
                    for t in range(NT):
                        ins = dve.bn_aggr(lnmv[:, t, :], lnst[:, t, :])
                    ins.then_inc(ln_chain.sem, 1)
                elif k == 2:
                    dve.wait_ge(ln_chain.sem, ln_chain.after(i, 2))
                    dve.tensor_scalar(lnve[:, :], lnmv[:, :, 1], EPS, None, ALU.add).then_inc(ln_chain.sem, 1)
                elif k < 3 + NR_STEPS:
                    rsqrt(dve, lny[:, :], lnve[:, :], lnt[:, :], ln_chain, i, 3, k - 3, k - 2)
                else:
                    dve.wait_ge(ln_chain.sem, ln_chain.after(i))
                    dve.wait_ge(ln_t2.sem, ln_t2.after(i - 1))
                    for t in range(NT):
                        ins = dve.tensor_scalar(lnx[:, t, :], lnk[:, t, :], lnmv[:, t, 0:1], lny[:, t:t + 1],
                                                ALU.subtract, ALU.mult)
                    ins.then_inc(ln_stats.sem, 1)

        def seq_cols(b, n=SEQ, off=0):
            return ds(b * SEQ + off, n) if not isinstance(b, int) else slice(b * SEQ + off, b * SEQ + off + n)

        def shifted_copy(dve, dst, b):
            h = D // 2
            dve.tensor_copy(dst[0:h, :], uT[0:h, seq_cols(b)])
            return dve.tensor_copy(dst[h:D, 1:SEQ], uT[h:D, seq_cols(b, SEQ - 1)])

        L_T, L_S, L_P, L_O = 1, 2, 3, 4
        L_N = UPB + 1

        def units(eng, layer):
            for bs, live in steps(eng, NB, 2):
                B = layer * NB + bs
                n0 = B * UPB
                for j in range(UPB):
                    yield bs, B, j, (lambda d, j=j, live=live: live((d - j + UPB - 1) // UPB)), (lambda d, n0=n0, j=j: n0 + j - d)

        def at_end(bs, j):
            return isinstance(bs, int) and bs == NB + 1 and j == 2

        def attention_pe(pe, layer):
            for bs, B, j, live, unit in units(pe, layer):
                if live(0):
                    n, h, t = unit(0), j // NT, j % NT
                    if j == 0:
                        pe.wait_ge(xs_in.sem, xs_in.after(layer * (NB + 1) + bs))
                    xt = xs[:, t * P:(t + 1) * P]
                    pe.wait_ge(q_sq.sem, q_sq.after(n - 1))
                    pe.matmul(bank[0][:, :], xt, wqkv[:, h * 512:(h + 1) * 512], start=True, stop=True).then_inc(q_mm.sem, 1)
                    pe.wait_ge(k_mul.sem, k_mul.after(n - 1))
                    pe.matmul(bank[1][:, :], xt, wqkv[:, INNER + h * 512:INNER + (h + 1) * 512],
                              start=True, stop=True).then_inc(k_mm.sem, 1)
                if live(L_N + j) and j in (1, 3):
                    i = LN_F + B - 2
                    last = (layer + 1) * NB * UPB - 1
                    pe.wait_ge(v_ev.sem, v_ev.after(unit(1) if live(1) else last))
                    pe.wait_ge(u_res.sem, u_res.after(unit(L_O + 1) if live(L_O + 1) else last))
                    if j == 1:
                        ln_turn_in(pe, i, lns, bank[2][:, 0:SEQ])
                    else:
                        ln_turn_out(pe, i, bank[2][:, 0:SEQ])
                if live(L_P):
                    n = unit(L_P)
                    pe.wait_ge(p_exp.sem, p_exp.after(n))
                    pe.wait_ge(pt_ev.sem, pt_ev.after(n - 1))
                    for p in range(HP):
                        mm = pe.transpose(bank[6][:, p * P:(p + 1) * P],
                                          pr[:, (j - L_P) % 2, 2 * p:2 * p + 2, :].rearrange("q h k -> q (h k)"), ident)
                    mm.then_inc(pt_mm.sem, 1)
                if live(L_O):
                    n = unit(L_O)
                    pe.wait_ge(o_norm.sem, o_norm.after(n))
                    if live(L_S):
                        pe.wait_ge(kt_ev.sem, kt_ev.after(unit(L_S)))
                    else:
                        pe.wait_ge(ot_ev.sem, ot_ev.after(n - 1))
                    for p in range(HP):
                        mm = pe.transpose(bank[4][:, p * P:(p + 1) * P],
                                          ob[:, (j - L_O) % 2, 2 * p:2 * p + 2, :].rearrange("q h k -> q (h k)"), ident)
                    mm.then_inc(ot_mm.sem, 1)
                if live(0):
                    n = unit(0)
                    pe.wait_ge(v_ev.sem, v_ev.after(n - 1))
                    pe.wait_ge(u_res.sem, u_res.after(n - L_O - 1))
                    if j == 0:
                        if isinstance(bs, int) and bs == 0:
                            pe.wait_ge(f_res.sem, f_res.after(B - 1))
                    if j in (1, 3) and live(L_N + j):
                        read, i = (ln_tok if j == 1 else ln_out), LN_F + B - 2
                        pe.wait_ge(read.sem, read.after(i))
                    pe.matmul(bank[2][:, :], xt, wqkv[:, 2 * INNER + h * 512:2 * INNER + (h + 1) * 512],
                              start=True, stop=True).then_inc(v_mm.sem, 1)
                if live(L_S):
                    n = unit(L_S)
                    h, t = (j - L_S) % UPB // NT, (j - L_S) % NT
                    pe.wait_ge(qt_ev.sem, qt_ev.after(n))
                    pe.wait_ge(kt_ev.sem, kt_ev.after(n))
                    pe.wait_ge(p_exp.sem, p_exp.after(n - 1))
                    pe.matmul(bank[5][:, :], bandsel[:, t, :], bandrhs[:, :], start=True, stop=False, skip_group_check=True)
                    for p in range(HP):
                        for w in range(NWT):
                            k0 = (t * NWT + w) * WIN
                            mm = pe.matmul(bank[5][w * WIN:(w + 1) * WIN, p * P:(p + 1) * P],
                                           qT[:, p, w * WIN:(w + 1) * WIN], kBD[:, h, p, :, k0:k0 + 2 * WIN],
                                           start=False, stop=True, skip_group_check=True)
                    mm.then_inc(s_mm.sem, 1)
                if live(L_T):
                    n, par = unit(L_T), (j - L_T) % 2
                    pe.wait_ge(q_add.sem, q_add.after(n))
                    pe.wait_ge(qt_ev.sem, qt_ev.after(n - 1))
                    for p in range(HP):
                        mm = pe.transpose(bank[3][:, p * P:(p + 1) * P], qr[:, par, p * P:(p + 1) * P], ident)
                    mm.then_inc(qt_mm.sem, 1)
                if live(L_P):
                    n = unit(L_P)
                    jj = (j - L_P) % UPB
                    h, t = jj // NT, jj % NT
                    pe.wait_ge(pt_ev.sem, pt_ev.after(n))
                    pe.wait_ge(v_dma[jj].sem, v_dma[jj].after(B if j >= L_P else B - 1))
                    pe.wait_ge(o_norm.sem, o_norm.after(n - 1))
                    for p in range(HP):
                        for w in range(NWT):
                            mm = pe.matmul(bank[7][w * WIN:(w + 1) * WIN, p * P:(p + 1) * P],
                                           pT[:, p, w * WIN:(w + 1) * WIN], vBD[:, h, t * NWT + w, :, p, :],
                                           start=True, stop=True)
                    mm.then_inc(o_mm.sem, 1)
                if live(L_T):
                    n, par = unit(L_T), (j - L_T) % 2
                    pe.wait_ge(k_norm.sem, k_norm.after(n))
                    pe.wait_ge(ot_ev.sem, ot_ev.after(n - 3))
                    for p in range(HP):
                        mm = pe.transpose(bank[4][:, p * P:(p + 1) * P],
                                          kr[:, par, 2 * p:2 * p + 2, :].rearrange("q h k -> q (h k)"), ident)
                    mm.then_inc(kt_mm.sem, 1)
                if live(L_O):
                    n, jj = unit(L_O), (j - L_O) % UPB
                    h, t = jj // NT, jj % NT
                    pe.wait_ge(ot_ev.sem, ot_ev.after(n))
                    pe.wait_ge(v_ev.sem, v_ev.after(unit(0) if live(0) else n))
                    pe.wait_ge(u_res.sem, u_res.after(n - 1))
                    if j in (1, 3) and live(L_N + j) and not live(0):
                        read, i = (ln_tok if j == 1 else ln_out), LN_F + B - 2
                        pe.wait_ge(read.sem, read.after(i))
                    for c in range(HP):
                        mm = pe.matmul(bank[2][:, 0:P], wo[:, h * HP + c, :], attT[:, h * HP + c, t * P:(t + 1) * P],
                                       start=(c == 0), stop=(c == HP - 1))
                    mm.then_inc(y_mm.sem, 1)
                if at_end(bs, j):
                    pe.wait_ge(ld_wf.sem, (layer + 1) * 16 * LF_LOADS)
                    mlp_up(pe, layer * NB, 0)

        def attention_act(act, layer):
            for bs, B, j, live, unit in units(act, layer):
                if live(0):
                    n = unit(0)
                    act.wait_ge(k_mm.sem, k_mm.after(n))
                    act.wait_ge(sq_half.sem, sq_half.after(n - 1))
                    act.activation(sq[:, HH:, :], bank[1][:, :].rearrange("p (h d) -> p h d", d=DH), ACT.Square).then_inc(k_sq.sem, 1)
                if live(L_N + j) and j == 1:
                    ln_keep(act, LN_F + B - 2, bank[2][:, 0:SEQ])
                if live(L_N + j) and j == 3:
                    act.wait_ge(ln_t2.sem, ln_t2.after(LN_F + B - 2))
                    act.wait_ge(ld_wf.sem, (layer + 1) * 16 * LF_LOADS)
                    act.activation(xnF[:, seq_cols(bs - 2)], bank[2][:, 0:SEQ], ACT.Identity, bias=lngb[:, 1:2],
                                   scale=lngb[:, 0:1]).then_inc(ln_out.sem, 1)
                if live(0):
                    act.wait_ge(q_mul.sem, q_mul.after(n))
                    act.activation(sq[:, 0:HH, :], bank[0][:, :].rearrange("p (h d) -> p h d", d=DH), ACT.Square).then_inc(q_sq.sem, 1)
                    act.wait_ge(v_mm.sem, v_mm.after(n))
                    act.wait_ge(v_dma[j].sem, v_dma[j].after(B - 1))
                    act.activation(vS[:, j, :, :, :].rearrange("p e q d -> p q e d"),
                                   bank[2][:, :].rearrange("p (q e d) -> p q e d", e=2, d=DH), ACT.Copy).then_inc(v_ev.sem, 1)
                if live(L_P):
                    n = unit(L_P)
                    act.wait_ge(pt_mm.sem, pt_mm.after(n))
                    act.wait_ge(o_mm.sem, o_mm.after(n - 1))
                    act.activation(pT[:, :, :].rearrange("p a b -> p (a b)"), bank[6][:, :], ACT.Copy).then_inc(pt_ev.sem, 1)
                if live(L_O):
                    n = unit(L_O)
                    jj = (j - L_O) % UPB
                    h, t = jj // NT, jj % NT
                    act.wait_ge(ot_mm.sem, ot_mm.after(n))
                    act.activation(attT[:, h * HP:(h + 1) * HP, t * P:(t + 1) * P],
                                   bank[4][:, :].rearrange("p (a b) -> p a b", a=HP), ACT.Copy).then_inc(ot_ev.sem, 1)
                if live(L_S):
                    n = unit(L_S)
                    par = (j - L_S) % 2
                    act.wait_ge(s_nb.sem, s_nb.after(n))
                    act.wait_ge(pt_mm.sem, pt_mm.after(n - 2))
                    act.wait_ge(p_sum.sem, p_sum.after(n - 2))
                    for hd in range(HH):
                        ins = act.activation(pr[:, par, hd, :], bank[5][:, hd * 64:(hd + 1) * 64], ACT.Exp,
                                             scale=sc8[:, (j - L_S) % UPB, hd:hd + 1], bias=nbias[:, par, hd:hd + 1])
                    ins.then_inc(p_exp.sem, 1)
                if live(L_T):
                    n = unit(L_T)
                    jj = (j - L_T) % UPB
                    h, t = jj // NT, jj % NT
                    act.wait_ge(qt_mm.sem, qt_mm.after(n))
                    act.activation(qT[:, :, :].rearrange("p a b -> p (a b)"), bank[3][:, :], ACT.Copy).then_inc(qt_ev.sem, 1)
                    act.wait_ge(kt_mm.sem, kt_mm.after(n))
                    for e in range(2):
                        ins = act.activation(kBD[64 * e:64 * e + 64, h, :, e, WIN + t * P:WIN + (t + 1) * P],
                                             bank[4][64 * e:64 * e + 64, :].rearrange("p (a b) -> p a b", a=HP), ACT.Copy)
                    ins.then_inc(kt_ev.sem, 1)
                if at_end(bs, j):
                    act.preload_act_table(ACT.Gelu)
                    mlp_gelu(act, layer * NB)

        def attention_dve(dve, layer):
            dve.wait_ge(tabs.sem, layer + 1)
            for bs, B, j, live, unit in units(dve, layer):
                def factors(lag, lo, hi):
                    if live(lag):
                        if lo == 0:
                            n = unit(lag)
                            dve.wait_ge(ss_red.sem, ss_red.after(n, 2))
                            dve.wait_ge(k_norm.sem, k_norm.after(n - 1))
                            dve.wait_ge(sc_done.sem, sc_done.after(n - 1))
                        rsqrt(dve, rn[:, :], ss[:, :], rnt[:, :], nr_chain, unit(lag), 0, lo, hi)

                def norm(at, lo, hi):
                    if j == at and live(L_N + j):
                        ln_normalise(dve, LN_F + B - 2, lo, hi)

                t = j % NT
                for m, (mm, mul, add) in enumerate(((q_mm, q_mul, q_add), (k_sq, k_mul, k_add))):
                    if live(0):
                        n = unit(0)
                        src = bank[m][:, :].rearrange("p (h d) -> p h d", d=DH)
                        swp = bank[m][:, :].rearrange("p (h s d) -> p h s d", h=HH, s=2)[:, :, ::-1, :]
                        tab = rot[:, t, 2 * m:2 * m + 2, :]
                        dve.wait_ge(mm.sem, mm.after(n))
                        dve.wait_ge(add.sem, add.after(n - 1))
                        dve.tensor_tensor(t1[:, m], src, tab[:, 0, :].unsqueeze(1).broadcast_to([P, HH, DH]), ALU.mult)
                    factors(L_T, 4 + 2 * m, 5 + 2 * m)
                    if live(0):
                        dve.tensor_tensor(t2[:, m].rearrange("p h (s d) -> p h s d", s=2), swp,
                                          tab[:, 1, :].rearrange("p (s d) -> p s d", s=2).unsqueeze(1).broadcast_to([P, HH, 2, DH // 2]),
                                          ALU.mult).then_inc(mul.sem, 1)
                    factors(L_T, 5 + 2 * m, 6 + 2 * m)
                if live(L_P):
                    n, par = unit(L_P), (j - L_P) % 2
                    dve.wait_ge(p_exp.sem, p_exp.after(n))
                    dve.tensor_reduce(psm[:, par, :], pr[:, par], AX.X, ALU.add).then_inc(p_sum.sem, 1)
                norm(2, 6, 7)
                factors(L_T, 8, 9)
                if live(L_P):
                    dve.wait_ge(p_sum.sem, p_sum.after(n))
                    dve.wait_ge(o_norm.sem, o_norm.after(n - 2))
                    dve.reciprocal(rinv[:, par, :], psm[:, par, :]).then_inc(p_inv.sem, 1)
                norm(2, 7, 8)
                factors(L_T, 9, NR_STEPS)
                if live(L_S):
                    n, par = unit(L_S), (j - L_S) % 2
                    dve.wait_ge(s_mm.sem, s_mm.after(n))
                    dve.tensor_reduce(mx[:, par, :], bank[5][:, :].rearrange("p (h k) -> p h k", h=HH), AX.X, ALU.max).then_inc(s_max.sem, 1)
                if live(L_S):
                    dve.wait_ge(s_max.sem, s_max.after(n))
                    dve.wait_ge(sc_done.sem, sc_done.after(n))
                    dve.wait_ge(p_exp.sem, p_exp.after(n - 2))
                    dve.scalar_tensor_tensor(out=nbias[:, par, :], in0=mx[:, par, :], scalar=-1.0,
                                             in1=sc8[:, (j - L_S) % UPB, :], op0=ALU.mult, op1=ALU.mult).then_inc(s_nb.sem, 1)
                norm(2, 8, 9)
                if live(L_T):
                    n, jj = unit(L_T), (j - L_T) % UPB
                    dve.wait_ge(nr_chain.sem, nr_chain.after(n))
                    dve.wait_ge(p_exp.sem, p_exp.after(n - UPB))
                    dve.tensor_scalar(sc8[:, jj, :], rn[:, 0:HH], 8.0, None, ALU.mult).then_inc(sc_done.sem, 1)
                norm(2, 9, 10)
                if live(0):
                    n = unit(0)
                    dve.wait_ge(sq_half.sem, sq_half.after(n))
                    dve.wait_ge(nr_chain.sem, nr_chain.after(n - 1))
                    dve.tensor_reduce(ss[:, :], sqh[:, :, :], AX.X, ALU.add).then_inc(ss_red.sem, 1)
                norm(1, 0, 1)
                if j == UPB - 1 and live(0):
                    dve.wait_ge(v_mm.sem, v_mm.after(unit(0)))
                    shifted_copy(dve, xs, bs + 1).then_inc(xs_in.sem, 1)
                if live(0):
                    dve.wait_ge(ss_red.sem, ss_red.after(n, 1))
                    dve.tensor_scalar(ss[:, :], ss[:, :], 1e-24, None, ALU.max).then_inc(ss_red.sem, 1)
                norm(1, 1, 2)
                norm(2, 10, 11)
                if live(L_P):
                    n, par = unit(L_P), (j - L_P) % 2
                    dve.wait_ge(o_mm.sem, o_mm.after(n))
                    dve.wait_ge(p_inv.sem, p_inv.after(n))
                    dve.wait_ge(ot_mm.sem, ot_mm.after(n - 2))
                    dve.tensor_tensor(ob[:, par], bank[7][:, :].rearrange("p (h d) -> p h d", h=HH),
                                      rinv[:, par, :].unsqueeze(2).broadcast_to([P, HH, DH]), ALU.mult).then_inc(o_norm.sem, 1)
                norm(1, 2, 3)
                norm(2, 11, 12)
                for k in range(4):
                    factors(0, k, k + 1)
                    if k < 3:
                        norm(1, 3 + k, 4 + k)
                        norm(2, 12 + k, 13 + k)
                if j == 0 and live(L_N + j):
                    dve.wait_ge(u_res.sem, u_res.after(unit(L_N)))
                    dve.wait_ge(ln_t1.sem, ln_t1.after(LN_F + B - 3))
                    shifted_copy(dve, lns, bs - 2).then_inc(ln_in.sem, 1)
                if live(L_O):
                    n = unit(L_O)
                    u = uT[:, seq_cols(bs if j >= L_O else bs - 1, P, (j - L_O) % NT * P)]
                    dve.wait_ge(y_mm.sem, y_mm.after(n))
                    dve.wait_ge(u_res.sem, u_res.after(n - NT))
                    dve.tensor_tensor(u, u, bank[2][:, 0:P], ALU.add).then_inc(u_res.sem, 1)
                if at_end(bs, j):
                    dve.wait_ge(ld_wf.sem, (layer + 1) * 16 * LF_LOADS)
                    for c in range(FC):
                        mlp_gate(dve, layer * NB, 0, c)

        def attention_pool(pool, layer):
            pool.wait_ge(ld_wa.sem, (layer + 1) * 16 * LA_LOADS)
            pool.wait_ge(k_mul.sem, k_mul.after(layer * NB * UPB - 1))
            for t in range(NT):
                ins = pool.tensor_tensor(rot[:, t], rot_base[:, t], qks[:, :, :], ALU.mult)
            ins.then_inc(tabs.sem, 1)
            for bs, B, j, live, unit in units(pool, layer):
                if live(0):
                    n, par = unit(0), j % 2
                    pool.wait_ge(q_mul.sem, q_mul.after(n))
                    pool.wait_ge(qt_mm.sem, qt_mm.after(n - 2))
                    pool.tensor_tensor(qr[:, par, :].rearrange("p (h d) -> p h d", h=HH), t1[:, 0], t2[:, 0], ALU.add).then_inc(q_add.sem, 1)
                    pool.wait_ge(k_sq.sem, k_sq.after(n))
                    pool.wait_ge(q_sq.sem, q_sq.after(n))
                    pool.wait_ge(ss_red.sem, ss_red.after(n - 1, 1))
                    pool.tensor_tensor(sqh[:, :, :], sq[:, :, 0:DH // 2], sq[:, :, DH // 2:], ALU.add).then_inc(sq_half.sem, 1)
                if live(L_T):
                    n, par = unit(L_T), (j - L_T) % 2
                    pool.wait_ge(k_add.sem, k_add.after(n))
                    pool.wait_ge(nr_chain.sem, nr_chain.after(n))
                    pool.wait_ge(kt_mm.sem, kt_mm.after(n - 2))
                    pool.tensor_tensor(kr[:, par], kr0[:, :, :], rn[:, HH:].unsqueeze(2).broadcast_to([P, HH, DH]),
                                       ALU.mult).then_inc(k_norm.sem, 1)
                if live(0):
                    n = unit(0)
                    pool.wait_ge(k_mul.sem, k_mul.after(n))
                    pool.wait_ge(k_norm.sem, k_norm.after(n - 1))
                    pool.tensor_tensor(kr0[:, :, :], t1[:, 1], t2[:, 1], ALU.add).then_inc(k_add.sem, 1)

        def value_moves(h, t, j):
            for e in range(2):
                base = 64 * e
                for w in range(t * NWT, (t + 1) * NWT + 1):
                    lo = w * WIN - WIN
                    a, b = max(lo, t * P), min(lo + 2 * WIN, (t + 1) * P)
                    if w < NW and a < b:
                        yield (vBD[base + a - lo:base + b - lo, h, w, e, :, :], vS[a - t * P:b - t * P, j, e, :, :])

        def attention_sp(sp, layer):
            with sp.Fori(0, NB) as b:
                B = layer * NB + b
                for j in range(UPB):
                    n = B * UPB + j
                    sp.wait_ge(v_ev.sem, v_ev.after(n))
                    hold(sp)
                    sp.wait_ge(o_mm.sem, o_mm.after(n - 3))
                    for dst, src in value_moves(j // NT, j % NT, j):
                        sp.dma_start(dst, src).then_inc(v_dma[j].sem, 16)

        def gated_cols(s, c):
            if isinstance(s, int):
                return hT[0:FSZ[c], s % 2, c, :]
            return hT[0:FSZ[c], ds(s % 2, 1), c, :].rearrange("p m k -> p (m k)")

        def is_first(s):
            return isinstance(s, int) and s == 0

        def mlp_up(pe, B, s):
            pe.wait_ge(ln_out.sem, ln_out.after(LN_F + B))
            for c in range(FC):
                pe.wait_ge(h_mul.sem, h_mul.after(B - 1, c + 1))
                for m in range(2):
                    o = m * FF + c * P
                    mm = pe.matmul(bank[3 + c][0:FSZ[c], m * SEQ:(m + 1) * SEQ], w1[:, o:o + FSZ[c]], xnF[:, seq_cols(s)],
                                   start=True, stop=True)
                mm.then_inc(h_mm.sem, 1)

        def mlp_gelu(act, B):
            for c in range(FC):
                act.wait_ge(h_mm.sem, h_mm.after(B, c + 1))
                act.wait_ge(h_mul.sem, h_mul.after(B - 1, c + 1))
                act.activation(gs[0:FSZ[c], c, :], bank[3 + c][0:FSZ[c], SEQ:2 * SEQ], ACT.Gelu,
                               bias=b1c[0:FSZ[c], 1, c:c + 1]).then_inc(g_act.sem, 1)

        def mlp_gate(dve, B, s, c):
            dve.wait_ge(g_act.sem, g_act.after(B, c + 1))
            dve.wait_ge(f_mm.sem, f_mm.after(B - 2))
            dve.scalar_tensor_tensor(out=gated_cols(s, c), in0=bank[3 + c][0:FSZ[c], 0:SEQ],
                                     scalar=b1c[0:FSZ[c], 0, c:c + 1], in1=gs[0:FSZ[c], c, :],
                                     op0=ALU.add, op1=ALU.mult).then_inc(h_mul.sem, 1)

        def mlp_pe(pe, layer):
            pe.wait_ge(u_res.sem, u_res.after((layer + 1) * NB * UPB - 1))
            hold(pe)
            for s, live in steps(pe, NB, 1):
                B = layer * NB + s
                if live(0) and not is_first(s):
                    mlp_up(pe, B, s)
                if live(1):
                    pe.wait_ge(h_mul.sem, h_mul.after(B - 1))
                    pe.wait_ge(f_res.sem, f_res.after(B - 2))
                    pe.wait_ge(ln_out.sem, ln_out.after(LN_F + (layer + 1) * NB - 1))
                    for c in range(FC):
                        mm = pe.matmul(bank[2][:, 0:SEQ], w2[0:FSZ[c], c, :], gated_cols(s - 1, c), start=(c == 0), stop=(c == FC - 1))
                    mm.then_inc(f_mm.sem, 1)

        def mlp_act(act, layer):
            with act.Fori(1, NB) as s:
                mlp_gelu(act, layer * NB + s)

        def mlp_dve(dve, layer):
            for s, live in steps(dve, NB, 1):
                B = layer * NB + s
                for c in range(FC):
                    if live(0) and not is_first(s):
                        mlp_gate(dve, B, s, c)
                if live(1):
                    b = s - 1
                    if not live(0):
                        dve.wait_ge(f_res.sem, f_res.after(layer * NB))
                        shifted_copy(dve, xs, 0).then_inc(xs_in.sem, 1)
                    dve.wait_ge(f_mm.sem, f_mm.after(B - 1))
                    dve.scalar_tensor_tensor(out=uT[:, seq_cols(b)], in0=bank[2][:, 0:SEQ], scalar=b2c[:, 0:1],
                                             in1=uT[:, seq_cols(b)], op0=ALU.add, op1=ALU.add).then_inc(f_res.sem, 1)

        def load_layer(sp, layer):
            def row(name):
                return A[name][ds(layer, 1)]

            half = DH // 2
            sp.wait_ge(y_mm.sem, y_mm.after(layer * NB * UPB - 1))
            hold(sp)
            for m, name in ((0, "L0_ffn_q_scale"), (2, "L0_ffn_k_scale")):
                v = row(name)
                sp.dma_start(qks[:, m, :], v.broadcast_to([P, DH])).then_inc(ld_wa.sem, 16)
                sp.dma_start(qks[:, m + 1, 0:half], v[:, half:DH].broadcast_to([P, half])).then_inc(ld_wa.sem, 16)
                sp.dma_start(qks[:, m + 1, half:DH], v[:, 0:half].broadcast_to([P, half])).then_inc(ld_wa.sem, 16)
            sp.dma_start(wqkv[:, :], row("L0_ffn_Wqkv").rearrange("l p n -> (l p) n")).then_inc(ld_wa.sem, 16)
            sp.dma_start(wo[:, :, :], row("L0_ffn_Wo").rearrange("l (c p) n -> p (l c) n", p=P)).then_inc(ld_wa.sem, 16)
            sp.wait_ge(f_res.sem, f_res.after(layer * NB - 1))
            hold(sp)
            full = (FC - 1) * P
            sp.dma_start(w1[:, :], row("L0_ffn_W1").rearrange("l p n -> (l p) n")).then_inc(ld_wf.sem, 16)
            v = row("L0_ffn_W2")
            sp.dma_start(w2[:, 0:FC - 1, :], v[:, 0:full, :].rearrange("l (c p) n -> p (l c) n", p=P)).then_inc(ld_wf.sem, 16)
            sp.dma_start(w2[0:FF - full, FC - 1, :], v[:, full:FF, :].rearrange("l p n -> (l p) n")).then_inc(ld_wf.sem, 16)
            v = row("L0_ffn_b1")
            for m in range(2):
                o = m * FF
                sp.dma_start(b1c[:, m, 0:FC - 1], v[:, o:o + full].rearrange("l (c p) -> p (l c)", p=P), allow_slow_non_contiguous=True).then_inc(ld_wf.sem, 16)
                sp.dma_start(b1c[0:FF - full, m, FC - 1:FC], v[:, o + full:o + FF].rearrange("l p -> p l"), allow_slow_non_contiguous=True).then_inc(ld_wf.sem, 16)
            for m, name in enumerate(("L0_ffn_ln_g", "L0_ffn_ln_b")):
                sp.dma_start(lngb[:, m:m + 1], row(name).rearrange("l p -> p l"), allow_slow_non_contiguous=True).then_inc(ld_wf.sem, 16)
            sp.dma_start(b2c[:, 0:1], row("L0_ffn_b2").rearrange("l p -> p l"), allow_slow_non_contiguous=True).then_inc(ld_wf.sem, 16)

        def tail_loads(sp):
            def load(dst, src, **how):
                sp.dma_start(dst, src, **how).then_inc(ld_tail.sem, 16)

            load(wqa[:, :], A["L1_attn_Wqa"])
            load(wqb[:, 0, :], A["L1_attn_Wqb"])
            load(wkva[:, :], A["L1_attn_Wkva"])
            load(wkvn[:, :, :, :], A["L1_attn_Wkvb"].rearrange("k (r d m) -> k r d m", r=KVH, d=QD))
            sp.wait_ge(zeroed_dve.sem, 1)
            for r in range(KVH):
                load(woutp[32 * r:32 * r + QD, :, :],
                     A["L1_attn_Wout"][r * GRP * QD:(r + 1) * GRP * QD, :].rearrange("(j d) n -> d j n", j=GRP))
            load(boutc[:, :], A["L1_attn_bout"].rearrange("(p o) -> p o", o=1), allow_slow_non_contiguous=True)
            load(b1e[:, :], A["L1_ffn_b1"].rearrange("e (c p) -> p (e c)", p=P), allow_slow_non_contiguous=True)
            load(b2e[:, :], A["L1_ffn_b2"])
            load(wg[:, :], A["L1_ffn_Wg"])
            load(bgb[:, :], A["L1_ffn_bg"].rearrange("(o e) -> o e", o=1).broadcast_to([P, NE]))

        def swap_weights(dve):
            dve.wait_ge(ld_tail.sem, 16 * TAIL_LOADS)
            dve.tensor_copy(wvb[:, :].rearrange("k (r d) -> k r d", r=KVH), wkvn[:, :, :, 1])
            dve.tensor_copy(wkb[:, 0, :].rearrange("k (r j d) -> k r j d", r=KVH, j=GRP),
                            wkvn[:, :, :, 0].unsqueeze(2).broadcast_to([KVL, KVH, GRP, QD])).then_inc(cswap.sem, 1)
            dve.wait_ge(cswap.sem, 1)
            for w in (wqb, wkb):
                ins = dve.tensor_copy(w[:, 1, :].rearrange("k (c s) -> k c s", s=2),
                                      w[:, 0, :].rearrange("k (c s) -> k c s", s=2)[:, :, ::-1])
            ins.then_inc(cswap.sem, 1)

        def xcols(t):
            return xT[:, t * P:(t + 1) * P]

        def gru_pe(pe):
            pe.wait_ge(ld_const.sem, 16)
            pe.wait_ge(ld_x.sem, 16)
            for g in range(NGR):
                for t in range(TG):
                    mm = pe.transpose(bank[g][:, t * P:(t + 1) * P], xtok[:, TG * g + t, :], ident)
                mm.then_inc(x_turned.sem, 1)
            for g in range(NGR):
                wide_back(pe, 0, g, bank[4 + g])
            pe.wait_ge(ld_gru.sem, 16 * 4)
            pe.wait_ge(x_kept.sem, NGR)

            def gates(g):
                pe.wait_ge(w_out.sem, w_out.after(g))
                if g >= 2:
                    pe.wait_ge(gru_b.sem, gru_b.after(g - 2))
                for m in range(2):
                    mm = pe.matmul(bank[2 * (g % 2) + m][:, :], wzh[:, m, :], xn1[:, g * GW:(g + 1) * GW], start=True, stop=True)
                mm.then_inc(zh_done.sem, 1)

            def turn(g):
                pe.wait_ge(gru_res.sem, gru_res.after(g))
                wide_turn(pe, 1, g, xcols, bank[4 + g])

            for g in range(NGR):
                gates(g)
                if g >= 2:
                    turn(g - 2)
            turn(NGR - 2)
            turn(NGR - 1)
            for g in range(NGR):
                wide_back(pe, 1, g, bank[g])

        def gru_act(act):
            act.preload_act_table(ACT.Sigmoid)
            for g in range(NGR):
                wide_out(act, 0, g, bank[4 + g], xn1)
            act.wait_ge(ld_gru.sem, 16 * 4)

            def keep(g):
                act.wait_ge(w_turn.sem, w_turn.after(g))
                act.activation(xtok[:, g * TG:(g + 1) * TG, :].rearrange("p t d -> p (t d)"), bank[4 + g][:, :],
                               ACT.Copy).then_inc(w_keep.sem, 1)

            for g in range(NGR):
                act.wait_ge(zh_done.sem, zh_done.after(g))
                if g:
                    act.wait_ge(gru_b.sem, gru_b.after(g - 1))
                act.activation(zs, bank[2 * (g % 2)][:, :], ACT.Sigmoid, bias=bzh[:, 0:1]).then_inc(z_sig.sem, 1)
                if g >= 2:
                    keep(g - 2)
            keep(NGR - 2)
            keep(NGR - 1)
            for g in range(NGR):
                wide_out(act, 1, g, bank[g], uT)

        def gru_dve(dve):
            dve.wait_ge(ld_x.sem, 16)
            for g in range(NGR):
                ins = wide_stats(dve, xtok, g)
            ins.then_inc(w_chain.sem, 1)
            wide_normalise(dve, 0, xtok)
            for g in range(NGR):
                dve.wait_ge(x_turned.sem, g + 1)
                dve.tensor_copy(xT[:, g * GW:(g + 1) * GW], bank[g][:, :]).then_inc(x_kept.sem, 1)
            dve.wait_ge(x_kept.sem, NGR)
            dve.wait_ge(ld_gru.sem, 16 * 4)

            def scan(g):
                dve.wait_ge(z_sig.sem, z_sig.after(g))
                if g:
                    dve.wait_ge(gru_scan.sem, gru_scan.after(g - 1))
                dve.tensor_scalar(za, zs, -1.0, 1.0, ALU.mult, ALU.add).then_inc(gru_a.sem, 1)
                dve.scalar_tensor_tensor(out=zb, in0=bank[2 * (g % 2) + 1][:, :], scalar=bzh[:, 1:2], in1=zs,
                                         op0=ALU.add, op1=ALU.mult).then_inc(gru_b.sem, 1)
                dve.wait_ge(gru_a.sem, gru_a.after(g))
                dve.wait_ge(gru_b.sem, gru_b.after(g))
                if g:
                    dve.wait_ge(gru_res.sem, gru_res.after(g - 1))
                for q in range(GW // SEQ):
                    c = slice(q * SEQ, (q + 1) * SEQ)
                    ins = dve.tensor_tensor_scan(hs[:, c], za[:, c], zb[:, c], 0.0, ALU.mult, ALU.add)
                ins.then_inc(gru_scan.sem, 1)
                dve.wait_ge(gru_scan.sem, gru_scan.after(g))
                x = xT[:, g * GW:(g + 1) * GW]
                dve.tensor_tensor(x, x, hs, ALU.add).then_inc(gru_res.sem, 1)

            def stats(g):
                dve.wait_ge(w_keep.sem, w_keep.after(g))
                return wide_stats(dve, xtok, g)

            for g in range(NGR):
                scan(g)
                if g >= 3:
                    stats(g - 3)
            for g in range(NGR - 3, NGR):
                ins = stats(g)
            ins.then_inc(w_chain.sem, 1)
            dve.wait_ge(w_back.sem, w_back.after(NGR - 1))
            wide_normalise(dve, 1, xtok)
            dve.wait_ge(w_out.sem, w_out.after(2 * NGR - 1))
            shifted_copy(dve, xs, 0).then_inc(xs_in.sem, 1)

        GROUPS = ([(0, r, 0, GRP, 1) for r in range(KVH)] + [(1, r, j, 2, 2) for j in (0, 2) for r in range(KVH)])
        NG = len(GROUPS)
        G_T = 2
        O_SLOT = KVH + 2
        obank = (bank[4], bank[1])

        def lagged(g, lag, live):
            k = g - lag
            return (live(1), 1, k) if k >= 0 else (live(2), 2, k + NG)

        def lat_pe(pe):
            pe.wait_ge(ld_tail.sem, 16 * TAIL_LOADS)
            pe.wait_ge(cast_done.sem, 4)
            pe.wait_ge(cswap.sem, 2)
            pe.wait_ge(f_res.sem, f_res.after(DEPTH * NB - 1))
            low, high = bank[0][:, 0:SEQ], bank[0][:, SEQ:2 * SEQ]
            for s, live in steps(pe, NB, 2):
                for g in range(NG):
                    if live(1):
                        b, G = s - 1, NG * (s - 1) + g
                        t, r, j0, nh, nk = GROUPS[g]
                        if g == 0:
                            pe.wait_ge(c_ckm.sem, c_ckm.after(b, 2))
                        if g == KVH:
                            pe.wait_ge(c_ckm.sem, c_ckm.after(b))
                            pe.wait_ge(c_cq.sem, c_cq.after(b))
                        pe.wait_ge(c_exp.sem, c_exp.after(G - 3))
                        sc = bank[5 + g % 3]
                        keys = ckm[32 * r:32 * r + 32, j0:j0 + nh, 0:nk * P]
                        pe.matmul(sc[:, :], cq[32 * r:32 * r + 32, t * P:(t + 1) * P], keys, start=True, stop=False,
                                  skip_group_check=True)
                        tri = causal[:, t, :].rearrange("p (h b k) -> p h b k", h=nh, b=nk)[:, :, nk - 1, :]
                        diag = sc[:, :].rearrange("p (h b k) -> p h b k", h=nh, b=nk)[:, :, nk - 1, :]
                        pe.matmul(diag, identb[:, :], tri, start=False, stop=True, skip_group_check=True).then_inc(c_s.sem, 1)
                    ok, lag, k = lagged(g, G_T, live)
                    if ok:
                        G = NG * (s - lag) + k
                        pe.wait_ge(c_exp.sem, c_exp.after(G))
                        pe.wait_ge(c_ptev.sem, c_ptev.after(G - 1))
                        for q in range(4):
                            mm = pe.transpose(bank[3][:, q * P:(q + 1) * P], cp[:, k % 3, q * P:(q + 1) * P], ident)
                        mm.then_inc(c_pt.sem, 1)
                    for n in range(3):
                        first = O_SLOT + KVH * n
                        c, ok = (s - 1, live(1)) if first < NG else (s - 2, live(2))
                        if g == first % NG and ok:
                            if n == 0:
                                pe.wait_ge(c_cv.sem, c_cv.after(c))
                            if n < 2:
                                pe.wait_ge(c_oev.sem, c_oev.after(2 * (c - 1) + n))
                            pe.wait_ge(c_ptev.sem, c_ptev.after(NG * c + KVH * n + KVH - 1))
                            set_ = GROUPS[KVH * n:KVH * n + KVH]
                            for kb in range(set_[0][4]):
                                for i, (t, r, j0, nh, nk) in enumerate(set_):
                                    probs = cpT[(KVH * n + i) % NTB].rearrange("p (h b k) -> p h b k", h=nh, b=nk)[:, :, kb, :]
                                    mm = pe.matmul(obank[t][32 * r:32 * r + 32, j0 * P:(j0 + nh) * P], cvp[:, kb, r, :], probs,
                                                   start=(kb == 0), stop=(kb == nk - 1))
                            mm.then_inc(c_o.sem, 1)
                    for t, slot in ((0, 0), (1, 8)):
                        c = s - 2
                        if g == slot and live(2):
                            pe.wait_ge(c_back[t].sem, c_back[t].after(c))
                            if t == 0:
                                pe.wait_ge(c_res.sem, c_res.after(c - 1))
                            else:
                                pe.wait_ge(c_nrm.sem, c_nrm.after(2 * c))
                                if live(1):
                                    pe.wait_ge(cv_ev.sem, cv_ev.after(s - 1))
                            pe.matmul(bank[2][:, :], zsel, cout[:, t, :], start=True, stop=True).then_inc(c_z.sem, 1)
                    if g == 10 and live(2):
                        c = s - 2
                        pe.wait_ge(c_nrm.sem, c_nrm.after(2 * c + 1))
                        for j in range(GRP):
                            mm = pe.matmul(bank[2][:, 0:SEQ], woutp[:, j, :], con[:, :, j * P:(j + 1) * P],
                                           start=(j == 0), stop=(j == GRP - 1))
                        mm.then_inc(c_y.sem, 1)
                    if g == 3 and live(1):
                        b = s - 1
                        if live(2):
                            pe.wait_ge(c_nrm.sem, c_nrm.after(2 * (s - 2)))
                        for t in range(NT):
                            mm = pe.matmul(bank[2][:, t * 32:(t + 1) * 32], ckva[:, t * P:(t + 1) * P], wvb[:, :], start=True, stop=True)
                        mm.then_inc(c_pv.sem, 1)
                    if live(0):
                        if g == 0:
                            pe.wait_ge(c_mq.sem, c_mq.after(s - 1))
                            ln_turn_in(pe, LN_C + s, lnin, low)
                        if g == 6:
                            ln_turn_out(pe, LN_C + s, high)
                        if g == 7:
                            pe.wait_ge(ln_out.sem, ln_out.after(LN_C + s))
                            pe.matmul(low[0:QL, :], wqa[:, :], xnT[:, :], start=True, stop=True)
                            pe.matmul(high[0:KVL, :], wkva[:, :], xnT[:, :], start=True, stop=True).then_inc(lat_mm.sem, 1)
                        if g == 8:
                            pe.wait_ge(lat_ev.sem, lat_ev.after(s))
                            for m in range(2):
                                mm = pe.matmul(bank[0][:, m * SEQ:(m + 1) * SEQ], wkb[:, m, :], ckva[:, :], start=True, stop=True)
                            mm.then_inc(c_pk.sem, 1)
                        if g == 9:
                            pe.wait_ge(c_mk.sem, c_mk.after(s))
                            for m in range(2):
                                mm = pe.matmul(bank[0][:, m * SEQ:(m + 1) * SEQ], wqb[:, m, :], cqa[:, :], start=True, stop=True)
                            mm.then_inc(c_pq.sem, 1)

        def lat_act(act):
            act.preload_act_table(ACT.Exp)
            for s, live in steps(act, NB, 2):
                for g in range(NG):
                    ok, lag, k = lagged(g, G_T, live)
                    if ok:
                        G = NG * (s - lag) + k
                        act.wait_ge(c_pt.sem, c_pt.after(G))
                        used = (k - NTB) // KVH
                        act.wait_ge(c_o.sem, c_o.after(3 * (s - lag) + used))
                        act.activation(cpT[k % NTB], bank[3][:, :], ACT.Copy).then_inc(c_ptev.sem, 1)
                    if live(1):
                        G = NG * (s - 1) + g
                        t, r, j0, nh, nk = GROUPS[g]
                        act.wait_ge(c_nb.sem, c_nb.after(G))
                        act.wait_ge(c_pt.sem, c_pt.after(G - 3))
                        n = nk * P
                        for hh in range(nh):
                            ins = act.activation(cp[:, g % 3, hh * n:(hh + 1) * n], bank[5 + g % 3][:, hh * n:(hh + 1) * n],
                                                 ACT.Exp, scale=QD ** -0.5, bias=cnb[:, g % 3, hh:hh + 1])
                        ins.then_inc(c_exp.sem, 1)
                    for t, slot in ((0, 7), (1, 3)):
                        c, ok = (s - 1, live(1)) if t == 0 else (s - 2, live(2))
                        if g == slot and ok:
                            act.wait_ge(c_o.sem, c_o.after(3 * c + 2 * t))
                            act.wait_ge(c_nrm.sem, c_nrm.after(2 * (c - 1) + t))
                            act.activation(cout[:, t, :], obank[t][:, :], ACT.Copy).then_inc(c_oev.sem, 1)
                    if live(0):
                        if g == 0:
                            ln_keep(act, LN_C + s, bank[0][:, 0:SEQ])
                        if g == 6:
                            act.wait_ge(ln_t2.sem, ln_t2.after(LN_C + s))
                            act.wait_ge(lat_mm.sem, lat_mm.after(s - 1))
                            act.activation(xnT[:, :], bank[0][:, SEQ:2 * SEQ], ACT.Copy).then_inc(ln_out.sem, 1)
                        if g == 7:
                            act.wait_ge(lat_mm.sem, lat_mm.after(s))
                            act.wait_ge(c_pq.sem, c_pq.after(s - 1))
                            act.wait_ge(c_pv.sem, c_pv.after(s - 1))
                            act.activation(cqa[:, :], bank[0][0:QL, 0:SEQ], ACT.Copy)
                            act.activation(ckva[:, :], bank[0][0:KVL, SEQ:2 * SEQ], ACT.Copy).then_inc(lat_ev.sem, 1)
                    if live(1) and g == 3:
                        b = s - 1
                        act.wait_ge(c_pv.sem, c_pv.after(b))
                        act.wait_ge(c_cv.sem, c_cv.after(b - 1))
                        act.activation(cvn[:, :, :, :].rearrange("p t r d -> p (t r d)"), bank[2][:, 0:NT * KVH * QD],
                                       ACT.Copy).then_inc(cv_ev.sem, 1)

        def lat_dve(dve):
            dve.wait_ge(f_res.sem, f_res.after(DEPTH * NB - 1))
            dve.tensor_tensor(xT[:, :], xT[:, :], uT[:, 0:NB * SEQ], ALU.add).then_inc(add_u.sem, 1)
            dve.wait_ge(add_u.sem, 1)
            dve.wait_ge(ld_tail.sem, 16 * TAIL_LOADS)
            for s, live in steps(dve, NB, 2):
                for g in range(NG):
                    if live(0) and g == 0:
                        dve.wait_ge(ln_t1.sem, ln_t1.after(LN_C + s - 1))
                        dve.tensor_copy(lnin[:, :], xT[:, seq_cols(s)]).then_inc(ln_in.sem, 1)
                    i = LN_C + s
                    norm = live(0) and 1 <= g <= 5
                    if live(1):
                        G = NG * (s - 1) + g
                        t, r, j0, nh, nk = GROUPS[g]
                        dve.wait_ge(c_s.sem, c_s.after(G))
                        dve.wait_ge(c_nb.sem, c_nb.after(G - 1))
                        dve.tensor_reduce(cmx[:, 0:nh], bank[5 + g % 3][:, :].rearrange("p (h k) -> p h k", h=nh), AX.X,
                                          ALU.max).then_inc(c_max.sem, 1)
                    if norm:
                        ln_normalise(dve, i, 3 * g - 3, 3 * g - 2)
                    if live(1):
                        dve.wait_ge(c_max.sem, c_max.after(G))
                        dve.wait_ge(c_exp.sem, c_exp.after(G - 3))
                        dve.tensor_scalar(cnb[:, g % 3, 0:nh], cmx[:, 0:nh], -(QD ** -0.5), None, ALU.mult).then_inc(c_nb.sem, 1)
                    if norm:
                        ln_normalise(dve, i, 3 * g - 2, 3 * g)
                    for t, slot in ((0, 9), (1, 5)):
                        c, ok = (s - 1, live(1)) if t == 0 else (s - 2, live(2))
                        if g == slot and ok:
                            dve.wait_ge(c_out[t].sem, c_out[t].after(c))
                            dve.wait_ge(c_back[t].sem, c_back[t].after(c - 1))
                            dve.reciprocal(crs[:, t, 1, :], crs[:, t, 0, :]).then_inc(c_rz.sem, 1)
                    for t, slot in ((0, 1), (1, 9)):
                        c = s - 2
                        if g == slot and live(2):
                            dve.wait_ge(c_z.sem, c_z.after(2 * c + t))
                            dve.wait_ge(c_y.sem, c_y.after(c - 1))
                            dve.tensor_tensor(con[:, t, :], cout[:, t, :], bank[2][:, :], ALU.mult).then_inc(c_nrm.sem, 1)
                    if g == 11 and live(2):
                        c = s - 2
                        dve.wait_ge(c_y.sem, c_y.after(c))
                        dve.scalar_tensor_tensor(out=xT[:, seq_cols(c)], in0=bank[2][:, 0:SEQ], scalar=boutc[:, 0:1],
                                                 in1=xT[:, seq_cols(c)], op0=ALU.add, op1=ALU.add).then_inc(c_res.sem, 1)
                    if live(0):
                        if g == 8:
                            dve.wait_ge(c_pk.sem, c_pk.after(s))
                            dve.wait_ge(c_ck.sem, c_ck.after(s - 1))
                            dve.tensor_tensor(ct[:, 1, :], bank[0][:, :], rope, ALU.mult).then_inc(c_mk.sem, 1)
                        if g == 9:
                            dve.wait_ge(c_pq.sem, c_pq.after(s))
                            dve.wait_ge(c_cq.sem, c_cq.after(s - 1))
                            dve.tensor_tensor(ct[:, 0, :], bank[0][:, :], rope, ALU.mult).then_inc(c_mq.sem, 1)

        def lat_pool(pool):
            pool.wait_ge(add_u.sem, 1)
            def prepare(s):
                def mask_keys(j, k0, k1):
                    pool.tensor_tensor(ckm[:, j:j + 2, k0:k1], ck[:, k0:k1].unsqueeze(1).broadcast_to([P, 2, k1 - k0]),
                                       cst("rowmask")[:, j:j + 2].unsqueeze(2).broadcast_to([P, 2, k1 - k0]),
                                       ALU.mult).then_inc(c_ckm.sem, 1)

                pool.wait_ge(c_mk.sem, c_mk.after(s))
                pool.tensor_tensor(ck[:, :], ct[:, 1, 0:SEQ], ct[:, 1, SEQ:], ALU.add).then_inc(c_ck.sem, 1)
                pool.wait_ge(c_ck.sem, c_ck.after(s))
                pool.wait_ge(c_s.sem, c_s.after(NG * s - KVH - 1))
                pool.wait_ge(c_mq.sem, c_mq.after(s))
                pool.tensor_tensor(cq[:, 0:P], ct[:, 0, 0:P], ct[:, 0, SEQ:SEQ + P], ALU.add)
                mask_keys(0, 0, SEQ)
                pool.wait_ge(c_s.sem, c_s.after(NG * s - 1))
                mask_keys(2, 0, P)
                mask_keys(2, P, SEQ)
                pool.tensor_tensor(cq[:, P:SEQ], ct[:, 0, P:SEQ], ct[:, 0, SEQ + P:], ALU.add).then_inc(c_cq.sem, 1)

            def values(s):
                pool.wait_ge(cv_ev.sem, cv_ev.after(s))
                hold(pool)
                pool.wait_ge(c_o.sem, c_o.after(3 * s - 1))
                hold(pool)
                pool.tensor_copy(cvp[:, :, :, 0:QD], cvn[:, :, :, :]).then_inc(c_cv.sem, 1)

            prepare(0)
            with pool.Fori(1, NB) as s:
                values(s - 1)
                prepare(s)
            values(NB - 1)

        def lat_sp(sp):
            def rows(t, r):
                return cout[32 * r + QD:32 * r + QD + 1, t, :]

            def spread(t, r, m):
                return crs[32 * r:32 * r + 32, t, m, :]

            with sp.Fori(0, NB) as c:
                for t in range(NT):
                    sp.wait_ge(c_oev.sem, c_oev.after(2 * c + t))
                    hold(sp)
                    sp.wait_ge(c_rz.sem, c_rz.after(2 * (c - 1) + t))
                    hold(sp)
                    for r in range(KVH):
                        sp.dma_start(spread(t, r, 0), rows(t, r)).then_inc(c_out[t].sem, 16)
                    sp.wait_ge(c_rz.sem, c_rz.after(2 * c + t))
                    hold(sp)
                    for r in range(KVH):
                        sp.dma_start(rows(t, r), spread(t, r, 1)).then_inc(c_back[t].sem, 16)

        def gate_pe(pe):
            pe.wait_ge(c_res.sem, c_res.after(NB - 1))
            for g in range(NGR):
                wide_turn(pe, 2, g, xcols, bank[g])
            for g in range(NGR):
                wide_back(pe, 2, g, bank[4 + g])
            pe.wait_ge(w_keep.sem, w_keep.after(NGR))
            for g in range(NGR):
                pe.wait_ge(w_out.sem, w_out.after(2 * NGR + g))
                for t in range(g * TG, (g + 1) * TG):
                    mm = pe.matmul(bank[0][:, t * NE:(t + 1) * NE], xnA[:, t * P:(t + 1) * P], wg[:, :], start=True, stop=True)
            mm.then_inc(d_lmm.sem, 1)
            pe.wait_ge(d_ch.sem, GATE_STEPS)
            for g in range(NGR):
                for t in range(TG):
                    mm = pe.transpose(bank[4 + g][0:NE, t * P:(t + 1) * P], wA[:, g * TG + t, :], ident)
                mm.then_inc(d_wT.sem, 1)
            for g in range(NGR):
                pe.wait_ge(d_wTev.sem, d_wTev.after(g))
                for t in range(TG):
                    o = (g * TG + t) * P
                    mm = pe.matmul(bank[g][:, t * P:(t + 1) * P], dwT[:, o:o + P], b2e[:, :], start=True, stop=True)
                mm.then_inc(d_b2.sem, 1)

        def gate_act(act):
            for g in range(NGR):
                act.wait_ge(w_turn.sem, w_turn.after(NGR + g))
                act.activation(acc[:, g * GW:(g + 1) * GW], bank[g][:, :], ACT.Copy).then_inc(w_keep.sem, 1)
            for g in range(NGR):
                wide_out(act, 2, g, bank[4 + g], xnA)
            act.wait_ge(d_ch.sem, 3)
            act.activation(dexp[:, :], ddiff[:, :], ACT.Exp).then_inc(d_e.sem, 1)
            for g in range(NGR):
                act.wait_ge(d_wT.sem, d_wT.after(g))
                act.activation(dwT[:, g * GW:(g + 1) * GW], bank[4 + g][0:NE, :], ACT.Copy).then_inc(d_wTev.sem, 1)

        GATE_STEPS = 11

        def gate_dve(dve):
            for g in range(NGR):
                dve.wait_ge(w_keep.sem, w_keep.after(NGR + g))
                ins = wide_stats(dve, xtok, g)
            ins.then_inc(w_chain.sem, 1)
            dve.wait_ge(c_y.sem, c_y.after(NB - 1))
            wide_normalise(dve, 2, xtok)
            k = 0

            def link(ins):
                nonlocal k
                k += 1
                ins.then_inc(d_ch.sem, 1)
                dve.wait_ge(d_ch.sem, k)

            def by_expert(v):
                return v.unsqueeze(2).broadcast_to([P, TILES, NE])

            dve.wait_ge(d_lmm.sem, 1)
            link(dve.tensor_tensor(dlg[:, :, :], bank[0][:, 0:TILES * NE].rearrange("p (t e) -> p t e", t=TILES),
                                   bgb[:, :].unsqueeze(1).broadcast_to([P, TILES, NE]), ALU.add))
            for t in range(TILES):
                ins = dve.max(dmx[:, t, :], dlg[:, t, :])
            link(ins)
            link(dve.tensor_tensor(ddiff[:, :], dmx[:, :, 1], dmx[:, :, 0], ALU.subtract))
            for t in range(TILES):
                ins = dve.max_index(dix[:, t, :], dmx[:, t, :], dlg[:, t, :])
            link(ins)
            link(dve.tensor_copy(dixf[:, :, :], dix[:, :, 0:2]))
            dve.wait_ge(d_e.sem, 1)
            link(dve.tensor_scalar(dden[:, :], dexp[:, :], 1.0, None, ALU.add))
            link(dve.reciprocal(dp[:, 0, :], dden[:, :]))
            link(dve.tensor_tensor(dp[:, 1, :], dexp[:, :], dp[:, 0, :], ALU.mult))
            for m in range(2):
                ins = dve.tensor_tensor(dw[:, m], cst("iota").unsqueeze(1).broadcast_to([P, TILES, NE]),
                                        by_expert(dixf[:, :, m]), ALU.is_equal)
            link(ins)
            for m in range(2):
                ins = dve.tensor_tensor(dw[:, m], dw[:, m], by_expert(dp[:, m, :]), ALU.mult)
            link(ins)
            link(dve.tensor_tensor(wA[:, :, :], dw[:, 0], dw[:, 1], ALU.add))
            for g in range(NGR):
                a = acc[:, g * GW:(g + 1) * GW]
                dve.wait_ge(d_b2.sem, d_b2.after(g))
                dve.tensor_tensor(a, a, bank[g][:, :], ALU.add).then_inc(d_acc.sem, 1)

        def expert_slots(eng):
            for s, live in steps(eng, NB, 1):
                for e in range(NE):
                    yield s, e, live(0), (live(0) if e else live(1)), NE * s + e

        def experts_pe(pe):
            pe.wait_ge(d_acc.sem, d_acc.after(NGR - 1))
            pe.wait_ge(ld_exp.sem, 32)
            for s, e, first, second, n in expert_slots(pe):
                if first:
                    for hb in range(2):
                        pe.wait_ge(e_gelu.sem, e_gelu.after(2 * (n - 2) + hb))
                        for c in range(2):
                            ch = 2 * hb + c
                            mm = pe.matmul(bank[2 * (e % 2) + hb][:, c * SEQ:(c + 1) * SEQ], w1e[:, e, ch * P:(ch + 1) * P],
                                           xnA[:, seq_cols(s)], start=True, stop=True)
                        mm.then_inc(e_up.sem, 1)
                if second:
                    m, pe_e = n - 1, (e - 1) % NE
                    pe.wait_ge(e_gelu.sem, e_gelu.after(2 * m + 1))
                    pe.wait_ge(e_acc.sem, e_acc.after(m - 2))
                    for t in range(NT):
                        for c in range(EC):
                            mm = pe.matmul(bank[4 + pe_e % 2][:, t * P:(t + 1) * P], eh[:, pe_e % 2, c, t * P:(t + 1) * P],
                                           w2e[:, pe_e, c, :], start=(c == 0), stop=(c == EC - 1))
                    mm.then_inc(e_down.sem, 1)

        def experts_act(act):
            act.preload_act_table(ACT.Gelu)
            for s, e, first, second, n in expert_slots(act):
                if first:
                    act.wait_ge(e_down.sem, e_down.after(n - 2))
                    for hb in range(2):
                        act.wait_ge(e_up.sem, e_up.after(2 * n + hb))
                        for c in range(2):
                            ch = 2 * hb + c
                            ins = act.activation(eh[:, e % 2, ch, :], bank[2 * (e % 2) + hb][:, c * SEQ:(c + 1) * SEQ], ACT.Gelu,
                                                 bias=b1e[:, e * EC + ch:e * EC + ch + 1])
                        ins.then_inc(e_gelu.sem, 1)

        def experts_dve(dve):
            dve.wait_ge(d_acc.sem, d_acc.after(NGR - 1))
            for s, e, first, second, n in expert_slots(dve):
                if second:
                    m, pe_e = n - 1, (e - 1) % NE
                    b = s if e else s - 1
                    dve.wait_ge(e_down.sem, e_down.after(m))
                    dve.wait_ge(e_acc.sem, e_acc.after(m - 1))
                    for t in range(NT):
                        if isinstance(b, int):
                            w = wA[:, b * NT + t, pe_e:pe_e + 1]
                        else:
                            w = wA[:, ds(b * NT + t, 1), pe_e:pe_e + 1].rearrange("p t e -> p (t e)")
                        a = acc[:, seq_cols(b, P, t * P)]
                        ins = dve.scalar_tensor_tensor(out=a, in0=bank[4 + pe_e % 2][:, t * P:(t + 1) * P], scalar=w, in1=a,
                                                       op0=ALU.mult, op1=ALU.add)
                    ins.then_inc(e_acc.sem, 1)

        block = ctx.enter_context(nc.Block())

        @block.sync
        def _(sp):
            for x in credited["sp"]:
                x.start(sp)
            sp.dma_start(const[:, :], A["const"]).then_inc(ld_const.sem, 16)
            sp.dma_start(xtok[:, :, :], A["L0_attn_x"].rearrange("b (t p) d -> p (b t) d", p=P)).then_inc(ld_x.sem, 16)
            for m, (w, b) in enumerate((("L0_attn_Wz", "L0_attn_bz"), ("L0_attn_Wh", "L0_attn_bh"))):
                sp.dma_start(wzh[:, m, :], A[w]).then_inc(ld_gru.sem, 16)
                sp.dma_start(bzh[:, m:m + 1], A[b].rearrange("(p o) -> p o", o=1), allow_slow_non_contiguous=True).then_inc(ld_gru.sem, 16)
            tail_loads(sp)
            sp.wait_ge(zeroed.sem, 2)
            with sp.Fori(0, DEPTH) as layer:
                load_layer(sp, layer)
                attention_sp(sp, layer)
            sp.wait_ge(y_mm.sem, y_mm.after(DEPTH * NB * UPB - 1))
            sp.dma_start(w1e, A["L1_ffn_W1"].rearrange("e p f -> p e f")).then_inc(ld_exp.sem, 16)
            sp.dma_start(w2e, A["L1_ffn_W2"].rearrange("e (c p) d -> p e c d", p=P)).then_inc(ld_exp.sem, 16)
            lat_sp(sp)
            with sp.Fori(0, NB) as b:
                sp.wait_ge(e_acc.sem, e_acc.after(NE * b + NE - 1))
                hold(sp)
                sp.dma_start(out[ds(b, 1)].rearrange("b (t p) d -> p (b t) d", p=P),
                             acc[:, seq_cols(b)].rearrange("p (t d) -> p t d", t=NT)).then_inc(st_out.sem, 16)
            sp.wait_ge(st_out.sem, 16 * NB)

        @block.gpsimd
        def _(pool):
            for x in credited["pool"]:
                x.start(pool)
            pool.memset(vBD[:, 0], 0.0).then_inc(zeroed.sem, 1)
            pool.memset(vBD[:, 1], 0.0).then_inc(zeroed.sem, 1)
            pool.wait_ge(ld_const.sem, 16)
            pool.tensor_copy(bandrhs[:, :], cst("band")[0:2 * WIN, :]).then_inc(cast_done.sem, 1)
            pool.tensor_copy(bandsel[:, :, :], cst("bandsel")[0:2 * WIN, :].rearrange("p (t q) -> p t q", t=NT)).then_inc(cast_done.sem, 1)
            pool.tensor_copy(causal[:, :, :], cst("causal").rearrange("p (t q) -> p t q", t=NT)).then_inc(cast_done.sem, 1)
            pool.tensor_copy(identb[:, :], ident).then_inc(cast_done.sem, 1)
            with pool.Fori(0, DEPTH) as layer:
                attention_pool(pool, layer)
            lat_pool(pool)

        @block.scalar
        def _(act):
            for x in credited["act"]:
                x.start(act)
            gru_act(act)
            act.wait_ge(zeroed_dve.sem, 1)
            with act.Fori(0, DEPTH) as layer:
                act.preload_act_table(ACT.Exp)
                attention_act(act, layer)
                mlp_act(act, layer)
            lat_act(act)
            gate_act(act)
            experts_act(act)

        @block.vector
        def _(dve):
            for x in credited["dve"]:
                x.start(dve)
            dve.memset(kBD[:, :, :, :, :], 0.0)
            dve.memset(woutp[:, :, :], 0.0)
            dve.memset(cvp[:, :, :, :], 0.0)
            dve.memset(uT[:, NB * SEQ:], 0.0)
            dve.memset(lns[:, 0:1], 0.0)
            dve.memset(xs[:, 0:1], 0.0).then_inc(zeroed_dve.sem, 1)
            dve.wait_ge(zeroed_dve.sem, 1)
            dve.memset(cvp[:, :, :, QD:QD + 1], 1.0)
            gru_dve(dve)
            swap_weights(dve)
            with dve.Fori(0, DEPTH) as layer:
                attention_dve(dve, layer)
                mlp_dve(dve, layer)
            lat_dve(dve)
            gate_dve(dve)
            experts_dve(dve)

        @block.tensor
        def _(pe):
            for x in credited["pe"]:
                x.start(pe)
            gru_pe(pe)
            pe.wait_ge(cast_done.sem, 4)
            pe.wait_ge(zeroed_dve.sem, 1)
            with pe.Fori(0, DEPTH) as layer:
                pe.wait_ge(ld_wa.sem, (layer + 1) * 16 * LA_LOADS)
                attention_pe(pe, layer)
                mlp_pe(pe, layer)
            lat_pe(pe)
            gate_pe(pe)
            experts_pe(pe)


def constants():
    c = np.zeros((P, CONST_N), np.float32)

    def put(name, v):
        a, b = CONST_COLS[name]
        c[:v.shape[0], a:b] = v.reshape(v.shape[0], b - a)

    f32 = np.float32
    put("ident", np.eye(P, dtype=f32))
    half = np.arange(0, DH, 2, dtype=f32)
    inv_freq = (f32(1.0) / f32(10000.0) ** (half / f32(DH))).astype(f32)
    tok = np.arange(SEQ, dtype=f32)
    freqs = (tok[:, None] * inv_freq[None, :]).astype(np.float64)
    base = ((half + f32(0.4 * DH)) / f32(1.4 * DH)).astype(np.float64)
    power = ((tok - SEQ // 2) / f32(WIN // 2)).astype(np.float64)
    scale = base[None, :] ** power[:, None]
    cos, sin = np.cos(freqs), np.sin(freqs)
    rot = np.zeros((SEQ, 4, DH))
    for m, s in ((0, scale), (2, 1.0 / scale)):
        rot[:, m] = np.concatenate([cos * s, cos * s], -1)
        rot[:, m + 1] = np.concatenate([-sin * s, sin * s], -1)
    put("rot", rot.reshape(NT, P, 4, DH).transpose(1, 0, 2, 3).astype(f32))
    inv8 = (f32(1.0) / f32(10000.0) ** (np.arange(0, QD, 2, dtype=f32) / f32(QD))).astype(f32)
    ang = (tok[:, None] * inv8[None, :]).astype(np.float64)
    pair = (np.arange(P) % QD) // 2
    sign = np.where(np.arange(P) % 2 == 0, -1.0, 1.0)[:, None]
    put("rope", np.concatenate([np.cos(ang)[:, pair].T, np.sin(ang)[:, pair].T * sign], 1).astype(f32))
    rows = np.arange(P)
    put("rowmask", (rows[:, None] % (GRP * QD) // QD == np.arange(GRP)[None, :]).astype(f32))
    put("zsel", ((rows[:, None] % 32 == QD) & (rows[:, None] // 32 == rows[None, :] // 32)).astype(f32))
    put("iota", np.tile(np.arange(NE, dtype=f32), (P, 1)))
    i, j = np.arange(WIN)[:, None], np.arange(2 * WIN)[None, :]
    band = np.where((i <= j) & (j <= i + WIN), 0.0, NEG)
    edge = np.where(j < WIN, NEG, 0.0) + 0.0 * i
    put("band", np.tile(np.concatenate([band, edge], 0), (1, HH)).astype(f32))
    sel = np.zeros((2 * WIN, NT, P), f32)
    for w in range(NWT):
        sel[np.arange(WIN), :, w * WIN + np.arange(WIN)] = 1.0
    sel[WIN + np.arange(WIN), 0, np.arange(WIN)] = 1.0
    put("bandsel", sel)
    tri = np.where(rows[None, :] <= rows[:, None], 0.0, NEG)
    put("causal", np.stack([np.tile(tri, (1, 4)), np.tile(np.concatenate([0.0 * tri, tri], 1), (1, 2))], 1).astype(f32))
    return c


_INS = ['L0_attn_x', 'L0_attn_Wz', 'L0_attn_bz', 'L0_attn_Wh', 'L0_attn_bh', 'L0_ffn_Wqkv', 'L0_ffn_q_scale',
        'L0_ffn_k_scale', 'L0_ffn_Wo', 'L0_ffn_ln_g', 'L0_ffn_ln_b', 'L0_ffn_W1', 'L0_ffn_b1', 'L0_ffn_W2', 'L0_ffn_b2',
        'L1_attn_Wqa', 'L1_attn_Wqb', 'L1_attn_Wkva', 'L1_attn_Wkvb', 'L1_attn_Wout', 'L1_attn_bout', 'L1_ffn_W1',
        'L1_ffn_b1', 'L1_ffn_W2', 'L1_ffn_b2', 'L1_ffn_Wg', 'L1_ffn_bg']


def kernel(**inputs):
    import concourse.bacc as _bacc
    from concourse.bass_utils import run_bass_kernel_spmd as _run

    nc = _bacc.Bacc("TRN2", target_bir_lowering=False, num_devices=1)
    arrays = {name: np.ascontiguousarray(inputs[name]) for name in _INS}
    arrays["const"] = constants()
    A = {}
    for name, a in arrays.items():
        A[name] = nc.dram_tensor(f"in_{name}_dram", a.shape, mybir.dt.from_np(a.dtype), kind="ExternalInput").ap()
    out = nc.dram_tensor("out_0_dram", (NB, SEQ, D), F32, kind="ExternalOutput").ap()
    mixed_kernel(nc, A, out)
    r = _run(nc, [{f"in_{name}_dram": a for name, a in arrays.items()}], core_ids=[0])
    return r.results[0]["out_0_dram"]
```
